# Optimizing a Trainium2 kernel written in Bass

```python
import numpy as np
import jax
import jax.numpy as jnp

def _softmax(x, axis=-1):
    return jax.nn.softmax(x, axis=axis)

def _gelu(x):
    return jax.nn.gelu(x, approximate=True)

def _silu(x):
    return jax.nn.silu(x)

def _sigmoid(x):
    return jax.nn.sigmoid(x)

def _layernorm(x, axis=-1, eps=1e-05):
    m = jnp.mean(x, axis=axis, keepdims=True)
    v = jnp.var(x, axis=axis, keepdims=True)
    return (x - m) / jnp.sqrt(v + eps)

def _scatter_add(tgt, idx, src, axis=0):
    return tgt.at[idx].add(src)

def _segment_sum(src, seg, n):
    return jax.ops.segment_sum(src, seg, n)
kernel_name = 'mk_decoder_preln_d2_seqx_r8_e7a060'

def setup_inputs(seed: int=0):
    np.random.seed(seed)
    _w = jnp.asarray

    def _rec_inputs():
        import jax
        import jax.numpy as jnp
        _rk = jax.random.key(seed)
        x = 7.22e-05 + 1 * jax.random.normal(jax.random.fold_in(_rk, 1), (4, 512, 128), jnp.float32)
        _lenS = 512 - jax.random.randint(jax.random.fold_in(_rk, 7), (4,), 0, max(1, 512 // 4) + 1, jnp.int32)
        _lenS2 = 77 - jax.random.randint(jax.random.fold_in(_rk, 8), (4,), 0, max(1, 77 // 4) + 1, jnp.int32)
        _ctx_1024P = jax.random.normal(jax.random.fold_in(_rk, 11), (4, 16, 128), jnp.float32)
        _ctx_1024c = jax.random.dirichlet(jax.random.fold_in(_rk, 511), 0.3 * jnp.ones((16,), jnp.float32), (4, 77))
        _ctx_1024t = jnp.einsum('bsk,bkd->bsd', _ctx_1024c, _ctx_1024P)
        _ctx_1024t = _ctx_1024t * jax.lax.rsqrt(jnp.mean(jnp.square(_ctx_1024t)) + 1e-12) * 0.953939
        ctx_1024 = 4.13588e-05 + 0.999923 * (_ctx_1024t + 0.3 * jax.random.normal(jax.random.fold_in(_rk, 611), (4, 77, 128), jnp.float32))
        _validS = jnp.arange(512)[None, :] < _lenS[:, None]
        _validS2 = jnp.arange(77)[None, :] < _lenS2[:, None]
        _causal = jnp.tril(jnp.ones((512, 512), dtype=bool))
        mask_Bx1xSxS2_if1 = jnp.where(jnp.ones((4, 1, 512, 77), dtype=bool), 1, 0).astype(jnp.int32)
        return (x, ctx_1024, mask_Bx1xSxS2_if1)
    x, ctx_1024, mask_Bx1xSxS2_if1 = _rec_inputs()

    def _L0_attn_setup():
        import math
        import jax, jax.numpy as jnp
        import numpy as np
        HEADS = 16
        DIM_HEAD = 64
        NUM_NULL_KV = 2
        ATTN_SCALE = 8.0
        LN_EPS = 1e-05

        def _alibi_slopes(heads):
            start = 2.0 ** (-2.0 ** (-(math.log2(heads) - 3.0)))
            return np.array([start * start ** i for i in range(heads)], dtype=np.float32)

        def _l2norm(t):
            return t / jnp.maximum(jnp.linalg.norm(t, axis=-1, keepdims=True), 1e-12)
        key = jax.random.key(seed)
        ks = jax.random.split(key, 5)
        b, n, dim = (4, 256, 128)
        return {'x': jax.random.normal(ks[0], (b, n, dim), dtype=jnp.float32), 'gamma': jnp.ones((dim,), dtype=jnp.float32), 'w_q': jax.random.normal(ks[1], (dim, HEADS * DIM_HEAD), dtype=jnp.float32) * 0.02, 'w_kv': jax.random.normal(ks[2], (dim, 2 * HEADS * DIM_HEAD), dtype=jnp.float32) * 0.02, 'null_kv': jax.random.normal(ks[3], (HEADS, 2 * NUM_NULL_KV, DIM_HEAD), dtype=jnp.float32), 'q_scale': jnp.ones((DIM_HEAD,), dtype=jnp.float32), 'k_scale': jnp.ones((DIM_HEAD,), dtype=jnp.float32), 'w_out': jax.random.normal(ks[4], (HEADS * DIM_HEAD, dim), dtype=jnp.float32) * 0.02}
    _L0_attn_all = _L0_attn_setup()
    _L0_attn_in = {k: v for k, v in _L0_attn_all.items() if k in ('gamma', 'w_q', 'w_kv', 'null_kv', 'q_scale', 'k_scale', 'w_out')}
    del _L0_attn_all

    def _L0_xattn_setup():
        import jax, jax.numpy as jnp
        import numpy as np
        B, T, D, H = (4, 256, 128, 8)
        HD = D // H

        def _heads(t):
            b, t_, _ = t.shape
            return t.reshape(b, t_, H, HD).transpose(0, 2, 1, 3)
        key = jax.random.key(seed)
        ks = jax.random.split(key, 10)
        s = 1.0 / np.sqrt(D)
        return {'x': jax.random.normal(ks[0], (B, T, D), jnp.float32), 'y': jax.random.normal(ks[1], (B, T, D), jnp.float32), 'Wq': jax.random.normal(ks[2], (D, D), jnp.float32) * s, 'bq': jnp.zeros((D,), jnp.float32), 'Wk': jax.random.normal(ks[3], (D, D), jnp.float32) * s, 'bk': jnp.zeros((D,), jnp.float32), 'Wv': jax.random.normal(ks[4], (D, D), jnp.float32) * s, 'bv': jnp.zeros((D,), jnp.float32), 'Wo': jax.random.normal(ks[5], (D, D), jnp.float32) * s, 'bo': jnp.zeros((D,), jnp.float32)}
    _L0_xattn_all = _L0_xattn_setup()
    _L0_xattn_in = {k: v for k, v in _L0_xattn_all.items() if k in ('Wq', 'bq', 'Wk', 'bk', 'Wv', 'bv', 'Wo', 'bo')}
    del _L0_xattn_all

    def _L0_ffn_setup():
        import jax, jax.numpy as jnp
        import numpy as np
        NUM_EXPERTS = 160
        TOP_K = 8
        ROUTED_SCALE = 2.5
        HIDDEN = 128
        INTER = 64
        key = jax.random.key(seed)
        ks = jax.random.split(key, 7)
        B, S = (1, 256)
        return {'hidden_states': jax.random.normal(ks[0], (B, S, HIDDEN), dtype=jnp.float32), 'router_w': jax.random.normal(ks[1], (NUM_EXPERTS, HIDDEN), dtype=jnp.float32) * 0.02, 'expert_bias': jnp.zeros((NUM_EXPERTS,), dtype=jnp.float32), 'w_gate': jax.random.normal(ks[2], (NUM_EXPERTS, INTER, HIDDEN), dtype=jnp.float32) * 0.02, 'w_down': jax.random.normal(ks[3], (NUM_EXPERTS, HIDDEN, INTER), dtype=jnp.float32) * 0.02, 'w_gate_shared': jax.random.normal(ks[4], (INTER, HIDDEN), dtype=jnp.float32) * 0.02, 'w_down_shared': jax.random.normal(ks[5], (HIDDEN, INTER), dtype=jnp.float32) * 0.02}
    _L0_ffn_all = _L0_ffn_setup()
    _L0_ffn_in = {k: v for k, v in _L0_ffn_all.items() if k in ('router_w', 'expert_bias', 'w_gate', 'w_down', 'w_gate_shared', 'w_down_shared')}
    del _L0_ffn_all

    def _L1_attn_setup():
        import jax, jax.numpy as jnp
        import numpy as np
        D_MODEL = 128
        N_HEADS = 16
        key = jax.random.key(seed)
        k1, k2, k3, k4 = jax.random.split(key, 4)
        B, T, D = (4, 256, D_MODEL)
        x = jax.random.normal(k1, (B, T, D), dtype=jnp.float32)
        w_qkv = jax.random.normal(k2, (D, 3 * D), dtype=jnp.float32) / np.sqrt(D)
        w_out = jax.random.normal(k3, (D, D), dtype=jnp.float32) / np.sqrt(D)
        b_out = jax.random.normal(k4, (D,), dtype=jnp.float32) * 0.01
        return {'x': x, 'w_qkv': w_qkv, 'w_out': w_out, 'b_out': b_out}
    _L1_attn_all = _L1_attn_setup()
    _L1_attn_in = {k: v for k, v in _L1_attn_all.items() if k in ('w_qkv', 'w_out', 'b_out')}
    del _L1_attn_all

    def _L1_xattn_setup():
        import jax, jax.numpy as jnp
        import numpy as np
        N, L, E, H = (4, 256, 128, 16)
        D = E // H
        key = jax.random.key(seed)
        ks = jax.random.split(key, 8)
        return {'values': jax.random.normal(ks[0], (N, L, E), dtype=jnp.float32), 'keys': jax.random.normal(ks[1], (N, L, E), dtype=jnp.float32), 'query': jax.random.normal(ks[2], (N, L, E), dtype=jnp.float32), 'mask': jnp.ones((N, 1, L, L), dtype=jnp.int32), 'Wv': jax.random.normal(ks[3], (D, D), dtype=jnp.float32) * D ** (-0.5), 'Wk': jax.random.normal(ks[4], (D, D), dtype=jnp.float32) * D ** (-0.5), 'Wq': jax.random.normal(ks[5], (D, D), dtype=jnp.float32) * D ** (-0.5), 'Wo': jax.random.normal(ks[6], (E, E), dtype=jnp.float32) * E ** (-0.5), 'bo': jnp.zeros((E,), dtype=jnp.float32)}
    _L1_xattn_all = _L1_xattn_setup()
    _L1_xattn_in = {k: v for k, v in _L1_xattn_all.items() if k in ('Wv', 'Wk', 'Wq', 'Wo', 'bo')}
    del _L1_xattn_all

    def _L1_ffn_setup():
        import jax, jax.numpy as jnp
        import numpy as np
        ALPHA = 1.702
        LIMIT = 9.0
        TOP_K = 2

        def swiglu(x):
            g, v = (x[..., 0::2], x[..., 1::2])
            g = jnp.clip(g, None, LIMIT)
            v = jnp.clip(v, -LIMIT, LIMIT)
            return g * jax.nn.sigmoid(ALPHA * g) * (v + 1)
        key = jax.random.key(seed)
        ks = jax.random.split(key, 6)
        B, L, D = (2, 256, 128)
        E, F = (8, 256)
        s_gate = 1.0 / np.sqrt(D)
        s1 = 1.0 / np.sqrt(D)
        s2 = 1.0 / np.sqrt(F)
        return {'x': jax.random.normal(ks[0], (B, L, D), dtype=jnp.float32), 'gate_w': jax.random.normal(ks[1], (D, E), dtype=jnp.float32) * s_gate, 'dense_1_w': jax.random.normal(ks[2], (E, 2 * F, D), dtype=jnp.float32) * s1, 'dense_1_b': jnp.zeros((E, 2 * F), dtype=jnp.float32), 'dense_2_w': jax.random.normal(ks[3], (E, D, F), dtype=jnp.float32) * s2, 'dense_2_b': jnp.zeros((E, D), dtype=jnp.float32)}
    _L1_ffn_all = _L1_ffn_setup()
    _L1_ffn_in = {k: v for k, v in _L1_ffn_all.items() if k in ('gate_w', 'dense_1_w', 'dense_1_b', 'dense_2_w', 'dense_2_b')}
    del _L1_ffn_all
    return {'x': x, 'ctx_1024': ctx_1024, 'mask_Bx1xSxS2_if1': mask_Bx1xSxS2_if1, 'L0_attn_gamma': _L0_attn_in['gamma'], 'L0_attn_w_q': _L0_attn_in['w_q'], 'L0_attn_w_kv': _L0_attn_in['w_kv'], 'L0_attn_null_kv': _L0_attn_in['null_kv'], 'L0_attn_q_scale': _L0_attn_in['q_scale'], 'L0_attn_k_scale': _L0_attn_in['k_scale'], 'L0_attn_w_out': _L0_attn_in['w_out'], 'L0_xattn_Wq': _L0_xattn_in['Wq'], 'L0_xattn_bq': _L0_xattn_in['bq'], 'L0_xattn_Wk': _L0_xattn_in['Wk'], 'L0_xattn_bk': _L0_xattn_in['bk'], 'L0_xattn_Wv': _L0_xattn_in['Wv'], 'L0_xattn_bv': _L0_xattn_in['bv'], 'L0_xattn_Wo': _L0_xattn_in['Wo'], 'L0_xattn_bo': _L0_xattn_in['bo'], 'L0_ffn_router_w': _L0_ffn_in['router_w'], 'L0_ffn_expert_bias': _L0_ffn_in['expert_bias'], 'L0_ffn_w_gate': _L0_ffn_in['w_gate'], 'L0_ffn_w_down': _L0_ffn_in['w_down'], 'L0_ffn_w_gate_shared': _L0_ffn_in['w_gate_shared'], 'L0_ffn_w_down_shared': _L0_ffn_in['w_down_shared'], 'L1_attn_w_qkv': _L1_attn_in['w_qkv'], 'L1_attn_w_out': _L1_attn_in['w_out'], 'L1_attn_b_out': _L1_attn_in['b_out'], 'L1_xattn_Wv': _L1_xattn_in['Wv'], 'L1_xattn_Wk': _L1_xattn_in['Wk'], 'L1_xattn_Wq': _L1_xattn_in['Wq'], 'L1_xattn_Wo': _L1_xattn_in['Wo'], 'L1_xattn_bo': _L1_xattn_in['bo'], 'L1_ffn_gate_w': _L1_ffn_in['gate_w'], 'L1_ffn_dense_1_w': _L1_ffn_in['dense_1_w'], 'L1_ffn_dense_1_b': _L1_ffn_in['dense_1_b'], 'L1_ffn_dense_2_w': _L1_ffn_in['dense_2_w'], 'L1_ffn_dense_2_b': _L1_ffn_in['dense_2_b']}

def reference(x, ctx_1024, mask_Bx1xSxS2_if1, L0_attn_gamma, L0_attn_w_q, L0_attn_w_kv, L0_attn_null_kv, L0_attn_q_scale, L0_attn_k_scale, L0_attn_w_out, L0_xattn_Wq, L0_xattn_bq, L0_xattn_Wk, L0_xattn_bk, L0_xattn_Wv, L0_xattn_bv, L0_xattn_Wo, L0_xattn_bo, L0_ffn_router_w, L0_ffn_expert_bias, L0_ffn_w_gate, L0_ffn_w_down, L0_ffn_w_gate_shared, L0_ffn_w_down_shared, L1_attn_w_qkv, L1_attn_w_out, L1_attn_b_out, L1_xattn_Wv, L1_xattn_Wk, L1_xattn_Wq, L1_xattn_Wo, L1_xattn_bo, L1_ffn_gate_w, L1_ffn_dense_1_w, L1_ffn_dense_1_b, L1_ffn_dense_2_w, L1_ffn_dense_2_b):
    import jax
    import jax.numpy as jnp

    def _L0_attn_ref(x, gamma, w_q, w_kv, null_kv, q_scale, k_scale, w_out):
        import math
        import jax, jax.numpy as jnp
        import numpy as np
        HEADS = 16
        DIM_HEAD = 64
        NUM_NULL_KV = 2
        ATTN_SCALE = 8.0
        LN_EPS = 1e-05

        def _alibi_slopes(heads):
            start = 2.0 ** (-2.0 ** (-(math.log2(heads) - 3.0)))
            return np.array([start * start ** i for i in range(heads)], dtype=np.float32)

        def _l2norm(t):
            return t / jnp.maximum(jnp.linalg.norm(t, axis=-1, keepdims=True), 1e-12)
        b, n, dim = x.shape
        mu = jnp.mean(x, axis=-1, keepdims=True)
        var = jnp.mean(jnp.square(x - mu), axis=-1, keepdims=True)
        xn = (x - mu) * jax.lax.rsqrt(var + LN_EPS) * gamma
        q = (xn @ w_q).reshape(b, n, HEADS, DIM_HEAD).transpose(0, 2, 1, 3)
        kv = xn @ w_kv
        k, v = jnp.split(kv, 2, axis=-1)
        k = k.reshape(b, n, HEADS, DIM_HEAD).transpose(0, 2, 1, 3)
        v = v.reshape(b, n, HEADS, DIM_HEAD).transpose(0, 2, 1, 3)
        nkv = null_kv.reshape(HEADS, NUM_NULL_KV, 2, DIM_HEAD)
        nk = jnp.broadcast_to(nkv[:, :, 0][None], (b, HEADS, NUM_NULL_KV, DIM_HEAD))
        nv = jnp.broadcast_to(nkv[:, :, 1][None], (b, HEADS, NUM_NULL_KV, DIM_HEAD))
        k = jnp.concatenate([nk, k], axis=2)
        v = jnp.concatenate([nv, v], axis=2)
        q = _l2norm(q) * q_scale
        k = _l2norm(k) * k_scale
        sim = jnp.einsum('bhid,bhjd->bhij', q, k) * ATTN_SCALE
        j = n + NUM_NULL_KV
        rows = jnp.arange(n)
        cols = jnp.arange(j)
        dist = -jnp.abs(cols[None, :] - (rows[:, None] + NUM_NULL_KV)).astype(sim.dtype)
        slopes = jnp.asarray(_alibi_slopes(HEADS))
        sim = sim + dist[None, None] * slopes[None, :, None, None]
        causal_mask = cols[None, :] > rows[:, None] + NUM_NULL_KV
        neg = -jnp.finfo(sim.dtype).max
        sim = jnp.where(causal_mask[None, None], neg, sim)
        attn = jax.nn.softmax(sim, axis=-1)
        out = jnp.einsum('bhij,bhjd->bhid', attn, v)
        out = out.transpose(0, 2, 1, 3).reshape(b, n, HEADS * DIM_HEAD)
        return out @ w_out

    def _L0_xattn_ref(x, y, Wq, bq, Wk, bk, Wv, bv, Wo, bo):
        import jax, jax.numpy as jnp
        import numpy as np
        B, T, D, H = (4, 256, 128, 8)
        HD = D // H

        def _heads(t):
            b, t_, _ = t.shape
            return t.reshape(b, t_, H, HD).transpose(0, 2, 1, 3)
        Tq, Tk = (x.shape[1], y.shape[1])
        q = _heads(x @ Wq.T + bq)
        k = _heads(y @ Wk.T + bk)
        v = _heads(y @ Wv.T + bv)
        scale = 1.0 / np.sqrt(HD)
        logits = jnp.einsum('bhqd,bhkd->bhqk', q, k) * scale
        causal = jnp.triu(jnp.full((Tq, Tk), -jnp.inf, jnp.float32), k=1)
        logits = logits + causal
        attn = jax.nn.softmax(logits, axis=-1)
        ctx = jnp.einsum('bhqk,bhkd->bhqd', attn, v)
        ctx = ctx.transpose(0, 2, 1, 3).reshape(x.shape[0], Tq, D)
        out = ctx @ Wo.T + bo
        return out

    def _L0_ffn_ref(hidden_states, router_w, expert_bias, w_gate, w_down, w_gate_shared, w_down_shared):
        import jax, jax.numpy as jnp
        import numpy as np
        NUM_EXPERTS = 160
        TOP_K = 8
        ROUTED_SCALE = 2.5
        HIDDEN = 128
        INTER = 64
        B, S, H = hidden_states.shape
        x = hidden_states.reshape(-1, H)
        T = x.shape[0]
        logits = x @ router_w.T + expert_bias[None, :]
        probs = jax.nn.sigmoid(logits)
        top_w, top_idx = jax.lax.top_k(probs, TOP_K)
        top_w = top_w / (jnp.sum(top_w, axis=-1, keepdims=True) + 1e-09)
        top_w = top_w * ROUTED_SCALE
        combine = jnp.zeros((T, NUM_EXPERTS), dtype=x.dtype)
        combine = combine.at[jnp.arange(T)[:, None], top_idx].set(top_w)
        h1 = jax.nn.silu(jnp.einsum('th,eih->eti', x, w_gate))
        h1w = h1 * combine.T[:, :, None]
        routed = jnp.einsum('eti,ehi->th', h1w, w_down)
        shared = jax.nn.silu(x @ w_gate_shared.T) @ w_down_shared.T
        return (routed + shared).reshape(B, S, H)

    def _L1_attn_ref(x, w_qkv, w_out, b_out):
        import jax, jax.numpy as jnp
        import numpy as np
        D_MODEL = 128
        N_HEADS = 16
        B, T, D = x.shape
        h = N_HEADS
        Hd = D // h
        qkv = jnp.einsum('btd,de->bte', x, w_qkv).reshape(B, T, 3, h, Hd)
        q = jnp.transpose(qkv[:, :, 0], (0, 2, 1, 3))
        k = jnp.transpose(qkv[:, :, 1], (0, 2, 1, 3))
        v = jnp.transpose(qkv[:, :, 2], (0, 2, 1, 3))
        scale = 1.0 / jnp.sqrt(jnp.array(Hd, dtype=x.dtype))
        logits = jnp.einsum('bhqd,bhkd->bhqk', q, k) * scale
        mask = jnp.tril(jnp.ones((T, T), dtype=x.dtype))
        big_neg = jnp.array(-10000000000.0, dtype=x.dtype)
        logits = logits + (1.0 - mask)[None, None, :, :] * big_neg
        attn = jax.nn.softmax(logits, axis=-1)
        out = jnp.einsum('bhqk,bhkd->bhqd', attn, v)
        out = jnp.transpose(out, (0, 2, 1, 3)).reshape(B, T, D)
        return jnp.einsum('btd,de->bte', out, w_out) + b_out

    def _L1_xattn_ref(values, keys, query, mask, Wv, Wk, Wq, Wo, bo):
        import jax, jax.numpy as jnp
        import numpy as np
        N, L, E, H = (4, 256, 128, 16)
        D = E // H
        n, lq, e = query.shape
        lk = keys.shape[1]
        v = values.reshape(n, lk, H, D) @ Wv.T
        k = keys.reshape(n, lk, H, D) @ Wk.T
        q = query.reshape(n, lq, H, D) @ Wq.T
        energy = jnp.einsum('nqhd,nkhd->nhqk', q, k)
        energy = jnp.where(mask == 0, jnp.float32(-1e+20), energy)
        attn = jax.nn.softmax(energy / jnp.sqrt(jnp.float32(e)), axis=3)
        out = jnp.einsum('nhqk,nkhd->nqhd', attn, v).reshape(n, lq, e)
        return out @ Wo.T + bo

    def _L1_ffn_ref(x, gate_w, dense_1_w, dense_1_b, dense_2_w, dense_2_b):
        import jax, jax.numpy as jnp
        import numpy as np
        ALPHA = 1.702
        LIMIT = 9.0
        TOP_K = 2

        def swiglu(x):
            g, v = (x[..., 0::2], x[..., 1::2])
            g = jnp.clip(g, None, LIMIT)
            v = jnp.clip(v, -LIMIT, LIMIT)
            return g * jax.nn.sigmoid(ALPHA * g) * (v + 1)
        B, L, D = x.shape
        xf = x.reshape(B * L, D)
        gate = xf @ gate_w
        weights, sel = jax.lax.top_k(gate, k=TOP_K)
        weights = jax.nn.softmax(weights, axis=-1)
        h = jnp.einsum('ecd,td->tec', dense_1_w, xf) + dense_1_b[None]
        h = swiglu(h)
        y = jnp.einsum('edf,tef->ted', dense_2_w, h) + dense_2_b[None]
        y_sel = jnp.take_along_axis(y, sel[:, :, None], axis=1)
        out = jnp.einsum('tkd,tk->td', y_sel, weights)
        return out.reshape(B, L, D)
    x = x + _L0_attn_ref(_layernorm(x, axis=-1), L0_attn_gamma, L0_attn_w_q, L0_attn_w_kv, L0_attn_null_kv, L0_attn_q_scale, L0_attn_k_scale, L0_attn_w_out)
    x = x + _L0_xattn_ref(_layernorm(x, axis=-1), ctx_1024, L0_xattn_Wq, L0_xattn_bq, L0_xattn_Wk, L0_xattn_bk, L0_xattn_Wv, L0_xattn_bv, L0_xattn_Wo, L0_xattn_bo)
    x = x + _L0_ffn_ref(_layernorm(x, axis=-1), L0_ffn_router_w, L0_ffn_expert_bias, L0_ffn_w_gate, L0_ffn_w_down, L0_ffn_w_gate_shared, L0_ffn_w_down_shared)
    x = x + _L1_attn_ref(_layernorm(x, axis=-1), L1_attn_w_qkv, L1_attn_w_out, L1_attn_b_out)
    x = x + _L1_xattn_ref(ctx_1024, ctx_1024, _layernorm(x, axis=-1), mask_Bx1xSxS2_if1, L1_xattn_Wv, L1_xattn_Wk, L1_xattn_Wq, L1_xattn_Wo, L1_xattn_bo)
    x = x + _L1_ffn_ref(_layernorm(x, axis=-1), L1_ffn_gate_w, L1_ffn_dense_1_w, L1_ffn_dense_1_b, L1_ffn_dense_2_w, L1_ffn_dense_2_b)
    return x

_drawn_inputs = setup_inputs


def setup_inputs(seed=0):
    import zlib

    import numpy as np

    out = dict(_drawn_inputs(seed))
    spreads = {'L0_attn_gamma': (1.0, 0.2),
     'L0_attn_q_scale': (1.0, 0.6),
     'L0_attn_k_scale': (1.0, 0.59),
     'L0_xattn_bq': (0.0, 0.1),
     'L0_xattn_bk': (0.0, 0.8),
     'L0_xattn_bv': (0.0, 0.1),
     'L0_xattn_bo': (0.0, 0.1),
     'L0_ffn_expert_bias': (0.0, 0.1),
     'L1_xattn_bo': (0.0, 0.1),
     'L1_ffn_dense_1_b': (0.0, 0.1),
     'L1_ffn_dense_2_b': (0.0, 0.1)}
    factors = {}
    for name, (base, spread) in spreads.items():
        noise = np.random.default_rng([zlib.crc32(name.encode()), seed]).standard_normal(out[name].shape)
        drawn = base * np.exp(spread * noise) if base else spread * noise
        out[name] = jnp.asarray(drawn.astype(out[name].dtype))
    for name, factor in factors.items():
        out[name] = (out[name] * factor).astype(out[name].dtype)
    return out
```

```python
from contextlib import ExitStack
import math

import numpy as np

import concourse.bass as bass
from concourse import mybir

ALU = mybir.AluOpType
ACT = mybir.ActivationFunctionType
AX = mybir.AxisListType.X
F32 = mybir.dt.float32
F32R = mybir.dt.float32r
BF16 = mybir.dt.bfloat16
I32 = mybir.dt.int32

P = 128
B = 4
S = 512
D = 128
NT = S // P
TT = B * NT
KC = 77
EPS = 1e-5

H0, HD0 = 16, 64
HC0, HDC0 = 8, 16
H1, HD1 = 16, 8
NE0, IN0, TOP0 = 160, 64, 8
NE1, FF1 = 8, 256
NEG = -1.0e30


def alibi_slopes():
    start = 2.0 ** (-2.0 ** (-(math.log2(H0) - 3.0)))
    return [float(np.float32(start * start ** i)) for i in range(H0)]


class Kernel:

    def __init__(self, nc, ctx, dram, out):
        self.nc, self.ctx, self.dram, self.out = nc, ctx, dram, out
        self.sems = []
        sb = self.sb
        self.ps = ctx.enter_context(nc.psum_tensor("ps", [P, 8, 512], F32))
        self.x = sb(ctx, "x_resid", [P, TT, D])
        self.ident = sb(ctx, "ident", [P, P])
        self.ident_bf = sb(ctx, "ident_bf", [P, P], BF16)
        self.mhalf = sb(ctx, "mhalf", [P, NT])
        self.stats = sb(ctx, "ln_stats", [P, NT, 6])
        self.mv = sb(ctx, "ln_mean_var", [P, NT, 2])
        self.ve = sb(ctx, "ln_var_eps", [P, NT])
        self.rstd = sb(ctx, "ln_rstd", [P, NT])
        self.z = sb(ctx, "ln_out", [P, NT, D])
        self.var_ready = self.sem("var_ready")
        self.rstd_ready = self.sem("rstd_ready")
        self.passed = self.sem("passed")
        self.n_ln = 0
        self.sems = []

    def sb(self, ctx, name, shape, dt=F32):
        return ctx.enter_context(self.nc.sbuf_tensor(name, shape, dt))

    def sem(self, name):
        self.sems.append(self.nc.alloc_semaphore(name=name))
        return self.sems[-1]

    def end_stage(self):
        self.nc.clear_and_free_semaphores(self.sems)
        self.nc.all_engine_barrier()
        self.sems = []

    def settle(self, engine):
        engine.sem_inc(self.passed, 1)

    def bank(self, b):
        return self.ps[:, b, :]


def split_product(pe, out, left, right, start=True, stop=True, skip=False):
    (lh, ll), (rh, rl) = left, right
    pe.matmul(out, lh, rh, start=start, stop=False, skip_group_check=skip)
    pe.matmul(out, ll, rh, start=False, stop=False, skip_group_check=skip)
    return pe.matmul(out, lh, rl, start=False, stop=stop, skip_group_check=skip)


def chain(engine, sem, per_pass=0, i=0):
    count = [0]

    def step(ins, k=None):
        count[0] += 1
        ins.then_inc(sem, 1)
        engine.wait_ge(sem, i * per_pass + count[0])
        if k:
            k.settle(engine)

    step.count = count
    return step


LN_STEPS = 3


def layernorm_vector(k, v, step, src, n_ln, b, lns):
    for t in range(NT):
        last = v.bn_stats(k.stats[:, t, :], src(t))
    step(last, k)
    for t in range(NT):
        last = v.bn_aggr(k.mv[:, t, :], k.stats[:, t, :])
    step(last)
    v.tensor_scalar(k.ve[:], k.mv[:, :, 1], EPS, None, ALU.add).then_inc(k.var_ready, 1)
    v.wait_ge(k.rstd_ready, k.n_ln + b * lns + n_ln + 1)
    for t in range(NT):
        last = v.tensor_scalar(k.z[:, t, :], src(t), k.mv[:, t, 0:1], k.rstd[:, t:t + 1], ALU.subtract, ALU.mult)
    step(last)


def layernorm_pool(k, pool, n_ln, b, lns):
    pool.wait_ge(k.var_ready, k.n_ln + b * lns + n_ln + 1)
    pool.tensor_tensor(k.rstd[:], k.ve[:], k.mhalf[:], ALU.pow).then_inc(k.rstd_ready, 1)


def stage_setup(k):
    nc, d = k.nc, k.dram
    made, x_in = k.sem("const_made"), k.sem("x_loaded")
    with nc.Block() as block:
        @block.sync
        def _(sp):
            sp.dma_start(k.x[:], d["x"].rearrange("b (t p) d -> p (b t) d", p=P)).then_inc(x_in, 16)
            sp.wait_ge(x_in, 16)

        @block.gpsimd
        def _(pool):
            pool.memset(k.mhalf[:], -0.5)
            pool.memset(k.ident[:], 1.0).then_inc(made, 1)
            pool.wait_ge(made, 1)
            pool.affine_select(out=k.ident[:], in_=k.ident[:], compare_op=ALU.is_equal, fill=0.0, base=0,
                               pattern=[[1, P]], channel_multiplier=-1).then_inc(made, 1)
            pool.wait_ge(made, 2)
            pool.tensor_copy(k.ident_bf[:], k.ident[:]).then_inc(made, 1)
            pool.wait_ge(made, 3)


def stage_store(k):
    nc = k.nc
    stored = k.sem("out_stored")
    with nc.Block() as block:
        @block.sync
        def _(sp):
            sp.dma_start(k.out.rearrange("b (t p) d -> p (b t) d", p=P), k.x[:]).then_inc(stored, 16)
            sp.wait_ge(stored, 16)
def stage_attention_0(k):
    nc, d = k.nc, k.dram
    PAIRS = H0 // 2
    NULLS = 2
    W = H0 * HD0
    NK = NULLS + S
    LNS = 2
    STEPS = LN_STEPS * LNS + NT * 4
    slopes = alibi_slopes()

    def keys(i):
        return NULLS + (i + 1) * P

    with ExitStack() as ctx:
        def sb(name, shape, dt=F32):
            return k.sb(ctx, "a0_" + name, shape, dt)

        wqkv = [[sb(f"w{n}{part}", [P, W], F32R) for part in "hl"] for n in "qkv"]
        wo = [sb(f"wo_{part}", [P, PAIRS, D], F32R) for part in "hl"]
        stage = sb("stage", [P, W])
        gamma = sb("gamma", [P, 1])
        qs_col = sb("qs_col", [P, 1])
        ks_col = sb("ks_col", [P, 1])
        kscale = sb("kscale", [P, 1])
        dist = sb("dist", [P, NK])
        nk_raw = sb("nk_raw", [NULLS, H0, HD0])
        nk_sq = sb("nk_sq", [NULLS, H0, HD0])
        nk_r = sb("nk_r", [NULLS, H0])
        nk_n = sb("nk_n", [NULLS, H0, HD0])
        nkh = sb("nkh", [P, PAIRS, NULLS], F32R)
        nkl = sb("nkl", [P, PAIRS, NULLS], F32R)
        nv = sb("nv", [4, PAIRS, P])
        xh, xl = sb("xh", [P, S], F32R), sb("xl", [P, S], F32R)
        sq = sb("sq", [P, 2, W])
        ss = sb("ss", [P, 2, H0])
        norm = sb("norm", [P, 2, H0])
        rnorm = sb("rnorm", [P, 2, H0])
        qn, kn, vv = (sb(n, [P, NT, W]) for n in ("qn", "kn", "vv"))
        qh = [[sb(f"qh{r}{e}", [P, S], F32R) for e in range(2)] for r in range(2)]
        ql = [[sb(f"ql{r}{e}", [P, S], F32R) for e in range(2)] for r in range(2)]
        kh = [sb(f"kh{r}", [P, NK], F32R) for r in range(2)]
        kl = [sb(f"kl{r}", [P, NK], F32R) for r in range(2)]
        ptok = [sb(f"ptok{r}", [P, NT, 4]) for r in range(2)]
        bias = [sb(f"bias{r}", [P, NK]) for r in range(2)]
        sc = [sb(f"sc{r}", [P, NK]) for r in range(2)]
        nmax = sb("nmax", [P, 2, NT])
        sums = sb("sums", [P, 2, NT])
        rsum = sb("rsum", [P, 2, NT])
        prob = sb("prob", [P, 2, NT, NK + 2])
        pt = [[sb(f"pt{r}_{kt}", [P, S - kt * P]) for kt in range(NT)] for r in range(2)]
        pn = sb("pn", [4, S])
        oh, ol = sb("oh", [P, S], F32R), sb("ol", [P, S], F32R)
        yT = sb("yT", [P, S])

        names = ("loaded staged split consts nulls step zT_ready xh_ready xT_ready q_done k_done v_done "
                 "sq_q sq_k ssum norm_ready v_free qT kT qhi_ready qst_ready kh_ready kst_ready bias_ready "
                 "score tile_scored exp_done prob_ready ptr pt_evac nptr npt_evac pv oh_ready o_ready y_done yT_ready "
                 "y_tok batch_done nT nt_done nkh_done rs_ready")
        s = {n: k.sem("a0_" + n) for n in names.split()}
        ps = k.ps
        TB, PB, OB, YB = 4, 5, 6, 7

        weights = [("wq", wqkv[0]), ("wk", wqkv[1]), ("wv", wqkv[2]), ("wo", wo)]

        with nc.Block() as block:
            @block.sync
            def _(sp):
                src = {"wq": d["L0_attn_w_q"], "wk": d["L0_attn_w_kv"][:, 0:W], "wv": d["L0_attn_w_kv"][:, W:2 * W],
                       "wo": d["L0_attn_w_out"].rearrange("(h p) d -> p h d", p=P)}
                for n, (name, _) in enumerate(weights):
                    if n:
                        sp.wait_ge(s["split"], 2 * n)
                    dst = stage[:] if name != "wo" else stage[:].rearrange("p (h d) -> p h d", d=D)
                    sp.dma_start(dst, src[name]).then_inc(s["staged"], 16)
                for col, name in ((gamma, "L0_attn_gamma"),):
                    sp.dma_start(col[:], d[name].rearrange("(p a) -> p a", a=1)).then_inc(s["loaded"], 16)
                for half in range(2):
                    sp.dma_start(qs_col[half * HD0:(half + 1) * HD0, :],
                                 d["L0_attn_q_scale"].rearrange("(p a) -> p a", a=1)).then_inc(s["loaded"], 16)
                    sp.dma_start(ks_col[half * HD0:(half + 1) * HD0, :],
                                 d["L0_attn_k_scale"].rearrange("(p a) -> p a", a=1)).then_inc(s["loaded"], 16)
                nkv = d["L0_attn_null_kv"].rearrange("h (n two) d -> two n h d", two=2)
                sp.dma_start(nk_raw[:], nkv[0]).then_inc(s["loaded"], 16)
                sp.wait_ge(s["nulls"], 1)
                nvp = d["L0_attn_null_kv"].rearrange("(g e) (n two) d -> e two n g d", two=2, e=2)
                for e in range(2):
                    sp.dma_start(nv[2 * e:2 * e + 2, :, e * HD0:(e + 1) * HD0], nvp[e, 1]).then_inc(s["loaded"], 16)
                sp.wait_ge(s["loaded"], 16 * 8)

            @block.gpsimd
            def _(pool):
                pool.memset(nv[:], 0.0).then_inc(s["nulls"], 1)
                for r in range(2):
                    for half in (qh, ql):
                        for e in range(2):
                            pool.memset(half[r][e][:].bitcast(F32), 0.0)
                pool.iota(dist[:], [[1, NK]], base=-(S - P) - NULLS, channel_multiplier=-1,
                          allow_small_or_imprecise_dtypes=True).then_inc(s["consts"], 1)
                pool.wait_ge(s["consts"], 1)
                pool.affine_select(out=dist[:], in_=dist[:], compare_op=ALU.is_ge, fill=NEG,
                                   base=(S - P) + NULLS, pattern=[[-1, NK]], channel_multiplier=1).then_inc(s["consts"], 1)

            @block.scalar
            def _(act):
                for n, (name, halves) in enumerate(weights):
                    act.wait_ge(s["staged"], 16 * (n + 1))
                    dst = halves[0][:] if name != "wo" else halves[0][:].rearrange("p h d -> p (h d)")
                    act.activation(dst, stage[:], ACT.Copy).then_inc(s["split"], 1)
                act.wait_ge(s["nt_done"], 1)
                act.activation(nk_r[:], nk_r[:], ACT.Sqrt).then_inc(s["nt_done"], 1)
                act.wait_ge(s["nT"], 1)
                act.activation(nkh[:].rearrange("p h n -> p (h n)"), ps[:, 0, 0:H0], ACT.Identity,
                               scale=kscale[:, 0:1]).then_inc(s["nkh_done"], 1)

            @block.vector
            def _(v):
                for n, (name, halves) in enumerate(weights):
                    v.wait_ge(s["split"], 2 * n + 1)
                    flat = (lambda t: t[:]) if name != "wo" else (lambda t: t[:].rearrange("p h d -> p (h d)"))
                    v.tensor_tensor(flat(halves[1]), stage[:], flat(halves[0]).bitcast(F32), ALU.subtract).then_inc(s["split"], 1)
                step = chain(v, s["step"])
                v.wait_ge(s["loaded"], 16 * 8)
                step(v.scalar_tensor_tensor(kscale[:], qs_col[:], 8.0, ks_col[:], ALU.mult, ALU.mult))
                step(v.tensor_tensor(nk_sq[:], nk_raw[:], nk_raw[:], ALU.mult))
                v.tensor_reduce(nk_r[:], nk_sq[:], AX, ALU.add).then_inc(s["nt_done"], 1)
                v.wait_ge(s["nt_done"], 2)
                step(v.tensor_scalar(nk_r[:], nk_r[:], 1e-12, None, ALU.max))
                step(v.reciprocal(nk_r[:], nk_r[:]))
                v.tensor_tensor(nk_n[:], nk_raw[:], nk_r[:].unsqueeze(2).to_broadcast([NULLS, H0, HD0]), ALU.mult).then_inc(s["nt_done"], 1)
                v.wait_ge(s["nkh_done"], 1)
                v.scalar_tensor_tensor(nkl[:].rearrange("p h n -> p (h n)"), ps[:, 0, 0:H0], kscale[:, 0:1],
                                       nkh[:].rearrange("p h n -> p (h n)").bitcast(F32), ALU.mult, ALU.subtract)

            @block.tensor
            def _(pe):
                pe.wait_ge(s["nt_done"], 3)
                for g in range(PAIRS):
                    last = pe.transpose(ps[:, 0, NULLS * g:NULLS * g + NULLS],
                                        nk_n[:, 2 * g:2 * g + 2, :].rearrange("p e d -> p (e d)"), k.ident[0:NULLS, 0:NULLS])
                last.then_inc(s["nT"], 1)

        step0 = 4

        with nc.Block() as block:
            @block.vector
            def _(v):
                with v.Fori(0, B) as b:
                    v.wait_ge(s["batch_done"], b)
                    step = chain(v, s["step"], STEPS, b)
                    step.count[0] = step0
                    layernorm_vector(k, v, step, lambda t: k.x[:, b * NT + t, :], 0, b, LNS)
                    layernorm_vector(k, v, step, lambda t: k.z[:, t, :], 1, b, LNS)
                    v.wait_ge(s["xh_ready"], b + 1)
                    v.scalar_tensor_tensor(xl[:], k.bank(0), gamma[:, 0:1], xh[:].bitcast(F32), ALU.mult,
                                           ALU.subtract).then_inc(s["xT_ready"], 1)
                    for t in range(NT):
                        v.wait_ge(s["sq_q"], b * NT + t + 1)
                        v.tensor_reduce(ss[:, 0, :], sq[:, 0, :].rearrange("p (h e) -> p h e", e=HD0), AX, ALU.add)
                        v.wait_ge(s["sq_k"], b * NT + t + 1)
                        v.tensor_reduce(ss[:, 1, :], sq[:, 1, :].rearrange("p (h e) -> p h e", e=HD0), AX,
                                        ALU.add).then_inc(s["ssum"], 1)
                        v.wait_ge(s["norm_ready"], b * NT + t + 1)
                        step(v.tensor_scalar(norm[:], norm[:], 1e-12, None, ALU.max))
                        step(v.reciprocal(rnorm[:], norm[:]))
                        for j, dst in enumerate((qn, kn)):
                            step(v.tensor_tensor(dst[:, t, :].rearrange("p (h e) -> p h e", e=HD0),
                                                 ps[:, 2 * j:2 * j + 2, :].rearrange("p a (h e) -> p (a h) e", e=HD0),
                                                 rnorm[:, j, :].unsqueeze(2).to_broadcast([P, H0, HD0]), ALU.mult))

                    def prepare_q(g):
                        r = g % 2
                        v.wait_ge(s["qhi_ready"], b * PAIRS + g + 1)
                        for e in range(2):
                            rows = slice(e * HD0, (e + 1) * HD0)
                            last = v.tensor_tensor(ql[r][e][rows, :], ps[rows, TB, :], qh[r][e][rows, :].bitcast(F32),
                                                   ALU.subtract)
                        last.then_inc(s["qst_ready"], 1)

                    def prepare_k(g):
                        r = g % 2
                        v.wait_ge(s["kh_ready"], b * PAIRS + g + 1)
                        v.scalar_tensor_tensor(kl[r][:, NULLS:NK], ps[:, TB, :], kscale[:, 0:1],
                                               kh[r][:, NULLS:NK].bitcast(F32), ALU.mult, ALU.subtract).then_inc(s["kst_ready"], 1)

                    def scores(h):
                        r = h % 2
                        v.wait_ge(s["bias_ready"], b * H0 + h + 1)
                        for i in range(NT):
                            u = h * NT + i
                            v.wait_ge(s["score"], b * H0 * NT + u + 1)
                            if u >= 2:
                                v.wait_ge(s["exp_done"], b * H0 * NT + u - 1)
                            k.settle(v)
                            v.tensor_tensor_reduce(sc[u % 2][:, 0:keys(i)],
                                                   ps[:, 2 * (u % 2):2 * (u % 2) + 2, :].rearrange("p a n -> p (a n)")[:, 0:keys(i)],
                                                   bias[r][:, S - P - i * P:NK], -1.0, 3.0e38, ALU.add, ALU.min,
                                                   nmax[:, r, i:i + 1]).then_inc(s["tile_scored"], 1)
                        v.wait_ge(s["exp_done"], b * H0 * NT + h * NT + NT)
                        v.reciprocal(rsum[:, r, :], sums[:, r, :]).then_inc(s["rs_ready"], 1)

                    def evacuate(h):
                        r = h % 2
                        for kt in (1, 3):
                            v.wait_ge(s["ptr"], b * H0 * NT + h * NT + kt + 1)
                            if h >= 2:
                                v.wait_ge(s["pv"], b * H0 + h - 1)
                            v.tensor_copy(pt[r][kt][:], ps[:, PB, 0:S - kt * P]).then_inc(s["pt_evac"], 1)

                    prepare_q(0)
                    prepare_k(0)
                    scores(0)
                    for h in range(H0):
                        if h // 2 + 1 < PAIRS:
                            (prepare_k if h % 2 else prepare_q)(h // 2 + 1)
                        evacuate(h)
                        if h % 2:
                            g = h // 2
                            v.wait_ge(s["oh_ready"], b * PAIRS + g + 1)
                            v.tensor_tensor(ol[:], k.bank(OB), oh[:].bitcast(F32), ALU.subtract).then_inc(s["o_ready"], 1)
                        if h + 1 < H0:
                            scores(h + 1)
                    v.wait_ge(s["y_tok"], b + 1)
                    v.tensor_tensor(k.x[:, bass.ds(b * NT, NT), :], k.x[:, bass.ds(b * NT, NT), :],
                                    k.bank(TB).rearrange("p (t d) -> p t d", d=D), ALU.add).then_inc(s["batch_done"], 1)
                    assert step.count[0] == step0 + STEPS

            @block.gpsimd
            def _(pool):
                with pool.Fori(0, B) as b:
                    pool.wait_ge(s["batch_done"], b)
                    layernorm_pool(k, pool, 0, b, LNS)
                    layernorm_pool(k, pool, 1, b, LNS)

                    def head_constants(h):
                        r = h % 2
                        if h >= 2:
                            pool.wait_ge(s["tile_scored"], b * H0 * NT + (h - 1) * NT)
                        k.settle(pool)
                        last = pool.tensor_scalar(bias[r][:], dist[:], slopes[h], 1.0, ALU.mult, ALU.mult)
                        if h % 2 == 0:
                            r = h // 2 % 2
                            pool.tensor_copy(kh[r][:, 0:NULLS], nkh[:, h // 2, :].bitcast(F32))
                            last = pool.tensor_copy(kl[r][:, 0:NULLS], nkl[:, h // 2, :].bitcast(F32))
                        last.then_inc(s["bias_ready"], 1)

                    head_constants(0)
                    for h in range(H0):
                        r = h % 2
                        if h + 1 < H0:
                            head_constants(h + 1)
                        pool.wait_ge(s["rs_ready"], b * H0 + h + 1)
                        k.settle(pool)
                        for i in range(NT):
                            last = pool.tensor_scalar(prob[:, r, i, 0:keys(i)], prob[:, r, i, 0:keys(i)], rsum[:, r, i:i + 1],
                                                      0.0, ALU.mult, ALU.add)
                        last.then_inc(s["prob_ready"], 1)
                        pool.wait_ge(s["prob_ready"], b * 2 * H0 + 2 * h + 1)
                        k.settle(pool)
                        pool.tensor_copy(ptok[h // 2 % 2][:, :, 2 * r:2 * r + 2], prob[:, r, :, 0:NULLS]).then_inc(s["prob_ready"], 1)

            @block.scalar
            def _(act):
                with act.Fori(0, B) as b:
                    act.wait_ge(s["zT_ready"], b + 1)
                    act.activation(xh[:], k.bank(0), ACT.Identity, scale=gamma[:, 0:1]).then_inc(s["xh_ready"], 1)
                    for t in range(NT):
                        n = b * NT + t + 1
                        act.wait_ge(s["q_done"], n)
                        act.activation(sq[:, 0, :], ps[:, 0:2, :].rearrange("p a n -> p (a n)"), ACT.Square).then_inc(s["sq_q"], 1)
                        act.wait_ge(s["k_done"], n)
                        act.activation(sq[:, 1, :], ps[:, 2:4, :].rearrange("p a n -> p (a n)"), ACT.Square).then_inc(s["sq_k"], 1)
                        act.wait_ge(s["v_done"], n)
                        act.activation(vv[:, t, :], ps[:, 6:8, :].rearrange("p a n -> p (a n)"), ACT.Copy).then_inc(s["v_free"], 1)
                        act.wait_ge(s["ssum"], n)
                        act.activation(norm[:], ss[:], ACT.Sqrt).then_inc(s["norm_ready"], 1)

                    def prepare_q(g):
                        act.wait_ge(s["qT"], b * PAIRS + g + 1)
                        for e in range(2):
                            rows = slice(e * HD0, (e + 1) * HD0)
                            last = act.activation(qh[g % 2][e][rows, :], ps[rows, TB, :], ACT.Copy)
                        last.then_inc(s["qhi_ready"], 1)

                    def prepare_k(g):
                        r = g % 2
                        act.wait_ge(s["kT"], b * PAIRS + g + 1)
                        act.activation(kh[r][:, NULLS:NK], ps[:, TB, :], ACT.Identity, scale=kscale[:, 0:1]).then_inc(s["kh_ready"], 1)

                    def exps(h):
                        r = h % 2
                        for i in range(NT):
                            u = h * NT + i
                            act.wait_ge(s["tile_scored"], b * H0 * NT + u + 1)
                            if h >= 2:
                                act.wait_ge(s["ptr"], b * H0 * NT + (h - 1) * NT)
                                if h % 2 == 0:
                                    act.wait_ge(s["nptr"], b * PAIRS + h // 2)
                            act.activation(prob[:, r, i, 0:keys(i)], sc[u % 2][:, 0:keys(i)], ACT.Exp, scale=-1.0,
                                           bias=nmax[:, r, i:i + 1], accum_out=sums[:, r, i:i + 1]).then_inc(s["exp_done"], 1)

                    def evacuate(h):
                        r = h % 2
                        for kt in (0, 2):
                            act.wait_ge(s["ptr"], b * H0 * NT + h * NT + kt + 1)
                            if h >= 2:
                                act.wait_ge(s["pv"], b * H0 + h - 1)
                            act.activation(pt[r][kt][:], ps[:, PB, 0:S - kt * P], ACT.Copy).then_inc(s["pt_evac"], 1)

                    prepare_q(0)
                    prepare_k(0)
                    exps(0)
                    for h in range(H0):
                        if h // 2 + 1 < PAIRS:
                            (prepare_k if h % 2 else prepare_q)(h // 2 + 1)
                        evacuate(h)
                        if h % 2:
                            g = h // 2
                            act.wait_ge(s["nptr"], b * PAIRS + g + 1)
                            act.activation(pn[:], ps[0:4, TB, :], ACT.Copy).then_inc(s["npt_evac"], 1)
                            act.wait_ge(s["pv"], b * H0 + h + 1)
                            if g:
                                act.wait_ge(s["y_done"], b * PAIRS + g)
                            act.activation(oh[:], k.bank(OB), ACT.Copy).then_inc(s["oh_ready"], 1)
                        if h + 1 < H0:
                            exps(h + 1)
                    act.wait_ge(s["y_done"], b * PAIRS + PAIRS)
                    act.activation(yT[:], k.bank(YB), ACT.Copy).then_inc(s["yT_ready"], 1)

            @block.tensor
            def _(pe):
                with pe.Fori(0, B) as b:
                    pe.wait_ge(s["step"], b * STEPS + step0 + 2 * LN_STEPS)
                    for t in range(NT):
                        last = pe.transpose(ps[:, 0, t * P:(t + 1) * P], k.z[:, t, :], k.ident[:])
                    last.then_inc(s["zT_ready"], 1)
                    pe.wait_ge(s["xT_ready"], b + 1)
                    for t in range(NT):
                        tok = slice(t * P, (t + 1) * P)
                        for j, done in ((0, "q_done"), (1, "k_done"), (2, "v_done")):
                            if t and j < 2:
                                pe.wait_ge(s["step"], b * STEPS + step0 + 2 * LN_STEPS + 4 * (t - 1) + 3 + j)
                            if t and j == 2:
                                pe.wait_ge(s["v_free"], b * NT + t)
                            for half in range(2):
                                cols = slice(half * 512, half * 512 + 512)
                                last = split_product(pe, k.bank((0, 2, 6)[j] + half), (xh[:, tok], xl[:, tok]),
                                                     (wqkv[j][0][:, cols], wqkv[j][1][:, cols]))
                            last.then_inc(s[done], 1)
                    pe.wait_ge(s["v_free"], b * NT + NT)

                    def prepare(g, src, done):
                        for t in range(NT):
                            last = pe.transpose(ps[:, TB, t * P:(t + 1) * P], src[:, t, g * P:(g + 1) * P], k.ident[:])
                        last.then_inc(s[done], 1)

                    def scores(h):
                        r, e = h // 2 % 2, h % 2
                        if e == 0:
                            pe.wait_ge(s["kst_ready"], b * PAIRS + h // 2 + 1)
                            pe.wait_ge(s["bias_ready"], b * H0 + h + 1)
                        for i in range(NT):
                            u = h * NT + i
                            if u >= 2:
                                pe.wait_ge(s["tile_scored"], b * H0 * NT + u - 1)
                            tile = slice(i * P, (i + 1) * P)
                            for lo, hi, bk in ((0, min(keys(i), 512), 0), (512, keys(i), 1)):
                                if hi <= lo:
                                    continue
                                out = ps[:, 2 * (u % 2) + bk, 0:hi - lo]
                                last = split_product(pe, out, (qh[r][e][:, tile], ql[r][e][:, tile]),
                                                     (kh[r][:, lo:hi], kl[r][:, lo:hi]))
                            last.then_inc(s["score"], 1)

                    def transpose_probs(h, kt):
                        r, u = h % 2, h * NT + kt
                        if u:
                            pe.wait_ge(s["pt_evac"], b * H0 * NT + u)
                        if kt == 0:
                            pe.wait_ge(s["prob_ready"], b * 2 * H0 + 2 * h + 1)
                        for i in range(kt, NT):
                            last = pe.transpose(ps[:, PB, (i - kt) * P:(i - kt + 1) * P],
                                                prob[:, r, i, NULLS + kt * P:NULLS + (kt + 1) * P], k.ident[:])
                        last.then_inc(s["ptr"], 1)

                    def values(h, kt):
                        r, e = h % 2, h % 2
                        pe.wait_ge(s["pt_evac"], b * H0 * NT + h * NT + kt + 1)
                        last = pe.matmul(ps[e * HD0:(e + 1) * HD0, OB, kt * P:S], vv[:, kt, h * HD0:(h + 1) * HD0], pt[r][kt][:],
                                         start=(kt == 0), stop=(kt == NT - 1 and e == 0), skip_group_check=True)
                        if kt == NT - 1 and e == 0:
                            last.then_inc(s["pv"], 1)

                    def pair_nulls(g):
                        pe.wait_ge(s["kst_ready"], b * PAIRS + min(g + 2, PAIRS))
                        pe.wait_ge(s["prob_ready"], b * 2 * H0 + 4 * g + 4)
                        for i in range(NT):
                            last = pe.transpose(ps[0:4, TB, i * P:(i + 1) * P], ptok[g % 2][:, i, :], k.ident[:])
                        last.then_inc(s["nptr"], 1)

                    def pair_end(g):
                        pe.wait_ge(s["npt_evac"], b * PAIRS + g + 1)
                        pe.matmul(k.bank(OB), nv[:, g, :], pn[:], start=False, stop=True,
                                  skip_group_check=True).then_inc(s["pv"], 1)

                    def project(g):
                        pe.wait_ge(s["o_ready"], b * PAIRS + g + 1)
                        split_product(pe, k.bank(YB), (wo[0][:, g, :], wo[1][:, g, :]), (oh[:], ol[:]), start=(g == 0),
                                      stop=(g == PAIRS - 1)).then_inc(s["y_done"], 1)

                    pe.wait_ge(s["step"], b * STEPS + step0 + 2 * LN_STEPS + 4 * NT)
                    prepare(0, qn, "qT")
                    pe.wait_ge(s["qst_ready"], b * PAIRS + 1)
                    prepare(0, kn, "kT")
                    scores(0)
                    for h in range(H0):
                        g = h // 2
                        if h % 2 == 0 and g + 1 < PAIRS:
                            if g:
                                pe.wait_ge(s["npt_evac"], b * PAIRS + g)
                            prepare(g + 1, qn, "qT")
                        transpose_probs(h, 0)
                        if h % 2 and g + 1 < PAIRS:
                            pe.wait_ge(s["qst_ready"], b * PAIRS + g + 2)
                            prepare(g + 1, kn, "kT")
                        if h % 2 == 0 and h:
                            pe.wait_ge(s["o_ready"], b * PAIRS + h // 2)
                        for kt in range(1, NT):
                            transpose_probs(h, kt)
                            values(h, kt - 1)
                        values(h, NT - 1)
                        if h % 2:
                            pair_nulls(h // 2)
                            pair_end(h // 2)
                        if h + 1 < H0:
                            scores(h + 1)
                        if h % 2:
                            project(h // 2)
                    pe.wait_ge(s["yT_ready"], b + 1)
                    for t in range(NT):
                        last = pe.transpose(ps[:, TB, t * P:(t + 1) * P], yT[:, t * P:(t + 1) * P], k.ident[:])
                    last.then_inc(s["y_tok"], 1)
    k.n_ln = k.n_ln + B * LNS


def cross_attention(k, pre, heads, hd, weights, biases, out_bias, scale, causal, mask):
    nc, d = k.nc, k.dram
    HALF = 8
    U1 = heads // HALF
    U = NT * U1
    G = heads // 4
    LNS = 1
    STEPS = LN_STEPS + U * (2 + 2 * (mask is not None)) + U1 * causal + NT - 1

    with ExitStack() as ctx:
        def sb(name, shape, dt=F32):
            return k.sb(ctx, pre + name, shape, dt)

        def sem(name):
            return k.sem(pre + name)

        w_nat = sb("w_nat", [P, 4, P])
        w = sb("w", [P, 3, P])
        wo = sb("wo", [P, G, P])
        woT = sb("woT", [P, P])
        bcol = sb("bcol", [P, 2])
        brow = sb("brow", [P, 2, P])
        head_mask = sb("head_mask", [P, heads])
        ctx_nat = sb("ctx_nat", [KC, B, D])
        ctxT = sb("ctxT", [P, B, KC])
        kT = sb("kT", [P, B, KC])
        kb = sb("kb", [P, B, heads, KC])
        vall = sb("vall", [KC, B, P])
        vpad = sb("vpad", [KC, heads, 32])
        zT, qT = sb("zT", [P, S]), sb("qT", [P, S])
        sc = [sb(f"sc{r}", [P, HALF, KC]) for r in range(2)]
        pr = [sb(f"pr{r}", [P, HALF, KC]) for r in range(2)]
        mx = [sb(f"mx{r}", [P, HALF]) for r in range(2)]
        sm = [sb(f"sm{r}", [P, HALF]) for r in range(2)]
        rs = sb("rs", [P, HALF])
        pT = [sb(f"pT{r}", [KC, HALF, P]) for r in range(2)]
        oT = [sb(f"oT{r}", [P, 2, P]) for r in range(2)]
        cmask = sb("cmask", [P, KC])
        if mask is not None:
            mraw = sb("mraw", [P, TT, KC], I32)
            keep = sb("keep", [P, TT, KC])
            drop = sb("drop", [P, TT, KC])

        names = ("loaded zeroed wT wT_out ctxTr ctxT_out kv_done kv_out zTr zT_out q_done q_out vpad_done score "
                 "scored exp_done norm ptr pt_evac pv o_evac y_done batch_done step woz wo_out consts y_used")
        s = {n: sem(n) for n in names.split()}
        ps = k.ps
        diag = weights[0].shape[0] == hd
        n_loads = 0

        with nc.Block() as block:
            loads = []
            if diag:
                for j in range(3):
                    for h in range(heads):
                        rows = slice(h * hd, (h + 1) * hd)
                        loads.append((w_nat[rows, j, rows], weights[j]))
            else:
                for j in range(3):
                    loads.append((w_nat[:, j, :], weights[j]))
            loads.append((w_nat[:, 3, :], weights[3]))
            loads.append((ctx_nat[:], d["ctx_1024"].rearrange("b k d -> k b d")))
            if biases is not None:
                for j in range(2):
                    loads.append((bcol[:, j:j + 1], biases[j].rearrange("(p a) -> p a", a=1)))
                loads.append((brow[:, 0, :], biases[2].partition_broadcast(P)))
            loads.append((brow[:, 1, :], out_bias.partition_broadcast(P)))
            if mask is not None:
                loads.append((mraw[:], mask.rearrange("b a (t p) k -> p (b a t) k", p=P)))

            @block.sync
            def _(sp):
                sp.wait_ge(s["zeroed"], 1)
                for dst, src in loads:
                    sp.dma_start(dst, src).then_inc(s["loaded"], 16)
                sp.wait_ge(s["loaded"], 16 * len(loads))

            @block.gpsimd
            def _(pool):
                pool.memset(vpad[:], 0.0)
                if biases is None:
                    pool.memset(bcol[:], 0.0)
                    pool.memset(brow[:, 0, :], 0.0)
                pool.memset(w_nat[:], 0.0).then_inc(s["zeroed"], 1)
                pool.memset(woT[:], 1.0)
                pool.memset(cmask[:], 0.0)
                pool.memset(head_mask[:], 1.0).then_inc(s["consts"], 1)
                pool.wait_ge(s["consts"], 1)
                pool.affine_select(out=head_mask[:], in_=head_mask[:], compare_op=ALU.is_ge, fill=0.0, base=0,
                                   pattern=[[-hd, heads]], channel_multiplier=1).then_inc(s["consts"], 1)
                pool.wait_ge(s["consts"], 2)
                pool.affine_select(out=head_mask[:], in_=head_mask[:], compare_op=ALU.is_ge, fill=0.0, base=hd - 1,
                                   pattern=[[hd, heads]], channel_multiplier=-1).then_inc(s["consts"], 1)
                pool.affine_select(out=cmask[:], in_=cmask[:], compare_op=ALU.is_ge, fill=NEG, base=0,
                                   pattern=[[-1, KC]], channel_multiplier=1).then_inc(s["consts"], 1)
                pool.wait_ge(s["consts"], 4)

            @block.tensor
            def _(pe):
                pe.wait_ge(s["loaded"], 16 * len(loads))
                for j in range(3):
                    last = pe.transpose(ps[:, 0, j * P:(j + 1) * P], w_nat[:, j, :], k.ident[:])
                last.then_inc(s["wT"], 1)
                for g in range(G):
                    for j in range(4):
                        h = 4 * g + j
                        last = pe.transpose(ps[0:hd, 1 + g, j * P:(j + 1) * P],
                                            w_nat[:, 3, h * hd:(h + 1) * hd], k.ident[:])
                last.then_inc(s["wT"], 1)
                for b in range(B):
                    last = pe.transpose(ps[:, 6, b * KC:(b + 1) * KC], ctx_nat[:, b, :], k.ident[0:KC, 0:KC])
                last.then_inc(s["ctxTr"], 1)
                pe.wait_ge(s["ctxT_out"], 1)
                pe.wait_ge(s["wT_out"], 1)
                pe.matmul(ps[:, 7, 0:B * KC], w[:, 1, :], ctxT[:].rearrange("p b k -> p (b k)"), start=True,
                          stop=True).then_inc(s["kv_done"], 1)
                for b in range(B):
                    last = pe.matmul(ps[0:KC, 0, b * P:(b + 1) * P], ctxT[:, b, :], w[:, 2, :], start=True, stop=True)
                last.then_inc(s["kv_done"], 1)

            @block.scalar
            def _(act):
                act.wait_ge(s["wT"], 1)
                act.activation(w[:].rearrange("p j d -> p (j d)"), ps[:, 0, 0:3 * P], ACT.Copy).then_inc(s["wT_out"], 1)
                act.wait_ge(s["kv_done"], 1)
                act.activation(kT[:].rearrange("p b k -> p (b k)"), ps[:, 7, 0:B * KC], ACT.Identity,
                               bias=bcol[:, 1:2]).then_inc(s["kv_out"], 1)

            @block.vector
            def _(v):
                v.memset(wo[:], 0.0).then_inc(s["woz"], 1)
                v.wait_ge(s["woz"], 1)
                v.wait_ge(s["wT"], 2)
                for h in range(heads):
                    last = v.tensor_copy(wo[32 * (h % 4):32 * (h % 4) + hd, h // 4, :], ps[0:hd, 1 + h // 4, (h % 4) * P:(h % 4 + 1) * P])
                last.then_inc(s["wo_out"], 1)
                v.wait_ge(s["ctxTr"], 1)
                v.tensor_copy(ctxT[:].rearrange("p b k -> p (b k)"), ps[:, 6, 0:B * KC]).then_inc(s["ctxT_out"], 1)
                v.wait_ge(s["consts"], 4)
                v.wait_ge(s["kv_out"], 1)
                for b in range(B):
                    v.tensor_tensor(kb[:, b, :, :], kT[:, b, :].unsqueeze(1).to_broadcast([P, heads, KC]),
                                    head_mask[:].unsqueeze(2).to_broadcast([P, heads, KC]), ALU.mult)
                v.wait_ge(s["kv_done"], 2)
                v.tensor_tensor(vall[:], ps[0:KC, 0, :].rearrange("p (b d) -> p b d", d=P),
                                brow[0:KC, 0, :].unsqueeze(1).to_broadcast([KC, B, P]), ALU.add)
                if mask is not None:
                    v.tensor_scalar(keep[:], mraw[:], 0, None, ALU.not_equal)
                    v.tensor_scalar(drop[:], mraw[:], 0, -1.0e20, ALU.is_equal, ALU.mult)

        with nc.Block() as block:
            @block.gpsimd
            def _(pool):
                with pool.Fori(0, B) as b:
                    pool.wait_ge(s["batch_done"], b)
                    layernorm_pool(k, pool, 0, b, LNS)
                    pool.tensor_copy(vpad[:, :, 0:hd], vall[:, b, :].rearrange("p (h e) -> p h e", e=hd)).then_inc(s["vpad_done"], 1)
                    for u in range(U):
                        pool.wait_ge(s["norm"], b * 2 * U + 2 * u + 1)
                        pool.tensor_tensor(pr[u % 2][:], pr[u % 2][:], rs[:].unsqueeze(2).to_broadcast([P, HALF, KC]), ALU.mult).then_inc(s["norm"], 1)

            @block.vector
            def _(v):
                with v.Fori(0, B) as b:
                    step = chain(v, s["step"], STEPS, b)
                    layernorm_vector(k, v, step, lambda t: k.x[:, b * NT + t, :], 0, b, LNS)

                    def soften(u):
                        i, half = u // U1, u % U1
                        v.wait_ge(s["score"], b * U + u + 1)
                        if u >= 2:
                            v.wait_ge(s["exp_done"], b * U + u - 1)
                        src = ps[:, 2 * (u % 2):2 * (u % 2) + 2, :].rearrange("p a (h n) -> p (a h) n", n=P)[:, :, 0:KC]
                        dst = sc[u % 2][:]
                        if mask is not None:
                            step(v.tensor_tensor(dst, src, keep[:, b * NT + i, :].unsqueeze(1).to_broadcast([P, HALF, KC]), ALU.mult))
                            step(v.tensor_tensor(dst, dst, drop[:, b * NT + i, :].unsqueeze(1).to_broadcast([P, HALF, KC]), ALU.add))
                            src = dst
                        elif causal and i == 0:
                            step(v.tensor_tensor(dst, src, cmask[:].unsqueeze(1).to_broadcast([P, HALF, KC]), ALU.add))
                            src = dst
                        step(v.tensor_reduce(mx[u % 2][:], src, AX, ALU.max))
                        v.tensor_tensor(dst, src, mx[u % 2][:].unsqueeze(2).to_broadcast([P, HALF, KC]),
                                        ALU.subtract).then_inc(s["scored"], 1)

                    def invert(u):
                        v.wait_ge(s["exp_done"], b * U + u + 1)
                        step(v.tensor_reduce(sm[u % 2][:], pr[u % 2][:], AX, ALU.add))
                        if u:
                            v.wait_ge(s["norm"], b * 2 * U + 2 * u)
                        v.reciprocal(rs[:], sm[u % 2][:]).then_inc(s["norm"], 1)

                    def finish(u):
                        v.wait_ge(s["pv"], b * U + u + 1)
                        v.tensor_copy(oT[u % 2][:].rearrange("p g q -> p (g q)"), ps[:, 6, 0:2 * P]).then_inc(s["o_evac"], 1)
                        if u % U1 == U1 - 1:
                            i = u // U1
                            v.wait_ge(s["y_done"], b * U + u + 1)
                            v.tensor_tensor(k.x[:, b * NT + i, :], k.x[:, b * NT + i, :], ps[:, 7, 0:P],
                                            ALU.add).then_inc(s["y_used"], 1)
                            v.wait_ge(s["y_used"], b * NT + i + 1)
                            last = v.tensor_tensor(k.x[:, b * NT + i, :], k.x[:, b * NT + i, :], brow[:, 1, :], ALU.add)
                            if i < NT - 1:
                                step(last)
                            else:
                                last.then_inc(s["batch_done"], 1)

                    soften(0)
                    for u in range(U):
                        if u + 1 < U:
                            soften(u + 1)
                        invert(u)
                        finish(u)
                    assert step.count[0] == STEPS, (step.count[0], STEPS)

            @block.scalar
            def _(act):
                with act.Fori(0, B) as b:
                    act.wait_ge(s["zTr"], b + 1)
                    act.activation(zT[:], k.bank(4), ACT.Copy).then_inc(s["zT_out"], 1)
                    act.wait_ge(s["q_done"], b + 1)
                    act.activation(qT[:], k.bank(5), ACT.Identity, bias=bcol[:, 0:1]).then_inc(s["q_out"], 1)

                    def exps(u):
                        act.wait_ge(s["scored"], b * U + u + 1)
                        if u >= 2:
                            act.wait_ge(s["ptr"], b * U + u - 1)
                        act.activation(pr[u % 2][:], sc[u % 2][:], ACT.Exp, scale=scale).then_inc(s["exp_done"], 1)

                    exps(0)
                    for u in range(U):
                        if u + 1 < U:
                            exps(u + 1)
                        act.wait_ge(s["ptr"], b * U + u + 1)
                        if u >= 2:
                            act.wait_ge(s["pv"], b * U + u - 1)
                        act.activation(pT[u % 2][:].rearrange("p h q -> p (h q)"),
                                       ps[0:KC, 4:6, :].rearrange("p a n -> p (a n)"), ACT.Copy).then_inc(s["pt_evac"], 1)

            @block.tensor
            def _(pe):
                with pe.Fori(0, B) as b:
                    pe.wait_ge(s["step"], b * STEPS + LN_STEPS)
                    for t in range(NT):
                        last = pe.transpose(ps[:, 4, t * P:(t + 1) * P], k.z[:, t, :], k.ident[:])
                    last.then_inc(s["zTr"], 1)
                    pe.wait_ge(s["zT_out"], b + 1)
                    pe.matmul(k.bank(5), w[:, 0, :], zT[:], start=True, stop=True).then_inc(s["q_done"], 1)
                    pe.wait_ge(s["q_out"], b + 1)

                    def scores(u):
                        i, half = u // U1, u % U1
                        if u >= 2:
                            pe.wait_ge(s["scored"], b * U + u - 1)
                        for a in range(2):
                            h = half * HALF + 4 * a
                            last = pe.matmul(ps[:, 2 * (u % 2) + a, :].rearrange("p (h n) -> p h n", n=P)[:, :, 0:KC], qT[:, i * P:(i + 1) * P],
                                             kb[:, b, h:h + 4, :], start=True, stop=True)
                        last.then_inc(s["score"], 1)

                    def values(u):
                        i, half = u // U1, u % U1
                        pe.wait_ge(s["pt_evac"], b * U + u + 1)
                        if u == 0:
                            pe.wait_ge(s["vpad_done"], b + 1)
                        else:
                            pe.wait_ge(s["o_evac"], b * U + u)
                        for j in range(HALF):
                            last = pe.matmul(ps[32 * (j % 4):32 * (j % 4) + 32, 6, (j // 4) * P:(j // 4 + 1) * P],
                                             vpad[:, half * HALF + j, :], pT[u % 2][:, j, :], start=True, stop=True)
                        last.then_inc(s["pv"], 1)

                    def project(u):
                        i, half = u // U1, u % U1
                        pe.wait_ge(s["o_evac"], b * U + u + 1)
                        if half == 0 and i:
                            pe.wait_ge(s["y_used"], b * NT + i)
                        for g in range(2):
                            last = pe.matmul(ps[:, 7, 0:P], oT[u % 2][:, g, :], wo[:, half * 2 + g, :],
                                             start=(half == 0 and g == 0), stop=(half == U1 - 1 and g == 1))
                        last.then_inc(s["y_done"], 1)

                    scores(0)
                    for u in range(U):
                        if u + 1 < U:
                            scores(u + 1)
                        pe.wait_ge(s["norm"], b * 2 * U + 2 * u + 2)
                        if u:
                            pe.wait_ge(s["pt_evac"], b * U + u)
                        for j in range(HALF):
                            last = pe.transpose(ps[0:KC, 4 + j // 4, (j % 4) * P:(j % 4 + 1) * P], pr[u % 2][:, j, :], k.ident[:])
                        last.then_inc(s["ptr"], 1)
                        values(u)
                        project(u)
    k.n_ln += B * LNS


def stage_cross_attention_0(k):
    d = k.dram
    cross_attention(k, "x0_", HC0, HDC0, [d["L0_xattn_W" + n] for n in "qkvo"], [d["L0_xattn_b" + n] for n in "qkv"],
                    d["L0_xattn_bo"], HDC0 ** -0.5, True, None)


def stage_cross_attention_1(k):
    d = k.dram
    cross_attention(k, "x1_", H1, HD1, [d["L1_xattn_W" + n] for n in "qkvo"], None,
                    d["L1_xattn_bo"], float(D) ** -0.5, False, d["mask_Bx1xSxS2_if1"])


def stage_experts_0(k):
    nc, d = k.nc, k.dram
    LNS = 1
    PAIRS = NE0 // 2
    GE = 40
    GROUPS = NE0 // GE
    ROWS = 3 * GE
    PER_IT = 4
    ITS = GE // 2 // PER_IT
    CH = B
    UNITS = PER_IT * CH
    LAG = 2
    RSTEPS = LN_STEPS + 14
    YB, HB, CB, TB = 0, 4, 6, 7

    with ExitStack() as ctx:
        def sb(name, shape, dt=F32):
            return k.sb(ctx, "f0_" + name, shape, dt)

        xh, xl = sb("xh", [P, B, S], F32R), sb("xl", [P, B, S], F32R)
        bh, bl = sb("bh", [P, S], F32R), sb("bl", [P, S], F32R)
        rw = sb("rw", [P, 2, P])
        rwh, rwl = sb("rwh", [P, NE0], F32R), sb("rwl", [P, NE0], F32R)
        ebias = sb("ebias", [P, NE0])
        wgs, wds = sb("wgs", [IN0, P]), sb("wds", [P, IN0])
        wgsh, wgsl = sb("wgsh", [P, IN0], F32R), sb("wgsl", [P, IN0], F32R)
        wdsT = sb("wdsT", [IN0, P])
        sel_f = sb("sel_f", [ROWS, GE // 2, 2, IN0])
        sel = sb("sel", [ROWS, GE // 2, P], BF16)
        ct = sb("ct", [ROWS, GROUPS, B * S], BF16)
        lg, prb, rep, chosen, comb, rest = (sb(n, [P, NT, NE0]) for n in ("lg", "prb", "rep", "chosen", "comb", "rest"))
        top = sb("top", [P, NT, 8])
        tot, inv = sb("tot", [P, NT]), sb("inv", [P, NT])
        parts = sb("parts", [P, NT, GROUPS, 3, GE], BF16)
        gn = [sb(f"gn{r}", [P, 2, P]) for r in range(2)]
        dn = [sb(f"dn{r}", [P, 4, IN0]) for r in range(2)]
        gh = [sb(f"gh{r}", [P, 2, P], F32R) for r in range(2)]
        gl = [sb(f"gl{r}", [P, 2, P], F32R) for r in range(2)]
        dT = [sb(f"dT{r}", [P, 2, P]) for r in range(2)]
        act_h = [sb(f"act_h{r}", [P, S]) for r in range(3)]
        hid = [sb(f"hid{r}", [P, S]) for r in range(3)]
        yT = sb("yT", [P, B, S])
        names = ("loaded consts wT w_out step zTr bh_ready bl_ready logits sig_in sig ptr ct_out sh_h sh_act "
                 "w_ina w_inb wt_done wh_out wt_out wl_out h_done c_done act_done hid_done y_units y_out y_tok")
        s = {n: k.sem("f0_" + n) for n in names.split()}
        ps = k.ps

        with nc.Block() as block:
            @block.sync
            def _(sp):
                r = d["L0_ffn_router_w"]
                sp.dma_start(rw[:, 0, :], r[0:P, :]).then_inc(s["loaded"], 16)
                sp.dma_start(rw[0:NE0 - P, 1, :], r[P:NE0, :]).then_inc(s["loaded"], 16)
                sp.dma_start(ebias[:], d["L0_ffn_expert_bias"].partition_broadcast(P)).then_inc(s["loaded"], 16)
                sp.dma_start(wgs[:], d["L0_ffn_w_gate_shared"]).then_inc(s["loaded"], 16)
                sp.dma_start(wds[:], d["L0_ffn_w_down_shared"]).then_inc(s["loaded"], 16)
                sp.wait_ge(s["loaded"], 16 * 5)

            @block.gpsimd
            def _(pool):
                pool.memset(sel_f[:].rearrange("p j h c -> p (j h c)"), 0.0).then_inc(s["consts"], 1)
                for part in range(3):
                    pool.wait_ge(s["consts"], part + 1)
                    pool.affine_select(out=sel_f[:].rearrange("p j h c -> p (j h) c"), in_=sel_f[:].rearrange("p j h c -> p (j h) c"),
                                       compare_op=ALU.not_equal, fill=1.0, base=-part * GE, pattern=[[-1, GE], [0, IN0]],
                                       channel_multiplier=1).then_inc(s["consts"], 1)
                pool.wait_ge(s["consts"], 4)
                pool.tensor_copy(sel[:].rearrange("p j c -> p (j c)"), sel_f[:].rearrange("p j h c -> p (j h c)"))

            @block.tensor
            def _(pe):
                pe.wait_ge(s["loaded"], 16 * 5)
                pe.transpose(ps[:, 0, 0:P], rw[:, 0, :], k.ident[:])
                pe.transpose(ps[:, 0, P:NE0], rw[0:NE0 - P, 1, :], k.ident[0:NE0 - P, 0:NE0 - P])
                pe.transpose(ps[:, 0, NE0:NE0 + IN0], wgs[:], k.ident[0:IN0, 0:IN0])
                pe.transpose(ps[0:IN0, 0, 256:256 + P], wds[:], k.ident[:]).then_inc(s["wT"], 1)

            @block.scalar
            def _(act):
                act.wait_ge(s["wT"], 1)
                act.activation(rwh[:], ps[:, 0, 0:NE0], ACT.Copy)
                act.activation(wgsh[:], ps[:, 0, NE0:NE0 + IN0], ACT.Copy)
                act.activation(wdsT[:], ps[0:IN0, 0, 256:256 + P], ACT.Copy).then_inc(s["w_out"], 1)

            @block.vector
            def _(v):
                v.wait_ge(s["w_out"], 1)
                v.tensor_tensor(rwl[:], ps[:, 0, 0:NE0], rwh[:].bitcast(F32), ALU.subtract)
                v.tensor_tensor(wgsl[:], ps[:, 0, NE0:NE0 + IN0], wgsh[:].bitcast(F32), ALU.subtract)

        with nc.Block() as block:
            @block.gpsimd
            def _(pool):
                with pool.Fori(0, B) as b:
                    layernorm_pool(k, pool, 0, b, LNS)

            @block.vector
            def _(v):
                with v.Fori(0, B) as b:
                    step = chain(v, s["step"], RSTEPS, b)
                    layernorm_vector(k, v, step, lambda t: k.x[:, b * NT + t, :], 0, b, LNS)
                    v.wait_ge(s["bh_ready"], b + 1)
                    v.tensor_tensor(bl[:], k.bank(TB), bh[:].bitcast(F32), ALU.subtract).then_inc(s["bl_ready"], 1)
                    v.tensor_copy(xh[:, b, :], bh[:].bitcast(F32))
                    v.wait_ge(s["bl_ready"], b + 1)
                    v.tensor_copy(xl[:, b, :], bl[:].bitcast(F32))
                    for t in range(NT):
                        v.wait_ge(s["logits"], b * NT + t + 1)
                        last = v.tensor_tensor(lg[:, t, :], ps[:, t, 0:NE0], ebias[:], ALU.add)
                    last.then_inc(s["sig_in"], 1)
                    v.wait_ge(s["sig_in"], b + 1)
                    k.settle(v)
                    for t in range(NT):
                        last = v.max(top[:, t, :], lg[:, t, :])
                    step(last, k)
                    for t in range(NT):
                        last = v.match_replace(rep[:, t, :], top[:, t, :], lg[:, t, :], -3.0e38)
                    step(last)
                    step(v.tensor_tensor(chosen[:], rep[:], lg[:], ALU.not_equal))
                    v.wait_ge(s["sig"], b + 1)
                    step(v.tensor_tensor(comb[:], chosen[:], prb[:], ALU.mult))
                    step(v.tensor_reduce(tot[:], comb[:], AX, ALU.add))
                    step(v.tensor_scalar(tot[:], tot[:], 1e-9, None, ALU.add))
                    step(v.reciprocal(inv[:], tot[:]))
                    step(v.tensor_scalar(inv[:], inv[:], 2.5, None, ALU.mult))
                    step(v.tensor_tensor(comb[:], comb[:], inv[:].unsqueeze(2).to_broadcast([P, NT, NE0]), ALU.mult))
                    src = comb
                    for part in range(3):
                        dst = parts[:, :, :, part, :]
                        step(v.tensor_copy(dst, src[:].rearrange("p t (g e) -> p t g e", e=GE)))
                        if part < 2:
                            for t in range(NT):
                                last = v.tensor_tensor(rest[:, t, :].rearrange("p (g e) -> p g e", e=GE),
                                                       src[:, t, :].rearrange("p (g e) -> p g e", e=GE),
                                                       parts[:, t, :, part, :], ALU.subtract)
                            step(last)
                        src = rest
                    assert step.count[0] == RSTEPS, step.count[0]

            @block.scalar
            def _(act):
                with act.Fori(0, B) as b:
                    act.wait_ge(s["zTr"], b + 1)
                    act.activation(bh[:], k.bank(TB), ACT.Copy).then_inc(s["bh_ready"], 1)
                    act.wait_ge(s["sig_in"], b + 1)
                    act.activation(prb[:], lg[:], ACT.Sigmoid).then_inc(s["sig"], 1)
                    act.wait_ge(s["ptr"], b + 1)
                    for t in range(NT):
                        last = act.activation(ct[:, :, bass.ds(b * S + t * P, P)],
                                              ps[0:ROWS, HB, :].bitcast(BF16).rearrange("p (t g n) -> p t g n", t=2, n=P)[:, t, :, :]
                                              if t < 2 else
                                              ps[0:ROWS, HB + 1, :].bitcast(BF16).rearrange("p (t g n) -> p t g n", t=2, n=P)[:, t - 2, :, :],
                                              ACT.Copy)
                    last.then_inc(s["ct_out"], 1)

            @block.tensor
            def _(pe):
                with pe.Fori(0, B) as b:
                    pe.wait_ge(s["step"], b * RSTEPS + LN_STEPS)
                    for t in range(NT):
                        last = pe.transpose(ps[:, TB, t * P:(t + 1) * P], k.z[:, t, :], k.ident[:])
                    last.then_inc(s["zTr"], 1)
                    pe.wait_ge(s["bl_ready"], b + 1)
                    for t in range(NT):
                        tok = slice(t * P, (t + 1) * P)
                        split_product(pe, ps[:, t, 0:NE0], (bh[:, tok], bl[:, tok]), (rwh[:], rwl[:])).then_inc(s["logits"], 1)
                    pe.wait_ge(s["step"], b * RSTEPS + RSTEPS)
                    pe.wait_ge(s["ct_out"], b)
                    for t in range(NT):
                        out = ps[0:ROWS, HB + t // 2, :].bitcast(BF16).rearrange("p (t g n) -> p t g n", t=2, n=P)
                        for g in range(GROUPS):
                            last = pe.transpose(out[:, t % 2, g, :], parts[:, t, g, :, :].rearrange("p a e -> p (a e)"), k.ident_bf[:])
                    last.then_inc(s["ptr"], 1)

        with nc.Block() as block:
            @block.tensor
            def _(pe):
                for c in range(CH):
                    if c >= 2:
                        pe.wait_ge(s["sh_act"], c - 1)
                    split_product(pe, ps[0:IN0, HB + c % 2, :], (wgsh[:], wgsl[:]), (xh[:, c, :], xl[:, c, :])).then_inc(s["sh_h"], 1)
                for c in range(CH):
                    pe.wait_ge(s["sh_act"], c + 1)
                    pe.matmul(k.bank(YB + c), wdsT[:], yT[0:IN0, c, :], start=True, stop=False, skip_group_check=True)

            @block.scalar
            def _(act):
                for c in range(CH):
                    act.wait_ge(s["sh_h"], c + 1)
                    act.activation(yT[0:IN0, c, :], ps[0:IN0, HB + c % 2, :], ACT.Silu).then_inc(s["sh_act"], 1)

        gate = d["L0_ffn_w_gate"].rearrange("(n q e) i h -> n (e i) q h", q=2, e=2)
        down = d["L0_ffn_w_down"].rearrange("(n e) h i -> n h e i", e=4)

        with nc.Block() as block:
            @block.sync
            def _(sp):
                with sp.Fori(0, GROUPS) as g:
                    with sp.Fori(0, ITS) as it:
                        n = g * ITS + it
                        for half in range(2):
                            sp.wait_ge(s["wt_done"], n * 2 + half - 1 if half else n * 2)
                            sp.dma_start(gn[half][:], gate[n * 2 + half]).then_inc(s["w_in" + "ab"[half]], 16)
                            sp.dma_start(dn[half][:], down[n * 2 + half]).then_inc(s["w_in" + "ab"[half]], 16)

            @block.tensor
            def _(pe):
                with pe.Fori(0, GROUPS) as g:
                    with pe.Fori(0, ITS) as it:
                        n = g * ITS + it

                        def prepare(half):
                            pe.wait_ge(s["w_in" + "ab"[half]], (n + 1) * 32)
                            pe.wait_ge(s["wt_out"], n * 2 + half)
                            pe.wait_ge(s["wl_out"], n * 2 + half)
                            for q in range(2):
                                pe.transpose(ps[:, TB, q * P:(q + 1) * P], gn[half][:, q, :], k.ident[:])
                            for q in range(2):
                                last = pe.transpose(ps[:, TB, (2 + q) * P:(3 + q) * P],
                                                    dn[half][:, 2 * q:2 * q + 2, :].rearrange("p e i -> p (e i)"), k.ident[:])
                            last.then_inc(s["wt_done"], 1)

                        def hidden(w):
                            q, c = w // CH, w % CH
                            half = q // 2
                            if q % 2 == 0 and c == 0:
                                pe.wait_ge(s["wt_out"], n * 2 + half + 1)
                                pe.wait_ge(s["wl_out"], n * 2 + half + 1)
                            if w >= 2:
                                pe.wait_ge(s["act_done"], n * UNITS + w - 1)
                            split_product(pe, k.bank(HB + w % 2), (gh[half][:, q % 2, :], gl[half][:, q % 2, :]),
                                          (xh[:, c, :], xl[:, c, :])).then_inc(s["h_done"], 1)
                            if w:
                                pe.wait_ge(s["hid_done"], n * UNITS + w)
                            pe.matmul(k.bank(CB), sel[:, it * PER_IT + q, :], ct[:, g, c * S:(c + 1) * S], start=True,
                                      stop=True).then_inc(s["c_done"], 1)

                        def output(w):
                            q, c = w // CH, w % CH
                            pe.wait_ge(s["hid_done"], n * UNITS + w + 1)
                            pe.matmul(k.bank(YB + c), dT[q // 2][:, q % 2, :], hid[w % 3][:], start=False, stop=False,
                                      skip_group_check=True).then_inc(s["y_units"], 1)

                        prepare(0)
                        prepare(1)
                        for w in range(UNITS + LAG):
                            if w < UNITS:
                                hidden(w)
                            if w >= LAG:
                                output(w - LAG)

            @block.scalar
            def _(act):
                with act.Fori(0, GROUPS) as g:
                    with act.Fori(0, ITS) as it:
                        n = g * ITS + it
                        for half in range(2):
                            act.wait_ge(s["wt_done"], n * 2 + half + 1)
                            act.activation(gh[half][:].rearrange("p q n -> p (q n)"), ps[:, TB, 0:2 * P], ACT.Copy).then_inc(s["wh_out"], 1)
                            act.activation(dT[half][:].rearrange("p q n -> p (q n)"), ps[:, TB, 2 * P:4 * P], ACT.Copy).then_inc(s["wt_out"], 1)
                        for w in range(UNITS):
                            act.wait_ge(s["h_done"], n * UNITS + w + 1)
                            if w >= 3:
                                act.wait_ge(s["hid_done"], n * UNITS + w - 2)
                            act.activation(act_h[w % 3][:], k.bank(HB + w % 2), ACT.Silu).then_inc(s["act_done"], 1)

            @block.vector
            def _(v):
                with v.Fori(0, GROUPS) as g:
                    with v.Fori(0, ITS) as it:
                        n = g * ITS + it
                        for half in range(2):
                            v.wait_ge(s["wh_out"], n * 2 + half + 1)
                            v.wait_ge(s["wt_out"], n * 2 + half + 1)
                            v.tensor_tensor(gl[half][:].rearrange("p q n -> p (q n)"), ps[:, TB, 0:2 * P],
                                            gh[half][:].rearrange("p q n -> p (q n)").bitcast(F32), ALU.subtract).then_inc(s["wl_out"], 1)
                        for w in range(UNITS):
                            v.wait_ge(s["act_done"], n * UNITS + w + 1)
                            v.wait_ge(s["c_done"], n * UNITS + w + 1)
                            if w >= 3:
                                v.wait_ge(s["y_units"], n * UNITS + w - 2)
                            v.tensor_tensor(hid[w % 3][:], act_h[w % 3][:], k.bank(CB), ALU.mult).then_inc(s["hid_done"], 1)

        residual_block(k, s, yT, YB)
    k.n_ln += B * LNS


def residual_block(k, s, yT, YB):
    nc, ps = k.nc, k.ps
    with nc.Block() as block:
        @block.scalar
        def _(act):
            for c in range(B):
                act.activation(yT[:, c, :], k.bank(YB + c), ACT.Copy).then_inc(s["y_out"], 1)

        @block.tensor
        def _(pe):
            for c in range(B):
                pe.wait_ge(s["y_out"], c + 1)
                for t in range(NT):
                    last = pe.transpose(ps[:, YB + 4 + c, t * P:(t + 1) * P], yT[:, c, t * P:(t + 1) * P], k.ident[:])
                last.then_inc(s["y_tok"], 1)

        @block.vector
        def _(v):
            for c in range(B):
                v.wait_ge(s["y_tok"], c + 1)
                v.tensor_tensor(k.x[:, c * NT:(c + 1) * NT, :], k.x[:, c * NT:(c + 1) * NT, :],
                                k.bank(YB + 4 + c).rearrange("p (t n) -> p t n", n=P), ALU.add)


def stage_attention_1(k):
    nc, d = k.nc, k.dram
    LNS = 1
    STEPS = LN_STEPS
    G = H1 // 4
    AHEAD = 2
    OFF = [0, 4 * P, 7 * P, 9 * P, 10 * P]
    EVAC = [(OFF[0], OFF[1]), (OFF[1], OFF[2]), (OFF[2], OFF[4])]
    SB, PB, OB, TB = 0, 4, 6, 7

    with ExitStack() as ctx:
        def sb(name, shape, dt=F32):
            return k.sb(ctx, "a1_" + name, shape, dt)

        wqkv = sb("wqkv", [P, 3 * P])
        wstack = [sb(f"wstack{n}", [P, G, 4, 4, HD1]) for n in "qk"]
        wo_nat = sb("wo_nat", [HD1, H1, P])
        wo = sb("wo", [P, G, P])
        brow = sb("brow", [P, P])
        row = sb("row", [P, 1], I32)
        sel_i = [sb(f"sel_i{n}", [P, 1], I32) for n in range(2)]
        sel = [sb(f"sel{n}", [P, 1]) for n in range(2)]
        mask = sb("mask", [P, S])
        zT = sb("zT", [P, S])
        vpad = sb("vpad", [P, NT, H1, 32])
        qhi, khi = sb("qhi", [P, S], F32R), sb("khi", [P, S], F32R)
        qz = [[sb(f"qz{r}{j}", [P, S], F32R) for j in range(4)] for r in range(2)]
        ks = [sb(f"ks{r}", [P, S], F32R) for r in range(2)]
        sc = [sb(f"sc{r}", [P, S]) for r in range(4)]
        nmax = sb("nmax", [P, 3, NT])
        sums = sb("sums", [P, 3, NT])
        rsum = sb("rsum", [P, 3, NT])
        prob = sb("prob", [P, 3, NT, S])
        pt = [[sb(f"pt{r}{j}", [P, OFF[4]]) for j in range(4)] for r in range(2)]
        oT = sb("oT", [P, G, S])
        names = ("loaded consts sel wo_zero step zTr zT_out q_done k_done qhi_ready khi_ready qk_ready v_done "
                 "v_out score tile_scored exp_done rs_ready prob_ready ptr pt_a pt_v pv o_out y_done y_used batch_done")
        s = {n: k.sem("a1_" + n) for n in names.split()}
        ps = k.ps

        def keys(i):
            return (i + 1) * P

        with nc.Block() as block:
            @block.sync
            def _(sp):
                sp.dma_start(wqkv[:], d["L1_attn_w_qkv"]).then_inc(s["loaded"], 16)
                sp.dma_start(brow[:], d["L1_attn_b_out"].partition_broadcast(P)).then_inc(s["loaded"], 16)
                sp.wait_ge(s["wo_zero"], 1)
                wo_d = d["L1_attn_w_out"].rearrange("(g j e) n -> j e g n", j=4, e=HD1)
                for j in range(4):
                    sp.dma_start(wo[32 * j:32 * j + HD1, :, :], wo_d[j]).then_inc(s["loaded"], 16)
                sp.wait_ge(s["loaded"], 16 * 6)

            @block.gpsimd
            def _(pool):
                pool.memset(vpad[:].rearrange("p t h e -> p (t h e)"), 0.0)
                pool.memset(wo[:], 0.0).then_inc(s["wo_zero"], 1)
                for r in range(2):
                    for j in range(4):
                        pool.memset(qz[r][j][:].bitcast(F32), 0.0)
                pool.iota(row[:], [[0, 1]], base=0, channel_multiplier=1).then_inc(s["consts"], 1)
                pool.memset(mask[:], 0.0).then_inc(s["consts"], 1)
                pool.wait_ge(s["consts"], 2)
                pool.affine_select(out=mask[:], in_=mask[:], compare_op=ALU.is_ge, fill=-1.0e10, base=S - P,
                                   pattern=[[-1, S]], channel_multiplier=1)

            @block.vector
            def _(v):
                v.wait_ge(s["consts"], 1)
                for n, shift in enumerate((3, 4)):
                    v.tensor_scalar(sel_i[n][:], row[:], shift, 1, ALU.logical_shift_right, ALU.bitwise_and).then_inc(s["sel"], 1)
                v.wait_ge(s["sel"], 2)
                for n in range(2):
                    v.tensor_scalar(sel[n][:], sel_i[n][:], -1.0, None, ALU.mult)
                v.wait_ge(s["loaded"], 16 * 6)
                for n, scale in ((0, HD1 ** -0.5), (1, 1.0)):
                    src = wqkv[:, n * P:(n + 1) * P].rearrange("p (h e) -> p h e", e=HD1)
                    dst = wstack[n][:].rearrange("p g j c e -> p (g j) c e")
                    for c in range(4):
                        v.tensor_scalar(dst[:, :, c, :], src, scale, None, ALU.mult)

        with nc.Block() as block:
            @block.vector
            def _(v):
                with v.Fori(0, B) as b:
                    step = chain(v, s["step"], STEPS, b)
                    layernorm_vector(k, v, step, lambda t: k.x[:, b * NT + t, :], 0, b, LNS)

                    def prepare(g):
                        r, n = g % 2, b * G + g + 1
                        v.wait_ge(s["qhi_ready"], n)
                        for j in range(4):
                            rows = slice(32 * j, 32 * j + 32)
                            last = v.scalar_tensor_tensor(qz[r][j][rows, :], qhi[rows, :].bitcast(F32), sel[0][rows, 0:1],
                                                          ps[rows, TB, :], ALU.mult, ALU.add)
                        last.then_inc(s["qk_ready"], 1)
                        v.wait_ge(s["khi_ready"], n)
                        v.scalar_tensor_tensor(ks[r][:], khi[:].bitcast(F32), sel[1][:, 0:1], ps[:, TB, :], ALU.mult,
                                               ALU.add).then_inc(s["qk_ready"], 1)

                    def scores(h):
                        for i in range(NT):
                            u = h * NT + i
                            v.wait_ge(s["score"], b * H1 * NT + u + 1)
                            if u >= 4:
                                v.wait_ge(s["exp_done"], b * H1 * NT + u - 3)
                            k.settle(v)
                            v.tensor_tensor_reduce(sc[u % 4][:, 0:keys(i)], ps[:, SB + u % 4, 0:keys(i)],
                                                   mask[:, S - P - i * P:S], -1.0, 3.0e38, ALU.add, ALU.min,
                                                   nmax[:, h % 3, i:i + 1]).then_inc(s["tile_scored"], 1)

                    def invert(h):
                        v.wait_ge(s["exp_done"], b * H1 * NT + h * NT + NT)
                        v.reciprocal(rsum[:, h % 3, :], sums[:, h % 3, :]).then_inc(s["rs_ready"], 1)

                    def evacuate(h):
                        r, j = h // 4 % 2, h % 4
                        v.wait_ge(s["ptr"], b * H1 * 3 + 3 * h + 3)
                        if h >= 8:
                            v.wait_ge(s["pv"], b * G + h // 4 - 1)
                        lo, hi = EVAC[2]
                        v.tensor_copy(pt[r][j][:, lo:hi], ps[:, PB + (3 * h + 2) % 2, 0:hi - lo]).then_inc(s["pt_v"], 1)

                    prepare(0)
                    for h in range(AHEAD):
                        scores(h)
                    invert(0)
                    for h in range(H1):
                        if h % 4 == 0 and h // 4 + 1 < G:
                            prepare(h // 4 + 1)
                        if h + AHEAD < H1:
                            scores(h + AHEAD)
                        if h + 1 < H1:
                            invert(h + 1)
                        evacuate(h)
                    for t in range(NT):
                        v.wait_ge(s["y_done"], b * NT + t + 1)
                        v.tensor_tensor(k.x[:, b * NT + t, :], k.x[:, b * NT + t, :], ps[:, TB, t * P:(t + 1) * P],
                                        ALU.add).then_inc(s["y_used"], 1)
                    v.wait_ge(s["y_used"], b * NT + NT)
                    v.tensor_tensor(k.x[:, bass.ds(b * NT, NT), :], k.x[:, bass.ds(b * NT, NT), :],
                                    brow[:].unsqueeze(1).to_broadcast([P, NT, P]), ALU.add).then_inc(s["batch_done"], 1)
                    v.wait_ge(s["batch_done"], b + 1)
                    assert step.count[0] == STEPS

            @block.gpsimd
            def _(pool):
                with pool.Fori(0, B) as b:
                    layernorm_pool(k, pool, 0, b, LNS)
                    for h in range(H1):
                        pool.wait_ge(s["rs_ready"], b * H1 + h + 1)
                        k.settle(pool)
                        for i in range(NT):
                            last = pool.tensor_scalar(prob[:, h % 3, i, 0:keys(i)], prob[:, h % 3, i, 0:keys(i)],
                                                      rsum[:, h % 3, i:i + 1], 0.0, ALU.mult, ALU.add)
                        last.then_inc(s["prob_ready"], 1)

            @block.scalar
            def _(act):
                with act.Fori(0, B) as b:
                    act.wait_ge(s["zTr"], b + 1)
                    act.activation(zT[:], k.bank(OB), ACT.Copy).then_inc(s["zT_out"], 1)

                    def prepare(g):
                        n = b * G + g + 1
                        act.wait_ge(s["q_done"], n)
                        act.activation(qhi[:], ps[:, TB, :], ACT.Copy).then_inc(s["qhi_ready"], 1)
                        act.wait_ge(s["k_done"], n)
                        act.activation(khi[:], ps[:, TB, :], ACT.Copy).then_inc(s["khi_ready"], 1)

                    def exps(h):
                        for i in range(NT):
                            u = h * NT + i
                            act.wait_ge(s["tile_scored"], b * H1 * NT + u + 1)
                            if i == 0 and h >= 3:
                                act.wait_ge(s["ptr"], b * H1 * 3 + 3 * (h - 2))
                            act.activation(prob[:, h % 3, i, 0:keys(i)], sc[u % 4][:, 0:keys(i)], ACT.Exp, scale=-1.0,
                                           bias=nmax[:, h % 3, i:i + 1], accum_out=sums[:, h % 3, i:i + 1]).then_inc(s["exp_done"], 1)

                    def evacuate(h):
                        r, j = h // 4 % 2, h % 4
                        for n in range(2):
                            act.wait_ge(s["ptr"], b * H1 * 3 + 3 * h + n + 1)
                            if h >= 8 and n == 0:
                                act.wait_ge(s["pv"], b * G + h // 4 - 1)
                            lo, hi = EVAC[n]
                            act.activation(pt[r][j][:, lo:hi], ps[:, PB + (3 * h + n) % 2, 0:hi - lo], ACT.Copy).then_inc(s["pt_a"], 1)

                    def output(g):
                        act.wait_ge(s["pv"], b * G + g + 1)
                        act.activation(oT[:, g, :], k.bank(OB), ACT.Copy).then_inc(s["o_out"], 1)

                    act.wait_ge(s["v_done"], b + 1)
                    act.activation(vpad[:, :, :, 0:HD1],
                                   k.bank(PB).rearrange("p (t h e) -> p t h e", h=H1, e=HD1), ACT.Copy).then_inc(s["v_out"], 1)
                    prepare(0)
                    for h in range(AHEAD):
                        exps(h)
                    for h in range(H1):
                        if h % 4 == 0 and h // 4 + 1 < G:
                            prepare(h // 4 + 1)
                        if h + AHEAD < H1:
                            exps(h + AHEAD)
                        if h % 4 == 0 and h:
                            output(h // 4 - 1)
                        evacuate(h)
                    output(G - 1)

            @block.tensor
            def _(pe):
                with pe.Fori(0, B) as b:
                    pe.wait_ge(s["step"], b * STEPS + LN_STEPS)
                    for t in range(NT):
                        last = pe.transpose(ps[:, OB, t * P:(t + 1) * P], k.z[:, t, :], k.ident[:])
                    last.then_inc(s["zTr"], 1)
                    pe.wait_ge(s["zT_out"], b + 1)
                    for t in range(NT):
                        last = pe.matmul(ps[:, PB, t * P:(t + 1) * P], zT[:, t * P:(t + 1) * P], wqkv[:, 2 * P:3 * P],
                                         start=True, stop=True)
                    last.then_inc(s["v_done"], 1)

                    def prepare(g):
                        if g:
                            pe.wait_ge(s["qk_ready"], b * 2 * G + 2 * g)
                        for n, done in ((0, "q_done"), (1, "k_done")):
                            if n:
                                pe.wait_ge(s["qk_ready"], b * 2 * G + 2 * g + 1)
                            pe.matmul(ps[:, TB, :], wstack[n][:, g, :, :, :].rearrange("p j c e -> p (j c e)"), zT[:],
                                      start=True, stop=True).then_inc(s[done], 1)

                    def scores(h):
                        r, j = h // 4 % 2, h % 4
                        if j == 0:
                            pe.wait_ge(s["qk_ready"], b * 2 * G + 2 * (h // 4) + 2)
                        for i in range(NT):
                            u = h * NT + i
                            if u >= 4:
                                pe.wait_ge(s["tile_scored"], b * H1 * NT + u - 3)
                            pe.matmul(ps[:, SB + u % 4, 0:keys(i)], qz[r][j][:, i * P:(i + 1) * P], ks[r][:, 0:keys(i)],
                                      start=True, stop=True).then_inc(s["score"], 1)

                    def transpose_probs(h):
                        for n in range(3):
                            if n == 0 and h:
                                pe.wait_ge(s["pt_a"], b * 2 * H1 + 2 * h)
                            elif n == 1 and h:
                                pe.wait_ge(s["pt_v"], b * H1 + h)
                            elif n == 2:
                                pe.wait_ge(s["pt_a"], b * 2 * H1 + 2 * h + 1)
                            if n == 0:
                                pe.wait_ge(s["prob_ready"], b * H1 + h + 1)
                            at = 0
                            for kt in ((0,), (1,), (2, 3))[n]:
                                for i in range(kt, NT):
                                    last = pe.transpose(ps[:, PB + (3 * h + n) % 2, at:at + P],
                                                        prob[:, h % 3, i, kt * P:(kt + 1) * P], k.ident[:])
                                    at += P
                            last.then_inc(s["ptr"], 1)

                    def values(g):
                        r = g % 2
                        if g:
                            pe.wait_ge(s["o_out"], b * G + g)
                        pe.wait_ge(s["pt_a"], b * 2 * H1 + 2 * (4 * g + 4))
                        pe.wait_ge(s["pt_v"], b * H1 + 4 * g + 4)
                        for kt in range(NT):
                            for j in range(4):
                                last = pe.matmul(ps[32 * j:32 * j + 32, OB, kt * P:S], vpad[:, kt, 4 * g + j, :],
                                                 pt[r][j][:, OFF[kt]:OFF[kt + 1]], start=(kt == 0), stop=(kt == NT - 1))
                        last.then_inc(s["pv"], 1)

                    prepare(0)
                    for h in range(AHEAD):
                        scores(h)
                    pe.wait_ge(s["v_out"], b + 1)
                    for h in range(H1):
                        if h % 4 == 0 and h // 4 + 1 < G:
                            prepare(h // 4 + 1)
                        if h + AHEAD < H1:
                            scores(h + AHEAD)
                        if h % 4 == 0 and h:
                            values(h // 4 - 1)
                        transpose_probs(h)
                    values(G - 1)
                    pe.wait_ge(s["o_out"], b * G + G)
                    for t in range(NT):
                        if t:
                            pe.wait_ge(s["y_used"], b * NT + t)
                        for g in range(G):
                            last = pe.matmul(ps[:, TB, t * P:(t + 1) * P], oT[:, g, t * P:(t + 1) * P], wo[:, g, :],
                                             start=(g == 0), stop=(g == G - 1))
                        last.then_inc(s["y_done"], 1)
    k.n_ln += B * LNS


def stage_experts_1(k):
    nc, d = k.nc, k.dram
    LNS = 1
    ROWS = 3 * NE1
    FB = FF1 // P
    EXPERTS = 2
    ITS = NE1 // EXPERTS
    CH = B
    E_UNITS = CH * FB
    UNITS = EXPERTS * E_UNITS
    CHUNKS = EXPERTS * CH
    MID = 4
    LAG = 2
    RSTEPS = LN_STEPS + 22
    YB, GB, VB, CB, TB = 0, 4, 5, 6, 7
    ALPHA, LIMIT = 1.702, 9.0

    with ExitStack() as ctx:
        def sb(name, shape, dt=F32):
            return k.sb(ctx, "f1_" + name, shape, dt)

        xh, xl = sb("xh", [P, B, S], F32R), sb("xl", [P, B, S], F32R)
        bh, bl = sb("bh", [P, S], F32R), sb("bl", [P, S], F32R)
        gw = sb("gw", [P, NE1])
        gwh, gwl = sb("gwh", [P, NE1], F32R), sb("gwl", [P, NE1], F32R)
        b1n = sb("b1n", [NE1 * FB, 2 * P])
        b1 = sb("b1", [P, 2, NE1 * FB])
        b2 = sb("b2", [NE1, P])
        order = sb("order", [P, NE1])
        sel_f = sb("sel_f", [ROWS, NE1, P])
        sel = sb("sel", [ROWS, NE1, P], BF16)
        ct = sb("ct", [ROWS, B * S], BF16)
        ct32 = sb("ct32", [NE1, B * S])
        g1, g2, eq, m1, m2, comb, rest = (sb(n, [P, NT, NE1]) for n in ("g1", "g2", "eq", "mask1", "mask2", "comb", "rest"))
        top1, top2, best, ex, den, inv, second = (sb(n, [P, NT]) for n in ("top1", "top2", "best", "ex", "den", "inv", "second"))
        parts = sb("parts", [P, NT, 3, NE1], BF16)
        wn = [sb(f"wn{r}", [P, FB, 2, P]) for r in range(2)]
        dn = [sb(f"dn{r}", [P, FB, P]) for r in range(2)]
        wh = [sb(f"wh{r}", [P, FB, 2, P], F32R) for r in range(2)]
        wl = [sb(f"wl{r}", [P, FB, 2, P], F32R) for r in range(2)]
        dT = [sb(f"dT{r}", [P, FB, P]) for r in range(2)]
        gate, val, sg, hid, hidw = ([sb(f"{n}{r}", [P, S]) for r in range(3)] for n in ("gate", "val", "sg", "hid", "hidw"))
        ce = [sb(f"ce{r}", [P, S]) for r in range(2)]
        yT = sb("yT", [P, B, S])
        names = ("loaded consts b1T w_out step zTr bh_ready bl_ready logits exp_in exp_out ptr ct_out w_in wt_done dt_done "
                 "wh_out wl_out dt_out g_done v_done c_done g_out v_out c_out sig_out t_done clipped h_done hid_done "
                 "y_units y_out y_tok")
        s = {n: k.sem("f1_" + n) for n in names.split()}
        ps = k.ps

        with nc.Block() as block:
            @block.sync
            def _(sp):
                sp.dma_start(gw[:], d["L1_ffn_gate_w"]).then_inc(s["loaded"], 16)
                sp.dma_start(b1n[:], d["L1_ffn_dense_1_b"].rearrange("e (a n) -> (e a) n", a=FB)).then_inc(s["loaded"], 16)
                sp.dma_start(b2[:], d["L1_ffn_dense_2_b"]).then_inc(s["loaded"], 16)
                sp.wait_ge(s["loaded"], 16 * 3)

            @block.gpsimd
            def _(pool):
                for e in range(NE1):
                    pool.memset(order[:, e:e + 1], float(NE1 - e))
                pool.memset(sel_f[:].rearrange("p e c -> p (e c)"), 0.0).then_inc(s["consts"], 1)
                for part in range(3):
                    pool.wait_ge(s["consts"], part + 1)
                    pool.affine_select(out=sel_f[:], in_=sel_f[:], compare_op=ALU.not_equal, fill=1.0, base=-part * NE1,
                                       pattern=[[-1, NE1], [0, P]], channel_multiplier=1).then_inc(s["consts"], 1)
                pool.wait_ge(s["consts"], 4)
                pool.tensor_copy(sel[:].rearrange("p e c -> p (e c)"), sel_f[:].rearrange("p e c -> p (e c)"))

            @block.tensor
            def _(pe):
                pe.wait_ge(s["loaded"], 16 * 3)
                for gv in range(2):
                    last = pe.transpose(ps[:, 0, gv * NE1 * FB:(gv + 1) * NE1 * FB],
                                        b1n[:].rearrange("e (p g) -> e g p", g=2)[:, gv, :], k.ident[0:NE1 * FB, 0:NE1 * FB])
                last.then_inc(s["b1T"], 1)

            @block.vector
            def _(v):
                v.wait_ge(s["loaded"], 16 * 3)
                v.tensor_copy(gwh[:], gw[:]).then_inc(s["w_out"], 1)
                v.wait_ge(s["w_out"], 1)
                v.tensor_tensor(gwl[:], gw[:], gwh[:].bitcast(F32), ALU.subtract)
                v.wait_ge(s["b1T"], 1)
                v.tensor_copy(b1[:].rearrange("p g n -> p (g n)"), ps[:, 0, 0:2 * NE1 * FB])

        with nc.Block() as block:
            @block.gpsimd
            def _(pool):
                with pool.Fori(0, B) as b:
                    layernorm_pool(k, pool, 0, b, LNS)

            @block.vector
            def _(v):
                with v.Fori(0, B) as b:
                    step = chain(v, s["step"], RSTEPS, b)
                    layernorm_vector(k, v, step, lambda t: k.x[:, b * NT + t, :], 0, b, LNS)
                    v.wait_ge(s["bh_ready"], b + 1)
                    v.tensor_tensor(bl[:], k.bank(TB), bh[:].bitcast(F32), ALU.subtract).then_inc(s["bl_ready"], 1)
                    v.tensor_copy(xh[:, b, :], bh[:].bitcast(F32))
                    v.wait_ge(s["bl_ready"], b + 1)
                    v.tensor_copy(xl[:, b, :], bl[:].bitcast(F32))

                    def wide(a):
                        return a[:].unsqueeze(2).to_broadcast([P, NT, NE1])

                    def best_of(gates, top, mask):
                        step(v.tensor_reduce(top[:], gates[:], AX, ALU.max))
                        step(v.tensor_tensor(eq[:], gates[:], wide(top), ALU.is_equal))
                        step(v.tensor_tensor(eq[:], eq[:], order[:].unsqueeze(1).to_broadcast([P, NT, NE1]), ALU.mult))
                        step(v.tensor_reduce(best[:], eq[:], AX, ALU.max))
                        step(v.tensor_tensor(mask[:], eq[:], wide(best), ALU.is_equal))

                    v.wait_ge(s["logits"], b + 1)
                    step(v.tensor_copy(g1[:], ps[:, 0:NT, 0:NE1]))
                    best_of(g1, top1, m1)
                    step(v.scalar_tensor_tensor(g2[:], m1[:], NEG, g1[:], ALU.mult, ALU.add))
                    best_of(g2, top2, m2)
                    v.tensor_tensor(ex[:], top2[:], top1[:], ALU.subtract).then_inc(s["exp_in"], 1)
                    v.wait_ge(s["exp_out"], b + 1)
                    step(v.tensor_scalar(inv[:], ex[:], 1.0, None, ALU.add))
                    step(v.reciprocal(den[:], inv[:]))
                    v.tensor_tensor(m1[:], m1[:], wide(den), ALU.mult)
                    step(v.tensor_tensor(second[:], ex[:], den[:], ALU.mult))
                    step(v.tensor_tensor(m2[:], m2[:], wide(second), ALU.mult))
                    step(v.tensor_tensor(comb[:], m1[:], m2[:], ALU.add))
                    step(v.tensor_copy(parts[:, :, 0, :], comb[:]))
                    step(v.tensor_tensor(rest[:], comb[:], parts[:, :, 0, :], ALU.subtract))
                    step(v.tensor_copy(parts[:, :, 1, :], rest[:]))
                    step(v.tensor_tensor(rest[:], rest[:], parts[:, :, 1, :], ALU.subtract))
                    step(v.tensor_copy(parts[:, :, 2, :], rest[:]))
                    assert step.count[0] == RSTEPS, step.count[0]

            @block.scalar
            def _(act):
                with act.Fori(0, B) as b:
                    act.wait_ge(s["zTr"], b + 1)
                    act.activation(bh[:], k.bank(TB), ACT.Copy).then_inc(s["bh_ready"], 1)
                    act.wait_ge(s["exp_in"], b + 1)
                    act.activation(ex[:], ex[:], ACT.Exp).then_inc(s["exp_out"], 1)
                    act.wait_ge(s["ptr"], b + 1)
                    act.activation(ct[:, bass.ds(b * S, S)], ps[0:ROWS, CB, 0:S // 2].bitcast(BF16), ACT.Copy)
                    act.activation(ct32[:, bass.ds(b * S, S)], ps[0:NE1, VB, :], ACT.Copy).then_inc(s["ct_out"], 1)

            @block.tensor
            def _(pe):
                with pe.Fori(0, B) as b:
                    pe.wait_ge(s["step"], b * RSTEPS + LN_STEPS)
                    for t in range(NT):
                        last = pe.transpose(ps[:, TB, t * P:(t + 1) * P], k.z[:, t, :], k.ident[:])
                    last.then_inc(s["zTr"], 1)
                    pe.wait_ge(s["bl_ready"], b + 1)
                    for t in range(NT):
                        tok = slice(t * P, (t + 1) * P)
                        last = split_product(pe, ps[:, t, 0:NE1], (bh[:, tok], bl[:, tok]), (gwh[:], gwl[:]))
                    last.then_inc(s["logits"], 1)
                    pe.wait_ge(s["step"], b * RSTEPS + RSTEPS)
                    pe.wait_ge(s["ct_out"], b)
                    for t in range(NT):
                        tok = slice(t * P, (t + 1) * P)
                        pe.transpose(ps[0:ROWS, CB, 0:S // 2].bitcast(BF16)[:, tok], parts[:, t, :, :].rearrange("p a e -> p (a e)"), k.ident_bf[:])
                        last = pe.transpose(ps[0:NE1, VB, tok], comb[:, t, :], k.ident[:])
                    last.then_inc(s["ptr"], 1)

        first = d["L1_ffn_dense_1_w"].rearrange("e (f p g) i -> e p f g i", p=P, g=2)
        down = d["L1_ffn_dense_2_w"].rearrange("e i (f n) -> e i f n", n=P)

        with nc.Block() as block:
            @block.sync
            def _(sp):
                with sp.Fori(0, ITS) as it:
                    sp.wait_ge(s["dt_done"], it * EXPERTS)
                    for e in range(EXPERTS):
                        sp.dma_start(wn[e][:], first[it * EXPERTS + e]).then_inc(s["w_in"], 16)
                        sp.dma_start(dn[e][:], down[it * EXPERTS + e]).then_inc(s["w_in"], 16)

            @block.tensor
            def _(pe):
                for c in range(CH):
                    pe.matmul(k.bank(YB + c), b2[:], ct32[:, c * S:(c + 1) * S], start=True, stop=False, skip_group_check=True)
                with pe.Fori(0, ITS) as it:
                    def prepare(e, chunks):
                        pe.wait_ge(s["w_in"], (it + 1) * 32 * EXPERTS)
                        pe.wait_ge(s["wl_out"], it * EXPERTS + e)
                        pe.wait_ge(s["wh_out"], it * EXPERTS + e)
                        for j in range(2 * FB):
                            last = pe.transpose(ps[:, TB, j * P:(j + 1) * P], wn[e][:, j // 2, j % 2, :], k.ident[:])
                        last.then_inc(s["wt_done"], 1)
                        pe.wait_ge(s["c_out"], it * CHUNKS + chunks)
                        for f in range(FB):
                            last = pe.transpose(ps[:, CB, f * P:(f + 1) * P], dn[e][:, f, :], k.ident[:])
                        last.then_inc(s["dt_done"], 1)

                    def hidden(w):
                        e, c, f = w // E_UNITS, w % E_UNITS // FB, w % FB
                        if c == 0 and f == 0:
                            pe.wait_ge(s["wh_out"], it * EXPERTS + e + 1)
                            pe.wait_ge(s["wl_out"], it * EXPERTS + e + 1)
                            pe.wait_ge(s["dt_out"], it * EXPERTS + e + 1)
                        x = (xh[:, c, :], xl[:, c, :])
                        pe.wait_ge(s["g_out"], it * UNITS + w)
                        split_product(pe, k.bank(GB), (wh[e][:, f, 0, :], wl[e][:, f, 0, :]), x).then_inc(s["g_done"], 1)
                        pe.wait_ge(s["v_out"], it * UNITS + w)
                        split_product(pe, k.bank(VB), (wh[e][:, f, 1, :], wl[e][:, f, 1, :]), x).then_inc(s["v_done"], 1)
                        if f == 0:
                            pe.wait_ge(s["c_out"], it * CHUNKS + w // FB)
                            pe.wait_ge(s["dt_out"], it * EXPERTS + (1 if w < MID else 2))
                            k.settle(pe)
                            pe.matmul(k.bank(CB), sel[:, it * EXPERTS + e, :], ct[:, c * S:(c + 1) * S], start=True,
                                      stop=True).then_inc(s["c_done"], 1)

                    def output(w):
                        e, c, f = w // E_UNITS, w % E_UNITS // FB, w % FB
                        pe.wait_ge(s["hid_done"], it * UNITS + w + 1)
                        pe.matmul(k.bank(YB + c), dT[e][:, f, :], hidw[w % 3][:], start=False, stop=False,
                                  skip_group_check=True).then_inc(s["y_units"], 1)

                    prepare(0, 0)
                    for w in range(UNITS + LAG):
                        if w == MID:
                            prepare(1, MID // FB)
                        if w < UNITS:
                            hidden(w)
                        if w >= LAG:
                            output(w - LAG)

            @block.scalar
            def _(act):
                with act.Fori(0, ITS) as it:
                    def prepare(e):
                        act.wait_ge(s["wt_done"], it * EXPERTS + e + 1)
                        act.activation(wh[e][:].rearrange("p f g n -> p (f g n)"), k.bank(TB), ACT.Copy).then_inc(s["wh_out"], 1)
                        act.wait_ge(s["dt_done"], it * EXPERTS + e + 1)
                        act.activation(dT[e][:].rearrange("p f n -> p (f n)"), ps[:, CB, 0:FB * P], ACT.Copy).then_inc(s["dt_out"], 1)

                    prepare(0)
                    for w in range(UNITS):
                        e, f = w // E_UNITS, w % FB
                        if w == MID:
                            prepare(1)
                        column = (it * EXPERTS + e) * FB + f
                        act.wait_ge(s["g_out"], it * UNITS + w + 1)
                        if w >= 3:
                            act.wait_ge(s["h_done"], it * UNITS + w - 2)
                        act.activation(sg[w % 3][:], gate[w % 3][:], ACT.Sigmoid, scale=ALPHA).then_inc(s["sig_out"], 1)
                        act.wait_ge(s["v_done"], it * UNITS + w + 1)
                        k.settle(act)
                        act.activation(val[w % 3][:], k.bank(VB), ACT.Identity, bias=b1[:, 1, bass.ds(column, 1)]).then_inc(s["v_out"], 1)
                        if f == 0:
                            m = w // FB
                            act.wait_ge(s["c_done"], it * CHUNKS + m + 1)
                            if m >= 2:
                                act.wait_ge(s["hid_done"], it * UNITS + (m - 1) * FB)
                            act.activation(ce[m % 2][:], k.bank(CB), ACT.Copy).then_inc(s["c_out"], 1)

            @block.vector
            def _(v):
                with v.Fori(0, ITS) as it:
                    def prepare(e):
                        v.wait_ge(s["wh_out"], it * EXPERTS + e + 1)
                        v.tensor_tensor(wl[e][:].rearrange("p f g n -> p (f g n)"), k.bank(TB),
                                        wh[e][:].rearrange("p f g n -> p (f g n)").bitcast(F32), ALU.subtract).then_inc(s["wl_out"], 1)

                    def gates(w):
                        e, f = w // E_UNITS, w % FB
                        column = (it * EXPERTS + e) * FB + f
                        v.wait_ge(s["g_done"], it * UNITS + w + 1)
                        v.wait_ge(s["t_done"], it * UNITS + (w - 2 if w >= 3 else 0))
                        v.tensor_scalar(gate[w % 3][:], k.bank(GB), b1[:, 0, bass.ds(column, 1)], LIMIT, ALU.add,
                                        ALU.min).then_inc(s["g_out"], 1)

                    def swiglu(w):
                        v.wait_ge(s["sig_out"], it * UNITS + w + 1)
                        v.tensor_tensor(sg[w % 3][:], gate[w % 3][:], sg[w % 3][:], ALU.mult).then_inc(s["t_done"], 1)
                        v.wait_ge(s["t_done"], it * UNITS + w + 1)
                        v.wait_ge(s["clipped"], it * UNITS + w + 1)
                        if w >= 3:
                            v.wait_ge(s["hid_done"], it * UNITS + w - 2)
                        v.scalar_tensor_tensor(hid[w % 3][:], val[w % 3][:], 1.0, sg[w % 3][:], ALU.add, ALU.mult).then_inc(s["h_done"], 1)

                    prepare(0)
                    for w in range(UNITS + 1):
                        if w == MID:
                            prepare(1)
                        if w < UNITS:
                            gates(w)
                        if w >= 1:
                            swiglu(w - 1)

            @block.gpsimd
            def _(pool):
                with pool.Fori(0, ITS) as it:
                    def weigh(w):
                        m = w // FB
                        pool.wait_ge(s["h_done"], it * UNITS + w + 1)
                        pool.wait_ge(s["c_out"], it * CHUNKS + m + 1)
                        if w >= 3:
                            pool.wait_ge(s["y_units"], it * UNITS + w - 2)
                        pool.tensor_tensor(hidw[w % 3][:], hid[w % 3][:], ce[m % 2][:], ALU.mult).then_inc(s["hid_done"], 1)

                    for w in range(UNITS + 1):
                        if w < UNITS:
                            pool.wait_ge(s["v_out"], it * UNITS + w + 1)
                            k.settle(pool)
                            pool.tensor_scalar(val[w % 3][:], val[w % 3][:], LIMIT, -LIMIT, ALU.min, ALU.max).then_inc(s["clipped"], 1)
                        if w >= 1:
                            weigh(w - 1)

        residual_block(k, s, yT, YB)
    k.n_ln += B * LNS
STAGES = [stage_attention_0, stage_cross_attention_0, stage_experts_0, stage_attention_1, stage_cross_attention_1, stage_experts_1]


def build(nc, dram, out):
    with ExitStack() as ctx:
        k = Kernel(nc, ctx, dram, out)
        stage_setup(k)
        for stage in STAGES:
            stage(k)
            k.end_stage()
        stage_store(k)



_INS = (
    "x", "ctx_1024", "mask_Bx1xSxS2_if1", "L0_attn_gamma",
    "L0_attn_w_q", "L0_attn_w_kv", "L0_attn_null_kv", "L0_attn_q_scale",
    "L0_attn_k_scale", "L0_attn_w_out", "L0_xattn_Wq", "L0_xattn_bq",
    "L0_xattn_Wk", "L0_xattn_bk", "L0_xattn_Wv", "L0_xattn_bv",
    "L0_xattn_Wo", "L0_xattn_bo", "L0_ffn_router_w", "L0_ffn_expert_bias",
    "L0_ffn_w_gate", "L0_ffn_w_down", "L0_ffn_w_gate_shared", "L0_ffn_w_down_shared",
    "L1_attn_w_qkv", "L1_attn_w_out", "L1_attn_b_out", "L1_xattn_Wv",
    "L1_xattn_Wk", "L1_xattn_Wq", "L1_xattn_Wo", "L1_xattn_bo",
    "L1_ffn_gate_w", "L1_ffn_dense_1_w", "L1_ffn_dense_1_b", "L1_ffn_dense_2_w",
    "L1_ffn_dense_2_b",
)


def kernel(**inputs):
    import numpy as _np
    import concourse.bacc as _bacc
    from concourse import mybir as _mybir
    from concourse.bass_utils import run_bass_kernel_spmd as _run

    nc = _bacc.Bacc("TRN2", target_bir_lowering=False, num_devices=1)
    arrays, dram = {}, {}
    for name in _INS:
        a = _np.ascontiguousarray(inputs[name])
        arrays[f"in_{name}_dram"] = a
        dram[name] = nc.dram_tensor(f"in_{name}_dram", a.shape, _mybir.dt.from_np(a.dtype), kind="ExternalInput").ap()
    out = nc.dram_tensor("out_0_dram", (B, S, D), F32, kind="ExternalOutput").ap()
    build(nc, dram, out)
    r = _run(nc, [arrays], core_ids=[0])
    return r.results[0]["out_0_dram"]
```

```python
from contextlib import ExitStack
import math

import numpy as np

import concourse.bass as bass
from concourse import mybir

ALU = mybir.AluOpType
ACT = mybir.ActivationFunctionType
AX = mybir.AxisListType.X
F32 = mybir.dt.float32
F32R = mybir.dt.float32r
BF16 = mybir.dt.bfloat16
I32 = mybir.dt.int32

P = 128
B = 4
S = 512
D = 128
NT = S // P
TT = B * NT
KC = 77
EPS = 1e-5

H0, HD0 = 16, 64
HC0, HDC0 = 8, 16
H1, HD1 = 16, 8
NE0, IN0, TOP0 = 160, 64, 8
NE1, FF1 = 8, 256
NEG = -1.0e30


def alibi_slopes():
    start = 2.0 ** (-2.0 ** (-(math.log2(H0) - 3.0)))
    return [float(np.float32(start * start ** i)) for i in range(H0)]


class Kernel:

    def __init__(self, nc, ctx, dram, out):
        self.nc, self.ctx, self.dram, self.out = nc, ctx, dram, out
        self.sems = []
        sb = self.sb
        self.ps = ctx.enter_context(nc.psum_tensor("ps", [P, 8, 512], F32))
        self.x = sb(ctx, "x_resid", [P, TT, D])
        self.ident = sb(ctx, "ident", [P, P])
        self.ident_bf = sb(ctx, "ident_bf", [P, P], BF16)
        self.mhalf = sb(ctx, "mhalf", [P, NT])
        self.stats = sb(ctx, "ln_stats", [P, TT, 6])
        self.mv = sb(ctx, "ln_mean_var", [P, TT, 2])
        self.ve = sb(ctx, "ln_var_eps", [P, TT])
        self.rstd = sb(ctx, "ln_rstd", [P, TT])
        self.z = sb(ctx, "ln_out", [P, TT, D])
        self.zb = sb(ctx, "ln_batch", [P, NT, D])
        self.zb_ready = self.sem("zb_ready")
        self.n_batches = 0
        self.var_ready = self.sem("var_ready")
        self.rstd_ready = self.sem("rstd_ready")
        self.ln_step = self.sem("ln_step")
        self.z_ready = self.sem("z_ready")
        self.passed = self.sem("passed")
        self.n_ln = 0
        self.sems = []

    def sb(self, ctx, name, shape, dt=F32):
        return ctx.enter_context(self.nc.sbuf_tensor(name, shape, dt))

    def sem(self, name):
        self.sems.append(self.nc.alloc_semaphore(name=name))
        return self.sems[-1]

    def end_stage(self):
        self.nc.clear_and_free_semaphores(self.sems)
        self.nc.all_engine_barrier()
        self.sems = []

    def settle(self, engine):
        engine.sem_inc(self.passed, 1)

    def bank(self, b):
        return self.ps[:, b, :]


def split_product(pe, out, left, right, start=True, stop=True, skip=False):
    (lh, ll), (rh, rl) = left, right
    pe.matmul(out, lh, rh, start=start, stop=False, skip_group_check=skip)
    pe.matmul(out, ll, rh, start=False, stop=False, skip_group_check=skip)
    return pe.matmul(out, lh, rl, start=False, stop=stop, skip_group_check=skip)


def chain(engine, sem, per_pass=0, i=0):
    count = [0]

    def step(ins, k=None):
        count[0] += 1
        ins.then_inc(sem, 1)
        engine.wait_ge(sem, i * per_pass + count[0])
        if k:
            k.settle(engine)

    step.count = count
    return step


def layernorm_vector(k, v, src, n=0):
    n = k.n_ln + n
    step = chain(v, k.ln_step)
    step.count[0] = 2 * B * n

    def statistics(b):
        tiles = range(b * NT, (b + 1) * NT)
        for t in tiles:
            last = v.bn_stats(k.stats[:, t, :], src[:, t, :])
        step(last)
        for t in tiles:
            last = v.bn_aggr(k.mv[:, t, :], k.stats[:, t, :])
        step(last)
        v.tensor_scalar(k.ve[:, b * NT:(b + 1) * NT], k.mv[:, b * NT:(b + 1) * NT, 1], EPS, None, ALU.add).then_inc(k.var_ready, 1)

    def scale(b):
        v.wait_ge(k.rstd_ready, B * n + b + 1)
        for t in range(b * NT, (b + 1) * NT):
            last = v.tensor_scalar(k.z[:, t, :], src[:, t, :], k.mv[:, t, 0:1], k.rstd[:, t:t + 1], ALU.subtract, ALU.mult)
        last.then_inc(k.z_ready, 1)

    for b in range(B + 1):
        if b < B:
            statistics(b)
        if b:
            scale(b - 1)
    v.wait_ge(k.z_ready, B * (n + 1))


def take_batch(k, v, b):
    v.tensor_copy(k.zb[:], k.z[:, bass.ds(b * NT, NT), :]).then_inc(k.zb_ready, 1)


def layernorm_pool(k, pool, n=0):
    for b in range(B):
        pool.wait_ge(k.var_ready, B * (k.n_ln + n) + b + 1)
        tiles = slice(b * NT, (b + 1) * NT)
        pool.tensor_tensor(k.rstd[:, tiles], k.ve[:, tiles], k.mhalf[:], ALU.pow).then_inc(k.rstd_ready, 1)


def stage_setup(k):
    nc, d = k.nc, k.dram
    made, x_in = k.sem("const_made"), k.sem("x_loaded")
    with nc.Block() as block:
        @block.sync
        def _(sp):
            sp.dma_start(k.x[:], d["x"].rearrange("b (t p) d -> p (b t) d", p=P)).then_inc(x_in, 16)
            sp.wait_ge(x_in, 16)

        @block.gpsimd
        def _(pool):
            pool.memset(k.mhalf[:], -0.5)
            pool.memset(k.ident[:], 1.0).then_inc(made, 1)
            pool.wait_ge(made, 1)
            pool.affine_select(out=k.ident[:], in_=k.ident[:], compare_op=ALU.is_equal, fill=0.0, base=0,
                               pattern=[[1, P]], channel_multiplier=-1).then_inc(made, 1)
            pool.wait_ge(made, 2)
            pool.tensor_copy(k.ident_bf[:], k.ident[:]).then_inc(made, 1)
            pool.wait_ge(made, 3)


def stage_store(k):
    nc = k.nc
    stored = k.sem("out_stored")
    with nc.Block() as block:
        @block.sync
        def _(sp):
            sp.dma_start(k.out.rearrange("b (t p) d -> p (b t) d", p=P), k.x[:]).then_inc(stored, 16)
            sp.wait_ge(stored, 16)
def stage_attention_0(k):
    nc, d = k.nc, k.dram
    PAIRS = H0 // 2
    NULLS = 2
    W = H0 * HD0
    NK = NULLS + S
    AHEAD = 2
    RP = 3
    STEPS = NT * 6
    slopes = alibi_slopes()

    def keys(i):
        return NULLS + (i + 1) * P

    with ExitStack() as ctx:
        def sb(name, shape, dt=F32):
            return k.sb(ctx, "a0_" + name, shape, dt)

        wqkv = [[sb(f"w{n}{part}", [P, W], F32R) for part in "hl"] for n in "qkv"]
        wo = [sb(f"wo_{part}", [P, PAIRS, D], F32R) for part in "hl"]
        stage = sb("stage", [P, W])
        gamma = sb("gamma", [P, 1])
        qs_col = sb("qs_col", [P, 1])
        ks_col = sb("ks_col", [P, 1])
        kscale = sb("kscale", [P, 1])
        dist = sb("dist", [P, NK])
        nk_raw = sb("nk_raw", [NULLS, H0, HD0])
        nk_sq = sb("nk_sq", [NULLS, H0, HD0])
        nk_r = sb("nk_r", [NULLS, H0])
        nk_n = sb("nk_n", [NULLS, H0, HD0])
        nkh = sb("nkh", [P, PAIRS, NULLS], F32R)
        nkl = sb("nkl", [P, PAIRS, NULLS], F32R)
        nv = sb("nv", [4, PAIRS, P])
        xh, xl = sb("xh", [P, S], F32R), sb("xl", [P, S], F32R)
        sq = sb("sq", [P, 2, W])
        ss = sb("ss", [P, 2, H0])
        norm = sb("norm", [P, 2, H0])
        rnorm = sb("rnorm", [P, 2, H0])
        qn, kn, vv = (sb(n, [P, NT, W]) for n in ("qn", "kn", "vv"))
        qh = [[sb(f"qh{r}{e}", [P, S], F32R) for e in range(2)] for r in range(2)]
        ql = [[sb(f"ql{r}{e}", [P, S], F32R) for e in range(2)] for r in range(2)]
        kh = [sb(f"kh{r}", [P, NK], F32R) for r in range(2)]
        kl = [sb(f"kl{r}", [P, NK], F32R) for r in range(2)]
        ptok = [sb(f"ptok{r}", [P, NT, 4]) for r in range(2)]
        bias = [sb(f"bias{r}", [P, NK]) for r in range(2)]
        sc = [sb(f"sc{r}", [P, NK]) for r in range(2)]
        nmax = sb("nmax", [P, RP, NT])
        sums = sb("sums", [P, RP, NT])
        rsum = sb("rsum", [P, RP, NT])
        prob = sb("prob", [P, RP, NT, NK + 2])
        pt = [[sb(f"pt{r}_{kt}", [P, S - kt * P]) for kt in range(NT)] for r in range(2)]
        pn = sb("pn", [4, S])
        oh, ol = sb("oh", [P, S], F32R), sb("ol", [P, S], F32R)
        yT = stage[:, 0:S]

        names = ("loaded staged split consts nulls step zT_ready xh_ready xT_ready q_done k_done v_done "
                 "sq_q sq_k ssum norm_ready v_free qT kT qhi_ready qst_ready kh_ready kst_ready bias_ready "
                 "score tile_scored exp_done prob_ready ptr pt_evac pt_evac_a nptr npt_evac pv oh_ready o_ready y_done yT_ready "
                 "y_tok batch_done nT nt_done nkh_done rs_ready")
        s = {n: k.sem("a0_" + n) for n in names.split()}
        ps = k.ps
        TB, OB, YB = 4, 6, 7
        PB = (3, 5)

        def slot(i):
            return ps[:, 0:2, :].rearrange("p a n -> p (a n)") if i % 2 else ps[:, 2, :]


        weights = [("wq", wqkv[0]), ("wk", wqkv[1]), ("wv", wqkv[2]), ("wo", wo)]

        with nc.Block() as block:
            @block.sync
            def _(sp):
                src = {"wq": d["L0_attn_w_q"], "wk": d["L0_attn_w_kv"][:, 0:W], "wv": d["L0_attn_w_kv"][:, W:2 * W],
                       "wo": d["L0_attn_w_out"].rearrange("(h p) d -> p h d", p=P)}
                for n, (name, _) in enumerate(weights):
                    if n:
                        sp.wait_ge(s["split"], 2 * n)
                    dst = stage[:] if name != "wo" else stage[:].rearrange("p (h d) -> p h d", d=D)
                    sp.dma_start(dst, src[name]).then_inc(s["staged"], 16)
                for col, name in ((gamma, "L0_attn_gamma"),):
                    sp.dma_start(col[:], d[name].rearrange("(p a) -> p a", a=1)).then_inc(s["loaded"], 16)
                for half in range(2):
                    sp.dma_start(qs_col[half * HD0:(half + 1) * HD0, :],
                                 d["L0_attn_q_scale"].rearrange("(p a) -> p a", a=1)).then_inc(s["loaded"], 16)
                    sp.dma_start(ks_col[half * HD0:(half + 1) * HD0, :],
                                 d["L0_attn_k_scale"].rearrange("(p a) -> p a", a=1)).then_inc(s["loaded"], 16)
                nkv = d["L0_attn_null_kv"].rearrange("h (n two) d -> two n h d", two=2)
                sp.dma_start(nk_raw[:], nkv[0]).then_inc(s["loaded"], 16)
                sp.wait_ge(s["nulls"], 1)
                nvp = d["L0_attn_null_kv"].rearrange("(g e) (n two) d -> e two n g d", two=2, e=2)
                for e in range(2):
                    sp.dma_start(nv[2 * e:2 * e + 2, :, e * HD0:(e + 1) * HD0], nvp[e, 1]).then_inc(s["loaded"], 16)
                sp.wait_ge(s["loaded"], 16 * 8)

            @block.gpsimd
            def _(pool):
                layernorm_pool(k, pool)
                layernorm_pool(k, pool, 1)
                pool.memset(nv[:], 0.0).then_inc(s["nulls"], 1)
                for r in range(2):
                    for half in (qh, ql):
                        for e in range(2):
                            pool.memset(half[r][e][:].bitcast(F32), 0.0)
                pool.iota(dist[:], [[1, NK]], base=-(S - P) - NULLS, channel_multiplier=-1,
                          allow_small_or_imprecise_dtypes=True).then_inc(s["consts"], 1)
                pool.wait_ge(s["consts"], 1)
                pool.affine_select(out=dist[:], in_=dist[:], compare_op=ALU.is_ge, fill=NEG,
                                   base=(S - P) + NULLS, pattern=[[-1, NK]], channel_multiplier=1).then_inc(s["consts"], 1)

            @block.scalar
            def _(act):
                for n, (name, halves) in enumerate(weights):
                    act.wait_ge(s["staged"], 16 * (n + 1))
                    dst = halves[0][:] if name != "wo" else halves[0][:].rearrange("p h d -> p (h d)")
                    act.activation(dst, stage[:], ACT.Copy).then_inc(s["split"], 1)
                act.wait_ge(s["nt_done"], 1)
                act.activation(nk_r[:], nk_r[:], ACT.Sqrt).then_inc(s["nt_done"], 1)
                act.wait_ge(s["nT"], 1)
                act.activation(nkh[:].rearrange("p h n -> p (h n)"), ps[:, 0, 0:H0], ACT.Identity,
                               scale=kscale[:, 0:1]).then_inc(s["nkh_done"], 1)

            @block.vector
            def _(v):
                layernorm_vector(k, v, k.x)
                layernorm_vector(k, v, k.z, 1)
                for n, (name, halves) in enumerate(weights):
                    v.wait_ge(s["split"], 2 * n + 1)
                    flat = (lambda t: t[:]) if name != "wo" else (lambda t: t[:].rearrange("p h d -> p (h d)"))
                    v.tensor_tensor(flat(halves[1]), stage[:], flat(halves[0]).bitcast(F32), ALU.subtract).then_inc(s["split"], 1)
                step = chain(v, s["step"])
                v.wait_ge(s["loaded"], 16 * 8)
                step(v.scalar_tensor_tensor(kscale[:], qs_col[:], 8.0, ks_col[:], ALU.mult, ALU.mult))
                step(v.tensor_tensor(nk_sq[:], nk_raw[:], nk_raw[:], ALU.mult))
                v.tensor_reduce(nk_r[:], nk_sq[:], AX, ALU.add).then_inc(s["nt_done"], 1)
                v.wait_ge(s["nt_done"], 2)
                step(v.tensor_scalar(nk_r[:], nk_r[:], 1e-12, None, ALU.max))
                step(v.reciprocal(nk_r[:], nk_r[:]))
                v.tensor_tensor(nk_n[:], nk_raw[:], nk_r[:].unsqueeze(2).to_broadcast([NULLS, H0, HD0]), ALU.mult).then_inc(s["nt_done"], 1)
                v.wait_ge(s["nkh_done"], 1)
                v.scalar_tensor_tensor(nkl[:].rearrange("p h n -> p (h n)"), ps[:, 0, 0:H0], kscale[:, 0:1],
                                       nkh[:].rearrange("p h n -> p (h n)").bitcast(F32), ALU.mult, ALU.subtract)

            @block.tensor
            def _(pe):
                pe.wait_ge(s["nt_done"], 3)
                for g in range(PAIRS):
                    last = pe.transpose(ps[:, 0, NULLS * g:NULLS * g + NULLS],
                                        nk_n[:, 2 * g:2 * g + 2, :].rearrange("p e d -> p (e d)"), k.ident[0:NULLS, 0:NULLS])
                last.then_inc(s["nT"], 1)

        step0 = 4

        with nc.Block() as block:
            @block.vector
            def _(v):
                with v.Fori(0, B) as b:
                    v.wait_ge(s["batch_done"], b)
                    take_batch(k, v, b)
                    step = chain(v, s["step"], STEPS, b)
                    step.count[0] = step0
                    v.wait_ge(s["xh_ready"], b + 1)
                    v.scalar_tensor_tensor(xl[:], k.bank(0), gamma[:, 0:1], xh[:].bitcast(F32), ALU.mult,
                                           ALU.subtract).then_inc(s["xT_ready"], 1)
                    for t in range(NT):
                        for j, (squared, dst) in enumerate((("sq_q", qn), ("sq_k", kn))):
                            v.wait_ge(s[squared], b * NT + t + 1)
                            v.tensor_reduce(ss[:, j, :], sq[:, j, :].rearrange("p (h e) -> p h e", e=HD0), AX,
                                            ALU.add).then_inc(s["ssum"], 1)
                            v.wait_ge(s["norm_ready"], b * 2 * NT + 2 * t + j + 1)
                            step(v.tensor_scalar(norm[:, j, :], norm[:, j, :], 1e-12, None, ALU.max))
                            step(v.reciprocal(rnorm[:, j, :], norm[:, j, :]))
                            step(v.tensor_tensor(dst[:, t, :].rearrange("p (h e) -> p h e", e=HD0),
                                                 ps[:, 2 * j:2 * j + 2, :].rearrange("p a (h e) -> p (a h) e", e=HD0),
                                                 rnorm[:, j, :].unsqueeze(2).to_broadcast([P, H0, HD0]), ALU.mult))

                    def prepare_q(g):
                        r = g % 2
                        v.wait_ge(s["qhi_ready"], b * PAIRS + g + 1)
                        for e in range(2):
                            rows = slice(e * HD0, (e + 1) * HD0)
                            last = v.tensor_tensor(ql[r][e][rows, :], ps[rows, TB, :], qh[r][e][rows, :].bitcast(F32),
                                                   ALU.subtract)
                        last.then_inc(s["qst_ready"], 1)

                    def prepare_k(g):
                        r = g % 2
                        v.wait_ge(s["kh_ready"], b * PAIRS + g + 1)
                        v.scalar_tensor_tensor(kl[r][:, NULLS:NK], ps[:, TB, :], kscale[:, 0:1],
                                               kh[r][:, NULLS:NK].bitcast(F32), ALU.mult, ALU.subtract).then_inc(s["kst_ready"], 1)

                    def score(h, i):
                        u = h * NT + i
                        if i == 0:
                            v.wait_ge(s["bias_ready"], b * H0 + h + 1)
                        v.wait_ge(s["score"], b * H0 * NT + u + 1)
                        if u >= 2:
                            v.wait_ge(s["exp_done"], b * H0 * NT + u - 1)
                        k.settle(v)
                        v.tensor_tensor_reduce(sc[u % 2][:, 0:keys(i)], slot(i)[:, 0:keys(i)],
                                               bias[h % 2][:, S - P - i * P:NK], -1.0, 3.0e38, ALU.add, ALU.min,
                                               nmax[:, h % RP, i:i + 1]).then_inc(s["tile_scored"], 1)

                    def output_low(g):
                        v.wait_ge(s["oh_ready"], b * PAIRS + g + 1)
                        v.tensor_tensor(ol[:], k.bank(OB), oh[:].bitcast(F32), ALU.subtract).then_inc(s["o_ready"], 1)

                    def invert(h):
                        v.wait_ge(s["exp_done"], b * H0 * NT + h * NT + NT)
                        v.reciprocal(rsum[:, h % RP, :], sums[:, h % RP, :]).then_inc(s["rs_ready"], 1)

                    def evacuate(h, kt):
                        r = h % 2
                        v.wait_ge(s["ptr"], b * H0 * NT + h * NT + kt + 1)
                        if h >= 2:
                            v.wait_ge(s["pv"], b * H0 + h - 1)
                        v.tensor_copy(pt[r][kt][:], ps[:, PB[kt % 2], 0:S - kt * P]).then_inc(s["pt_evac"], 1)

                    prepare_q(0)
                    prepare_k(0)
                    for h in range(AHEAD):
                        for i in range(NT):
                            score(h, i)
                    invert(0)
                    prepare_q(1)
                    prepare_k(1)
                    for h in range(H0):
                        if h % 2 == 0 and h:
                            output_low(h // 2 - 1)
                        for i in range(NT):
                            if h + AHEAD < H0:
                                score(h + AHEAD, i)
                            if i == 0 and h + 1 < H0:
                                invert(h + 1)
                            if i == 2 and h // 2 + 2 < PAIRS:
                                (prepare_k if h % 2 else prepare_q)(h // 2 + 2)
                            if i % 2:
                                evacuate(h, i)
                    output_low(PAIRS - 1)
                    v.wait_ge(s["y_tok"], b + 1)
                    v.tensor_tensor(k.x[:, bass.ds(b * NT, NT), :], k.x[:, bass.ds(b * NT, NT), :],
                                    k.bank(TB).rearrange("p (t d) -> p t d", d=D), ALU.add).then_inc(s["batch_done"], 1)
                    assert step.count[0] == step0 + STEPS

            @block.gpsimd
            def _(pool):
                with pool.Fori(0, B) as b:
                    pool.wait_ge(s["batch_done"], b)

                    def head_constants(h):
                        r = h % 2
                        if h >= 2:
                            pool.wait_ge(s["tile_scored"], b * H0 * NT + (h - 1) * NT)
                        k.settle(pool)
                        last = pool.tensor_scalar(bias[r][:], dist[:], slopes[h], 1.0, ALU.mult, ALU.mult)
                        if h % 2 == 0:
                            r = h // 2 % 2
                            pool.tensor_copy(kh[r][:, 0:NULLS], nkh[:, h // 2, :].bitcast(F32))
                            last = pool.tensor_copy(kl[r][:, 0:NULLS], nkl[:, h // 2, :].bitcast(F32))
                        last.then_inc(s["bias_ready"], 1)

                    for h in range(AHEAD):
                        head_constants(h)
                    for h in range(H0):
                        r = h % RP
                        pool.wait_ge(s["rs_ready"], b * H0 + h + 1)
                        k.settle(pool)
                        for i in range(NT):
                            last = pool.tensor_scalar(prob[:, r, i, 0:keys(i)], prob[:, r, i, 0:keys(i)], rsum[:, r, i:i + 1],
                                                      0.0, ALU.mult, ALU.add)
                        last.then_inc(s["prob_ready"], 1)
                        if h + AHEAD < H0:
                            head_constants(h + AHEAD)
                        pool.wait_ge(s["prob_ready"], b * 2 * H0 + 2 * h + 1)
                        k.settle(pool)
                        pool.tensor_copy(ptok[h // 2 % 2][:, :, 2 * (h % 2):2 * (h % 2) + 2], prob[:, r, :, 0:NULLS]).then_inc(s["prob_ready"], 1)

            @block.scalar
            def _(act):
                with act.Fori(0, B) as b:
                    act.wait_ge(s["zT_ready"], b + 1)
                    act.activation(xh[:], k.bank(0), ACT.Identity, scale=gamma[:, 0:1]).then_inc(s["xh_ready"], 1)
                    for t in range(NT):
                        n = b * NT + t + 1
                        act.wait_ge(s["q_done"], n)
                        act.activation(sq[:, 0, :], ps[:, 0:2, :].rearrange("p a n -> p (a n)"), ACT.Square).then_inc(s["sq_q"], 1)
                        act.wait_ge(s["ssum"], 2 * (b * NT + t) + 1)
                        act.activation(norm[:, 0, :], ss[:, 0, :], ACT.Sqrt).then_inc(s["norm_ready"], 1)
                        act.wait_ge(s["k_done"], n)
                        act.activation(sq[:, 1, :], ps[:, 2:4, :].rearrange("p a n -> p (a n)"), ACT.Square).then_inc(s["sq_k"], 1)
                        act.wait_ge(s["v_done"], n)
                        act.activation(vv[:, t, :], ps[:, 6:8, :].rearrange("p a n -> p (a n)"), ACT.Copy).then_inc(s["v_free"], 1)
                        act.wait_ge(s["ssum"], 2 * (b * NT + t) + 2)
                        act.activation(norm[:, 1, :], ss[:, 1, :], ACT.Sqrt).then_inc(s["norm_ready"], 1)

                    def prepare_q(g):
                        act.wait_ge(s["qT"], b * PAIRS + g + 1)
                        for e in range(2):
                            rows = slice(e * HD0, (e + 1) * HD0)
                            last = act.activation(qh[g % 2][e][rows, :], ps[rows, TB, :], ACT.Copy)
                        last.then_inc(s["qhi_ready"], 1)

                    def prepare_k(g):
                        r = g % 2
                        act.wait_ge(s["kT"], b * PAIRS + g + 1)
                        act.activation(kh[r][:, NULLS:NK], ps[:, TB, :], ACT.Identity, scale=kscale[:, 0:1]).then_inc(s["kh_ready"], 1)

                    def exp(h, i):
                        r, u = h % RP, h * NT + i
                        act.wait_ge(s["tile_scored"], b * H0 * NT + u + 1)
                        if h >= RP:
                            act.wait_ge(s["ptr"], b * H0 * NT + (h - RP + 1) * NT)
                            act.wait_ge(s["prob_ready"], b * 2 * H0 + 2 * (h - RP + 1))
                        act.activation(prob[:, r, i, 0:keys(i)], sc[u % 2][:, 0:keys(i)], ACT.Exp, scale=-1.0,
                                       bias=nmax[:, r, i:i + 1], accum_out=sums[:, r, i:i + 1]).then_inc(s["exp_done"], 1)

                    def evacuate(h, kt):
                        r = h % 2
                        act.wait_ge(s["ptr"], b * H0 * NT + h * NT + kt + 1)
                        if h >= 2:
                            act.wait_ge(s["pv"], b * H0 + h - 1)
                        act.activation(pt[r][kt][:], ps[:, PB[kt % 2], 0:S - kt * P], ACT.Copy).then_inc(s["pt_evac_a"], 1)

                    prepare_q(0)
                    prepare_k(0)
                    for h in range(AHEAD):
                        for i in range(NT):
                            exp(h, i)
                    prepare_q(1)
                    prepare_k(1)
                    for h in range(H0):
                        for i in range(NT):
                            if i % 2 == 0:
                                evacuate(h, i)
                            if h + AHEAD < H0:
                                exp(h + AHEAD, i)
                            if i == 1 and h // 2 + 2 < PAIRS:
                                (prepare_k if h % 2 else prepare_q)(h // 2 + 2)
                        if h % 2:
                            g = h // 2
                            act.wait_ge(s["nptr"], b * PAIRS + g + 1)
                            act.activation(pn[:], ps[0:4, PB[0], :], ACT.Copy).then_inc(s["npt_evac"], 1)
                            act.wait_ge(s["pv"], b * H0 + h + 1)
                            if g:
                                act.wait_ge(s["y_done"], b * PAIRS + g)
                            act.activation(oh[:], k.bank(OB), ACT.Copy).then_inc(s["oh_ready"], 1)
                    act.wait_ge(s["y_done"], b * PAIRS + PAIRS)
                    act.activation(yT, k.bank(YB), ACT.Copy).then_inc(s["yT_ready"], 1)

            @block.tensor
            def _(pe):
                with pe.Fori(0, B) as b:
                    pe.wait_ge(s["step"], b * STEPS + step0)
                    pe.wait_ge(k.zb_ready, k.n_batches + b + 1)
                    for t in range(NT):
                        last = pe.transpose(ps[:, 0, t * P:(t + 1) * P], k.zb[:, t, :], k.ident[:])
                    last.then_inc(s["zT_ready"], 1)
                    pe.wait_ge(s["xT_ready"], b + 1)
                    for t in range(NT):
                        tok = slice(t * P, (t + 1) * P)
                        for j, done in ((0, "q_done"), (1, "k_done"), (2, "v_done")):
                            if t and j < 2:
                                pe.wait_ge(s["step"], b * STEPS + step0 + 6 * (t - 1) + 3 + 3 * j)
                            if t and j == 2:
                                pe.wait_ge(s["v_free"], b * NT + t)
                            for half in range(2):
                                cols = slice(half * 512, half * 512 + 512)
                                last = split_product(pe, k.bank((0, 2, 6)[j] + half), (xh[:, tok], xl[:, tok]),
                                                     (wqkv[j][0][:, cols], wqkv[j][1][:, cols]))
                            last.then_inc(s[done], 1)
                    pe.wait_ge(s["v_free"], b * NT + NT)

                    def prepare(g, src, done):
                        for t in range(NT):
                            last = pe.transpose(ps[:, TB, t * P:(t + 1) * P], src[:, t, g * P:(g + 1) * P], k.ident[:])
                        last.then_inc(s[done], 1)

                    def keys_ready(h):
                        if h % 2 == 0:
                            pe.wait_ge(s["kst_ready"], b * PAIRS + h // 2 + 1)
                            pe.wait_ge(s["bias_ready"], b * H0 + h + 1)

                    def score(h, i):
                        r, e, u = h // 2 % 2, h % 2, h * NT + i
                        if i == 0:
                            keys_ready(h)
                        if u >= 2:
                            pe.wait_ge(s["tile_scored"], b * H0 * NT + u - 1)
                        tile = slice(i * P, (i + 1) * P)
                        for lo, hi in ((0, min(keys(i), 512)), (512, keys(i))):
                            if hi > lo:
                                last = split_product(pe, slot(i)[:, lo:hi], (qh[r][e][:, tile], ql[r][e][:, tile]),
                                                     (kh[r][:, lo:hi], kl[r][:, lo:hi]))
                        last.then_inc(s["score"], 1)

                    def evacuated(h, kt):
                        if kt % 2:
                            pe.wait_ge(s["pt_evac"], b * H0 * 2 + h * 2 + kt // 2 + 1)
                        else:
                            pe.wait_ge(s["pt_evac_a"], b * H0 * 2 + h * 2 + kt // 2 + 1)

                    def transpose_probs(h, kt):
                        r, u = h % RP, h * NT + kt
                        if u >= 2:
                            evacuated((u - 2) // NT, (u - 2) % NT)
                        if kt == 0 and h and h % 2 == 0:
                            pe.wait_ge(s["npt_evac"], b * PAIRS + h // 2)
                        if kt == 0:
                            pe.wait_ge(s["prob_ready"], b * 2 * H0 + 2 * h + 1)
                        for i in range(kt, NT):
                            last = pe.transpose(ps[:, PB[kt % 2], (i - kt) * P:(i - kt + 1) * P],
                                                prob[:, r, i, NULLS + kt * P:NULLS + (kt + 1) * P], k.ident[:])
                        last.then_inc(s["ptr"], 1)

                    def values(h, kt):
                        r, e = h % 2, h % 2
                        evacuated(h, kt)
                        last = pe.matmul(ps[e * HD0:(e + 1) * HD0, OB, kt * P:S], vv[:, kt, h * HD0:(h + 1) * HD0], pt[r][kt][:],
                                         start=(kt == 0), stop=(kt == NT - 1 and e == 0), skip_group_check=True)
                        if kt == NT - 1 and e == 0:
                            last.then_inc(s["pv"], 1)

                    def pair_nulls(g):
                        evacuated(2 * g + 1, 2)
                        pe.wait_ge(s["prob_ready"], b * 2 * H0 + 4 * g + 4)
                        for i in range(NT):
                            last = pe.transpose(ps[0:4, PB[0], i * P:(i + 1) * P], ptok[g % 2][:, i, :], k.ident[:])
                        last.then_inc(s["nptr"], 1)

                    def pair_end(g):
                        pe.wait_ge(s["npt_evac"], b * PAIRS + g + 1)
                        pe.matmul(k.bank(OB), nv[:, g, :], pn[:], start=False, stop=True,
                                  skip_group_check=True).then_inc(s["pv"], 1)

                    def project(g):
                        pe.wait_ge(s["o_ready"], b * PAIRS + g + 1)
                        split_product(pe, k.bank(YB), (wo[0][:, g, :], wo[1][:, g, :]), (oh[:], ol[:]), start=(g == 0),
                                      stop=(g == PAIRS - 1)).then_inc(s["y_done"], 1)

                    pe.wait_ge(s["step"], b * STEPS + step0 + 6 * NT)
                    for g in range(2):
                        if g:
                            pe.wait_ge(s["kst_ready"], b * PAIRS + g)
                        prepare(g, qn, "qT")
                        pe.wait_ge(s["qst_ready"], b * PAIRS + g + 1)
                        prepare(g, kn, "kT")
                        if g == 0:
                            for h in range(AHEAD):
                                for i in range(NT):
                                    score(h, i)
                    for h in range(H0):
                        g = h // 2
                        if g + 2 < PAIRS:
                            if h % 2:
                                pe.wait_ge(s["qst_ready"], b * PAIRS + g + 3)
                                prepare(g + 2, kn, "kT")
                            else:
                                pe.wait_ge(s["kst_ready"], b * PAIRS + g + 2)
                                prepare(g + 2, qn, "qT")
                        for i in range(NT):
                            if h + AHEAD < H0:
                                score(h + AHEAD, i)
                            transpose_probs(h, i)
                            if i == 1 and h % 2 == 0 and h:
                                project(g - 1)
                            if i == 3 and h % 2:
                                pair_nulls(g)
                            if i == 0:
                                if h % 2 == 0 and h:
                                    pe.wait_ge(s["o_ready"], b * PAIRS + h // 2)
                            else:
                                values(h, i - 1)
                        values(h, NT - 1)
                        if h % 2:
                            pair_end(g)
                    project(PAIRS - 1)
                    pe.wait_ge(s["yT_ready"], b + 1)
                    for t in range(NT):
                        last = pe.transpose(ps[:, TB, t * P:(t + 1) * P], yT[:, t * P:(t + 1) * P], k.ident[:])
                    last.then_inc(s["y_tok"], 1)
    k.n_ln += 2
    k.n_batches += B


def cross_attention(k, pre, heads, hd, weights, biases, out_bias, scale, causal, mask):
    nc, d = k.nc, k.dram
    HALF = 8
    U1 = heads // HALF
    U = NT * U1
    G = heads // 4
    STEPS = U * (2 + (mask is not None)) + U1 * causal + NT - 1
    RP = 4

    with ExitStack() as ctx:
        def sb(name, shape, dt=F32):
            return k.sb(ctx, pre + name, shape, dt)

        def sem(name):
            return k.sem(pre + name)

        w_nat = sb("w_nat", [P, 4, P])
        wt = sb("w", [P, 3, P])
        wo = sb("wo", [P, G, P])
        woT = sb("woT", [P, P])
        bcol = sb("bcol", [P, 2])
        brow = sb("brow", [P, 2, P])
        head_mask = sb("head_mask", [P, heads])
        ctx_nat = sb("ctx_nat", [KC, B, D])
        ctxT = sb("ctxT", [P, B, KC])
        kT = sb("kT", [P, B, KC])
        kb = sb("kb", [P, B, heads, KC])
        vall = sb("vall", [KC, B, P])
        vpad = sb("vpad", [KC, heads, 32])
        zT, qT = sb("zT", [P, S]), sb("qT", [P, S])
        sc = [sb(f"sc{r}", [P, HALF, KC]) for r in range(2)]
        pr = [sb(f"pr{r}", [P, HALF, KC]) for r in range(RP)]
        mx = [sb(f"mx{r}", [P, HALF]) for r in range(2)]
        sm = [sb(f"sm{r}", [P, HALF]) for r in range(2)]
        rs = [sb(f"rs{r}", [P, HALF]) for r in range(2)]
        pT = [sb(f"pT{r}", [KC, HALF, P]) for r in range(2)]
        oT = [sb(f"oT{r}", [P, 2, P]) for r in range(2)]
        cmask = sb("cmask", [P, KC])
        if mask is not None:
            mraw = sb("mraw", [P, TT, KC], I32)
            drop = sb("drop", [P, TT, KC])

        names = ("loaded zeroed wT wT_out ctxTr ctxT_out kv_done kv_out zTr zT_out q_done q_out vpad_done score "
                 "scored exp_done inverted normed ptr pt_evac pv o_evac y_done batch_done step woz wo_out consts y_used")
        s = {n: sem(n) for n in names.split()}
        ps = k.ps
        diag = weights[0].shape[0] == hd
        n_loads = 0

        with nc.Block() as block:
            loads = []
            if diag:
                for j in range(3):
                    for h in range(heads):
                        rows = slice(h * hd, (h + 1) * hd)
                        loads.append((w_nat[rows, j, rows], weights[j]))
            else:
                for j in range(3):
                    loads.append((w_nat[:, j, :], weights[j]))
            loads.append((w_nat[:, 3, :], weights[3]))
            loads.append((ctx_nat[:], d["ctx_1024"].rearrange("b k d -> k b d")))
            if biases is not None:
                for j in range(2):
                    loads.append((bcol[:, j:j + 1], biases[j].rearrange("(p a) -> p a", a=1)))
                loads.append((brow[:, 0, :], biases[2].partition_broadcast(P)))
            loads.append((brow[:, 1, :], out_bias.partition_broadcast(P)))
            if mask is not None:
                loads.append((mraw[:], mask.rearrange("b a (t p) k -> p (b a t) k", p=P)))

            @block.sync
            def _(sp):
                sp.wait_ge(s["zeroed"], 1)
                for dst, src in loads:
                    sp.dma_start(dst, src).then_inc(s["loaded"], 16)
                sp.wait_ge(s["loaded"], 16 * len(loads))

            @block.gpsimd
            def _(pool):
                layernorm_pool(k, pool)
                pool.memset(vpad[:], 0.0)
                if biases is None:
                    pool.memset(bcol[:], 0.0)
                    pool.memset(brow[:, 0, :], 0.0)
                pool.memset(w_nat[:], 0.0).then_inc(s["zeroed"], 1)
                pool.memset(woT[:], 1.0)
                pool.memset(cmask[:], 0.0)
                pool.memset(head_mask[:], 1.0).then_inc(s["consts"], 1)
                pool.wait_ge(s["consts"], 1)
                pool.affine_select(out=head_mask[:], in_=head_mask[:], compare_op=ALU.is_ge, fill=0.0, base=0,
                                   pattern=[[-hd, heads]], channel_multiplier=1).then_inc(s["consts"], 1)
                pool.wait_ge(s["consts"], 2)
                pool.affine_select(out=head_mask[:], in_=head_mask[:], compare_op=ALU.is_ge, fill=0.0, base=hd - 1,
                                   pattern=[[hd, heads]], channel_multiplier=-1).then_inc(s["consts"], 1)
                pool.affine_select(out=cmask[:], in_=cmask[:], compare_op=ALU.is_ge, fill=NEG, base=0,
                                   pattern=[[-1, KC]], channel_multiplier=1).then_inc(s["consts"], 1)
                pool.wait_ge(s["consts"], 4)

            @block.tensor
            def _(pe):
                pe.wait_ge(s["loaded"], 16 * len(loads))
                for j in range(3):
                    last = pe.transpose(ps[:, 0, j * P:(j + 1) * P], w_nat[:, j, :], k.ident[:])
                last.then_inc(s["wT"], 1)
                for g in range(G):
                    for j in range(4):
                        h = 4 * g + j
                        last = pe.transpose(ps[0:hd, 1 + g, j * P:(j + 1) * P],
                                            w_nat[:, 3, h * hd:(h + 1) * hd], k.ident[:])
                last.then_inc(s["wT"], 1)
                for b in range(B):
                    last = pe.transpose(ps[:, 6, b * KC:(b + 1) * KC], ctx_nat[:, b, :], k.ident[0:KC, 0:KC])
                last.then_inc(s["ctxTr"], 1)
                pe.wait_ge(s["ctxT_out"], 1)
                pe.wait_ge(s["wT_out"], 1)
                pe.matmul(ps[:, 7, 0:B * KC], wt[:, 1, :], ctxT[:].rearrange("p b k -> p (b k)"), start=True,
                          stop=True).then_inc(s["kv_done"], 1)
                for b in range(B):
                    last = pe.matmul(ps[0:KC, 0, b * P:(b + 1) * P], ctxT[:, b, :], wt[:, 2, :], start=True, stop=True)
                last.then_inc(s["kv_done"], 1)

            @block.scalar
            def _(act):
                act.wait_ge(s["wT"], 1)
                act.activation(wt[:].rearrange("p j d -> p (j d)"), ps[:, 0, 0:3 * P], ACT.Copy).then_inc(s["wT_out"], 1)
                act.wait_ge(s["kv_done"], 1)
                act.activation(kT[:].rearrange("p b k -> p (b k)"), ps[:, 7, 0:B * KC], ACT.Identity,
                               bias=bcol[:, 1:2]).then_inc(s["kv_out"], 1)

            @block.vector
            def _(v):
                layernorm_vector(k, v, k.x)
                v.memset(wo[:], 0.0).then_inc(s["woz"], 1)
                v.wait_ge(s["woz"], 1)
                v.wait_ge(s["wT"], 2)
                for h in range(heads):
                    last = v.tensor_copy(wo[32 * (h % 4):32 * (h % 4) + hd, h // 4, :], ps[0:hd, 1 + h // 4, (h % 4) * P:(h % 4 + 1) * P])
                last.then_inc(s["wo_out"], 1)
                v.wait_ge(s["ctxTr"], 1)
                v.tensor_copy(ctxT[:].rearrange("p b k -> p (b k)"), ps[:, 6, 0:B * KC]).then_inc(s["ctxT_out"], 1)
                v.wait_ge(s["consts"], 4)
                v.wait_ge(s["kv_out"], 1)
                for b in range(B):
                    v.tensor_tensor(kb[:, b, :, :], kT[:, b, :].unsqueeze(1).to_broadcast([P, heads, KC]),
                                    head_mask[:].unsqueeze(2).to_broadcast([P, heads, KC]), ALU.mult)
                v.wait_ge(s["kv_done"], 2)
                v.tensor_tensor(vall[:], ps[0:KC, 0, :].rearrange("p (b d) -> p b d", d=P),
                                brow[0:KC, 0, :].unsqueeze(1).to_broadcast([KC, B, P]), ALU.add)
                if mask is not None:
                    v.tensor_scalar(drop[:], mraw[:], 0, -1.0e20, ALU.is_equal, ALU.mult)

        with nc.Block() as block:
            @block.gpsimd
            def _(pool):
                with pool.Fori(0, B) as b:
                    pool.wait_ge(s["batch_done"], b)
                    pool.tensor_copy(vpad[:, :, 0:hd], vall[:, b, :].rearrange("p (h e) -> p h e", e=hd)).then_inc(s["vpad_done"], 1)
                    for u in range(U):
                        pool.wait_ge(s["inverted"], b * U + u + 1)
                        pool.tensor_tensor(pr[u % RP][:], pr[u % RP][:], rs[u % 2][:].unsqueeze(2).to_broadcast([P, HALF, KC]),
                                           ALU.mult).then_inc(s["normed"], 1)

            @block.vector
            def _(v):
                with v.Fori(0, B) as b:
                    take_batch(k, v, b)
                    step = chain(v, s["step"], STEPS, b)

                    def soften(u):
                        i, half = u // U1, u % U1
                        v.wait_ge(s["score"], b * U + u + 1)
                        if u >= 2:
                            v.wait_ge(s["exp_done"], b * U + u - 1)
                        src = ps[:, 2 * (u % 2):2 * (u % 2) + 2, :].rearrange("p a (h n) -> p (a h) n", n=P)[:, :, 0:KC]
                        dst = sc[u % 2][:]
                        if mask is not None:
                            step(v.tensor_tensor(dst, src, drop[:, b * NT + i, :].unsqueeze(1).to_broadcast([P, HALF, KC]), ALU.add))
                            src = dst
                        elif causal and i == 0:
                            step(v.tensor_tensor(dst, src, cmask[:].unsqueeze(1).to_broadcast([P, HALF, KC]), ALU.add))
                            src = dst
                        step(v.tensor_reduce(mx[u % 2][:], src, AX, ALU.max))
                        v.tensor_tensor(dst, src, mx[u % 2][:].unsqueeze(2).to_broadcast([P, HALF, KC]),
                                        ALU.subtract).then_inc(s["scored"], 1)

                    def invert(u):
                        v.wait_ge(s["exp_done"], b * U + u + 1)
                        step(v.tensor_reduce(sm[u % 2][:], pr[u % RP][:], AX, ALU.add))
                        if u >= 2:
                            v.wait_ge(s["normed"], b * U + u - 1)
                        v.reciprocal(rs[u % 2][:], sm[u % 2][:]).then_inc(s["inverted"], 1)

                    def output(u):
                        v.wait_ge(s["pv"], b * U + u + 1)
                        if u >= 2:
                            v.wait_ge(s["y_done"], b * U + u - 1)
                        v.tensor_copy(oT[u % 2][:].rearrange("p g q -> p (g q)"), ps[:, 6, 0:2 * P]).then_inc(s["o_evac"], 1)

                    def residual(i):
                        v.wait_ge(s["y_done"], b * U + (i + 1) * U1)
                        v.tensor_tensor(k.x[:, b * NT + i, :], k.x[:, b * NT + i, :], ps[:, 7, 0:P], ALU.add).then_inc(s["y_used"], 1)
                        v.wait_ge(s["y_used"], b * NT + i + 1)
                        last = v.tensor_tensor(k.x[:, b * NT + i, :], k.x[:, b * NT + i, :], brow[:, 1, :], ALU.add)
                        if i < NT - 1:
                            step(last)
                        else:
                            last.then_inc(s["batch_done"], 1)

                    for w in range(U + 5):
                        if w >= 5 and (w - 5) % U1 == U1 - 1:
                            residual((w - 5) // U1)
                        if w < U:
                            soften(w)
                        if 1 <= w <= U:
                            invert(w - 1)
                        if 3 <= w < U + 3:
                            output(w - 3)
                    assert step.count[0] == STEPS, (step.count[0], STEPS)

            @block.scalar
            def _(act):
                with act.Fori(0, B) as b:
                    act.wait_ge(s["zTr"], b + 1)
                    act.activation(zT[:], k.bank(4), ACT.Copy).then_inc(s["zT_out"], 1)
                    act.wait_ge(s["q_done"], b + 1)
                    act.activation(qT[:], k.bank(5), ACT.Identity, bias=bcol[:, 0:1]).then_inc(s["q_out"], 1)

                    def exps(u):
                        act.wait_ge(s["scored"], b * U + u + 1)
                        if u >= RP:
                            act.wait_ge(s["ptr"], b * U + u - RP + 1)
                        act.activation(pr[u % RP][:], sc[u % 2][:], ACT.Exp, scale=scale).then_inc(s["exp_done"], 1)

                    def evacuate(u):
                        act.wait_ge(s["ptr"], b * U + u + 1)
                        if u >= 2:
                            act.wait_ge(s["pv"], b * U + u - 1)
                        act.activation(pT[u % 2][:].rearrange("p h q -> p (h q)"),
                                       ps[0:KC, 4:6, :].rearrange("p a n -> p (a n)"), ACT.Copy).then_inc(s["pt_evac"], 1)

                    for w in range(U + 2):
                        if w < U:
                            exps(w)
                        if w >= 2:
                            evacuate(w - 2)

            @block.tensor
            def _(pe):
                with pe.Fori(0, B) as b:
                    pe.wait_ge(s["batch_done"], b)
                    pe.wait_ge(k.zb_ready, k.n_batches + b + 1)
                    for t in range(NT):
                        last = pe.transpose(ps[:, 4, t * P:(t + 1) * P], k.zb[:, t, :], k.ident[:])
                    last.then_inc(s["zTr"], 1)
                    pe.wait_ge(s["zT_out"], b + 1)
                    pe.matmul(k.bank(5), wt[:, 0, :], zT[:], start=True, stop=True).then_inc(s["q_done"], 1)
                    pe.wait_ge(s["q_out"], b + 1)

                    def scores(u):
                        i, half = u // U1, u % U1
                        if u >= 2:
                            pe.wait_ge(s["scored"], b * U + u - 1)
                        for a in range(2):
                            h = half * HALF + 4 * a
                            last = pe.matmul(ps[:, 2 * (u % 2) + a, :].rearrange("p (h n) -> p h n", n=P)[:, :, 0:KC], qT[:, i * P:(i + 1) * P],
                                             kb[:, b, h:h + 4, :], start=True, stop=True)
                        last.then_inc(s["score"], 1)

                    def values(u):
                        i, half = u // U1, u % U1
                        pe.wait_ge(s["pt_evac"], b * U + u + 1)
                        if u == 0:
                            pe.wait_ge(s["vpad_done"], b + 1)
                        else:
                            pe.wait_ge(s["o_evac"], b * U + u)
                        for j in range(HALF):
                            last = pe.matmul(ps[32 * (j % 4):32 * (j % 4) + 32, 6, (j // 4) * P:(j // 4 + 1) * P],
                                             vpad[:, half * HALF + j, :], pT[u % 2][:, j, :], start=True, stop=True)
                        last.then_inc(s["pv"], 1)

                    def project(u):
                        i, half = u // U1, u % U1
                        pe.wait_ge(s["o_evac"], b * U + u + 1)
                        if half == 0 and i:
                            pe.wait_ge(s["y_used"], b * NT + i)
                        for g in range(2):
                            last = pe.matmul(ps[:, 7, 0:P], oT[u % 2][:, g, :], wo[:, half * 2 + g, :],
                                             start=(half == 0 and g == 0), stop=(half == U1 - 1 and g == 1))
                        last.then_inc(s["y_done"], 1)

                    def transpose_probs(u):
                        pe.wait_ge(s["normed"], b * U + u + 1)
                        if u:
                            pe.wait_ge(s["pt_evac"], b * U + u)
                        for j in range(HALF):
                            last = pe.transpose(ps[0:KC, 4 + j // 4, (j % 4) * P:(j % 4 + 1) * P], pr[u % RP][:, j, :], k.ident[:])
                        last.then_inc(s["ptr"], 1)

                    for w in range(U + 4):
                        if w < U:
                            scores(w)
                        if 3 <= w < U + 3:
                            values(w - 3)
                        if 2 <= w < U + 2:
                            transpose_probs(w - 2)
                        if w >= 4:
                            project(w - 4)
    k.n_ln += 1
    k.n_batches += B


def stage_cross_attention_0(k):
    d = k.dram
    cross_attention(k, "x0_", HC0, HDC0, [d["L0_xattn_W" + n] for n in "qkvo"], [d["L0_xattn_b" + n] for n in "qkv"],
                    d["L0_xattn_bo"], HDC0 ** -0.5, True, None)


def stage_cross_attention_1(k):
    d = k.dram
    cross_attention(k, "x1_", H1, HD1, [d["L1_xattn_W" + n] for n in "qkvo"], None,
                    d["L1_xattn_bo"], float(D) ** -0.5, False, d["mask_Bx1xSxS2_if1"])


def stage_experts_0(k):
    nc, d = k.nc, k.dram
    PAIRS = NE0 // 2
    GE = 40
    GROUPS = NE0 // GE
    ROWS = 3 * GE
    PER_IT = 4
    ITS = GE // 2 // PER_IT
    CH = B
    UNITS = PER_IT * CH
    LAG = 3
    R = 4
    AHEAD = LAG + 1
    RSTEPS = 13
    TAKEN = -3.0e38
    YB, HB, CB, TB = 0, 4, 6, 7

    with ExitStack() as ctx:
        def sb(name, shape, dt=F32):
            return k.sb(ctx, "f0_" + name, shape, dt)

        xh, xl = sb("xh", [P, B, S], F32R), sb("xl", [P, B, S], F32R)
        bh, bl = sb("bh", [P, S], F32R), sb("bl", [P, S], F32R)
        rw = sb("rw", [P, 2, P])
        rwh, rwl = sb("rwh", [P, NE0], F32R), sb("rwl", [P, NE0], F32R)
        ebias = sb("ebias", [P, NE0])
        wgs, wds = sb("wgs", [IN0, P]), sb("wds", [P, IN0])
        wgsh, wgsl = sb("wgsh", [P, IN0], F32R), sb("wgsl", [P, IN0], F32R)
        wdsT = sb("wdsT", [IN0, P])
        sel_f = sb("sel_f", [ROWS, GE // 2, 2, IN0])
        sel = sb("sel", [ROWS, GE // 2, P], BF16)
        ct = sb("ct", [ROWS, GROUPS, B * S], BF16)
        lg, prb, rep, comb, rest = (sb(n, [P, NT, NE0]) for n in ("lg", "prb", "rep", "comb", "rest"))
        top = sb("top", [P, NT, 8])
        tot, inv = sb("tot", [P, NT]), sb("inv", [P, NT])
        parts = sb("parts", [P, NT, GROUPS, 3, GE], BF16)
        gn = [sb(f"gn{r}", [P, 2, P]) for r in range(2)]
        dn = [sb(f"dn{r}", [P, 4, IN0]) for r in range(2)]
        wh = [sb(f"wh{r}", [P, 4, P], F32R) for r in range(2)]
        wl = [sb(f"wl{r}", [P, 4, P], F32R) for r in range(2)]
        act_h = [sb(f"act_h{r}", [P, S]) for r in range(R)]
        hid = [sb(f"hid{r}", [P, S]) for r in range(R)]
        hh = [sb(f"hh{r}", [P, S], F32R) for r in range(R)]
        hl = [sb(f"hl{r}", [P, S], F32R) for r in range(R)]
        yT = sb("yT", [P, B, S])
        names = ("loaded consts wT w_out step zTr bh_ready bl_ready logits sig_in sig ptr ct_out sh_h sh_act "
                 "w_ina w_inb wt_done wh_out wl_out h_done c_done act_done hid_done hh_done hl_done y_units y_out y_tok")
        s = {n: k.sem("f0_" + n) for n in names.split()}
        ps = k.ps

        with nc.Block() as block:
            @block.sync
            def _(sp):
                r = d["L0_ffn_router_w"]
                sp.dma_start(rw[:, 0, :], r[0:P, :]).then_inc(s["loaded"], 16)
                sp.dma_start(rw[0:NE0 - P, 1, :], r[P:NE0, :]).then_inc(s["loaded"], 16)
                sp.dma_start(ebias[:], d["L0_ffn_expert_bias"].partition_broadcast(P)).then_inc(s["loaded"], 16)
                sp.dma_start(wgs[:], d["L0_ffn_w_gate_shared"]).then_inc(s["loaded"], 16)
                sp.dma_start(wds[:], d["L0_ffn_w_down_shared"]).then_inc(s["loaded"], 16)
                sp.wait_ge(s["loaded"], 16 * 5)

            @block.gpsimd
            def _(pool):
                layernorm_pool(k, pool)
                pool.memset(sel_f[:].rearrange("p j h c -> p (j h c)"), 0.0).then_inc(s["consts"], 1)
                for part in range(3):
                    pool.wait_ge(s["consts"], part + 1)
                    pool.affine_select(out=sel_f[:].rearrange("p j h c -> p (j h) c"), in_=sel_f[:].rearrange("p j h c -> p (j h) c"),
                                       compare_op=ALU.not_equal, fill=1.0, base=-part * GE, pattern=[[-1, GE], [0, IN0]],
                                       channel_multiplier=1).then_inc(s["consts"], 1)

            @block.tensor
            def _(pe):
                pe.wait_ge(s["loaded"], 16 * 5)
                pe.transpose(ps[:, 0, 0:P], rw[:, 0, :], k.ident[:])
                pe.transpose(ps[:, 0, P:NE0], rw[0:NE0 - P, 1, :], k.ident[0:NE0 - P, 0:NE0 - P])
                pe.transpose(ps[:, 0, NE0:NE0 + IN0], wgs[:], k.ident[0:IN0, 0:IN0])
                pe.transpose(ps[0:IN0, 0, 256:256 + P], wds[:], k.ident[:]).then_inc(s["wT"], 1)

            @block.scalar
            def _(act):
                act.wait_ge(s["wT"], 1)
                act.activation(rwh[:], ps[:, 0, 0:NE0], ACT.Copy)
                act.activation(wgsh[:], ps[:, 0, NE0:NE0 + IN0], ACT.Copy)
                act.activation(wdsT[:], ps[0:IN0, 0, 256:256 + P], ACT.Copy).then_inc(s["w_out"], 1)
                act.wait_ge(s["consts"], 4)
                act.activation(sel[:].rearrange("p j c -> p (j c)"), sel_f[:].rearrange("p j h c -> p (j h c)"), ACT.Copy)

            @block.vector
            def _(v):
                layernorm_vector(k, v, k.x)
                v.wait_ge(s["w_out"], 1)
                v.tensor_tensor(rwl[:], ps[:, 0, 0:NE0], rwh[:].bitcast(F32), ALU.subtract)
                v.tensor_tensor(wgsl[:], ps[:, 0, NE0:NE0 + IN0], wgsh[:].bitcast(F32), ALU.subtract)

        with nc.Block() as block:
            @block.vector
            def _(v):
                with v.Fori(0, B) as b:
                    take_batch(k, v, b)
                    step = chain(v, s["step"], RSTEPS, b)
                    v.wait_ge(s["bh_ready"], b + 1)
                    v.tensor_tensor(bl[:], k.bank(TB), bh[:].bitcast(F32), ALU.subtract).then_inc(s["bl_ready"], 1)
                    v.tensor_copy(xh[:, b, :], bh[:].bitcast(F32))
                    v.wait_ge(s["bl_ready"], b + 1)
                    v.tensor_copy(xl[:, b, :], bl[:].bitcast(F32))
                    for t in range(NT):
                        v.wait_ge(s["logits"], b * NT + t + 1)
                        last = v.tensor_tensor(lg[:, t, :], ps[:, t, 0:NE0], ebias[:], ALU.add)
                    last.then_inc(s["sig_in"], 1)
                    v.wait_ge(s["sig_in"], b + 1)
                    k.settle(v)
                    for t in range(NT):
                        last = v.max(top[:, t, :], lg[:, t, :])
                    step(last, k)
                    for t in range(NT):
                        last = v.match_replace(rep[:, t, :], top[:, t, :], lg[:, t, :], TAKEN)
                    step(last)
                    v.wait_ge(s["sig"], b + 1)
                    step(v.scalar_tensor_tensor(comb[:], rep[:], TAKEN, prb[:], ALU.is_equal, ALU.mult))
                    step(v.tensor_reduce(tot[:], comb[:], AX, ALU.add))
                    step(v.tensor_scalar(tot[:], tot[:], 1e-9, None, ALU.add))
                    step(v.reciprocal(inv[:], tot[:]))
                    step(v.tensor_scalar(inv[:], inv[:], 2.5, None, ALU.mult))
                    step(v.tensor_tensor(comb[:], comb[:], inv[:].unsqueeze(2).to_broadcast([P, NT, NE0]), ALU.mult))
                    src = comb
                    for part in range(3):
                        dst = parts[:, :, :, part, :]
                        step(v.tensor_copy(dst, src[:].rearrange("p t (g e) -> p t g e", e=GE)))
                        if part < 2:
                            for t in range(NT):
                                last = v.tensor_tensor(rest[:, t, :].rearrange("p (g e) -> p g e", e=GE),
                                                       src[:, t, :].rearrange("p (g e) -> p g e", e=GE),
                                                       parts[:, t, :, part, :], ALU.subtract)
                            step(last)
                        src = rest
                    assert step.count[0] == RSTEPS, step.count[0]

            @block.scalar
            def _(act):
                with act.Fori(0, B) as b:
                    act.wait_ge(s["zTr"], b + 1)
                    act.activation(bh[:], k.bank(TB), ACT.Copy).then_inc(s["bh_ready"], 1)
                    act.wait_ge(s["sig_in"], b + 1)
                    act.activation(prb[:], lg[:], ACT.Sigmoid).then_inc(s["sig"], 1)
                    act.wait_ge(s["ptr"], b + 1)
                    for t in range(NT):
                        last = act.activation(ct[:, :, bass.ds(b * S + t * P, P)],
                                              ps[0:ROWS, HB, :].bitcast(BF16).rearrange("p (t g n) -> p t g n", t=2, n=P)[:, t, :, :]
                                              if t < 2 else
                                              ps[0:ROWS, HB + 1, :].bitcast(BF16).rearrange("p (t g n) -> p t g n", t=2, n=P)[:, t - 2, :, :],
                                              ACT.Copy)
                    last.then_inc(s["ct_out"], 1)

            @block.tensor
            def _(pe):
                with pe.Fori(0, B) as b:
                    pe.wait_ge(s["step"], b * RSTEPS)
                    pe.wait_ge(k.zb_ready, k.n_batches + b + 1)
                    for t in range(NT):
                        last = pe.transpose(ps[:, TB, t * P:(t + 1) * P], k.zb[:, t, :], k.ident[:])
                    last.then_inc(s["zTr"], 1)
                    pe.wait_ge(s["bl_ready"], b + 1)
                    for t in range(NT):
                        tok = slice(t * P, (t + 1) * P)
                        split_product(pe, ps[:, t, 0:NE0], (bh[:, tok], bl[:, tok]), (rwh[:], rwl[:])).then_inc(s["logits"], 1)
                    pe.wait_ge(s["step"], b * RSTEPS + RSTEPS)
                    pe.wait_ge(s["ct_out"], b)
                    for t in range(NT):
                        out = ps[0:ROWS, HB + t // 2, :].bitcast(BF16).rearrange("p (t g n) -> p t g n", t=2, n=P)
                        for g in range(GROUPS):
                            last = pe.transpose(out[:, t % 2, g, :], parts[:, t, g, :, :].rearrange("p a e -> p (a e)"), k.ident_bf[:])
                    last.then_inc(s["ptr"], 1)

        with nc.Block() as block:
            @block.tensor
            def _(pe):
                for c in range(CH):
                    if c >= 2:
                        pe.wait_ge(s["sh_act"], c - 1)
                    split_product(pe, ps[0:IN0, HB + c % 2, :], (wgsh[:], wgsl[:]), (xh[:, c, :], xl[:, c, :])).then_inc(s["sh_h"], 1)
                for c in range(CH):
                    pe.wait_ge(s["sh_act"], c + 1)
                    pe.matmul(k.bank(YB + c), wdsT[:], yT[0:IN0, c, :], start=True, stop=False, skip_group_check=True)

            @block.scalar
            def _(act):
                for c in range(CH):
                    act.wait_ge(s["sh_h"], c + 1)
                    act.activation(yT[0:IN0, c, :], ps[0:IN0, HB + c % 2, :], ACT.Silu).then_inc(s["sh_act"], 1)

        gate = d["L0_ffn_w_gate"].rearrange("(n q e) i h -> n (e i) q h", q=2, e=2)
        down = d["L0_ffn_w_down"].rearrange("(n e) h i -> n h e i", e=4)

        with nc.Block() as block:
            @block.sync
            def _(sp):
                def load(half, block, transposed):
                    if transposed is not None:
                        sp.wait_ge(s["wt_done"], transposed)
                    sp.dma_start(gn[half][:], gate[block]).then_inc(s["w_in" + "ab"[half]], 16)
                    sp.dma_start(dn[half][:], down[block]).then_inc(s["w_in" + "ab"[half]], 16)

                load(0, 0, None)
                with sp.Fori(0, GROUPS * ITS - 1) as n:
                    load(1, n * 2 + 1, n * 2)
                    load(0, n * 2 + 2, n * 2 + 1)
                n = GROUPS * ITS - 1
                load(1, n * 2 + 1, n * 2)
                load(0, 0, n * 2 + 1)

            @block.tensor
            def _(pe):
                def prepare(half, n):
                    pe.wait_ge(s["w_in" + "ab"[half]], (n + 1) * 32)
                    if not (isinstance(n, int) and half == 0):
                        pe.wait_ge(s["wl_out"], n * 2 + half)
                    for q in range(2):
                        pe.transpose(ps[:, TB, q * P:(q + 1) * P], gn[half][:, q, :], k.ident[:])
                    for q in range(2):
                        last = pe.transpose(ps[:, TB, (2 + q) * P:(3 + q) * P],
                                            dn[half][:, 2 * q:2 * q + 2, :].rearrange("p e i -> p (e i)"), k.ident[:])
                    last.then_inc(s["wt_done"], 1)

                prepare(0, 0)
                with pe.Fori(0, GROUPS) as g:
                    with pe.Fori(0, ITS) as it:
                        n = g * ITS + it

                        def hidden(w):
                            q, c = w // CH, w % CH
                            half = q // 2
                            if q % 2 == 0 and c == 0:
                                pe.wait_ge(s["wl_out"], n * 2 + half + 1)
                            if w >= 2:
                                pe.wait_ge(s["act_done"], n * UNITS + w - 1)
                            split_product(pe, k.bank(HB + w % 2), (wh[half][:, q % 2, :], wl[half][:, q % 2, :]),
                                          (xh[:, c, :], xl[:, c, :])).then_inc(s["h_done"], 1)
                            if w:
                                pe.wait_ge(s["hid_done"], n * UNITS + w)
                            pe.matmul(k.bank(CB), sel[:, it * PER_IT + q, :], ct[:, g, c * S:(c + 1) * S], start=True,
                                      stop=True).then_inc(s["c_done"], 1)

                        def output(w):
                            q, c = w // CH, w % CH
                            pe.wait_ge(s["hl_done"], n * UNITS + w + 1)
                            half, j = q // 2, 2 + q % 2
                            split_product(pe, k.bank(YB + c), (wh[half][:, j, :], wl[half][:, j, :]), (hh[w % R][:], hl[w % R][:]),
                                          start=False, stop=False, skip=True).then_inc(s["y_units"], 1)

                        for w in range(UNITS + LAG):
                            if w == AHEAD:
                                prepare(1, n)
                            elif w == UNITS // 2 + AHEAD:
                                prepare(0, n + 1)
                            if w < UNITS:
                                hidden(w)
                            if w >= LAG:
                                output(w - LAG)

            @block.scalar
            def _(act):
                def prepare(half, n):
                    act.wait_ge(s["wt_done"], n * 2 + half + 1)
                    act.activation(wh[half][:].rearrange("p q n -> p (q n)"), k.bank(TB), ACT.Copy).then_inc(s["wh_out"], 1)

                prepare(0, 0)
                with act.Fori(0, GROUPS) as g:
                    with act.Fori(0, ITS) as it:
                        n = g * ITS + it

                        def high(w):
                            act.wait_ge(s["hid_done"], n * UNITS + w + 1)
                            if w >= R:
                                act.wait_ge(s["y_units"], n * UNITS + w - R + 1)
                            act.activation(hh[w % R][:], hid[w % R][:], ACT.Copy).then_inc(s["hh_done"], 1)

                        for w in range(UNITS):
                            if w == AHEAD:
                                prepare(1, n)
                            elif w == UNITS // 2 + AHEAD:
                                prepare(0, n + 1)
                            act.wait_ge(s["h_done"], n * UNITS + w + 1)
                            if w >= R:
                                act.wait_ge(s["hid_done"], n * UNITS + w - R + 1)
                            act.activation(act_h[w % R][:], k.bank(HB + w % 2), ACT.Silu).then_inc(s["act_done"], 1)
                            if w:
                                high(w - 1)
                        high(UNITS - 1)

            @block.vector
            def _(v):
                def prepare(half, n):
                    v.wait_ge(s["wh_out"], n * 2 + half + 1)
                    v.tensor_tensor(wl[half][:].rearrange("p q n -> p (q n)"), k.bank(TB),
                                    wh[half][:].rearrange("p q n -> p (q n)").bitcast(F32), ALU.subtract).then_inc(s["wl_out"], 1)

                prepare(0, 0)
                with v.Fori(0, GROUPS) as g:
                    with v.Fori(0, ITS) as it:
                        n = g * ITS + it

                        def low(w):
                            v.wait_ge(s["hh_done"], n * UNITS + w + 1)
                            v.tensor_tensor(hl[w % R][:], hid[w % R][:], hh[w % R][:].bitcast(F32), ALU.subtract).then_inc(s["hl_done"], 1)

                        for w in range(UNITS):
                            if w == AHEAD:
                                prepare(1, n)
                            elif w == UNITS // 2 + AHEAD:
                                prepare(0, n + 1)
                            v.wait_ge(s["act_done"], n * UNITS + w + 1)
                            v.wait_ge(s["c_done"], n * UNITS + w + 1)
                            if w >= R:
                                v.wait_ge(s["hl_done"], n * UNITS + w - R + 1)
                            v.tensor_tensor(hid[w % R][:], act_h[w % R][:], k.bank(CB), ALU.mult).then_inc(s["hid_done"], 1)
                            if w:
                                low(w - 1)
                        low(UNITS - 1)

        residual_block(k, s, yT, YB)
    k.n_ln += 1
    k.n_batches += B


def residual_block(k, s, yT, YB):
    nc, ps = k.nc, k.ps
    with nc.Block() as block:
        @block.scalar
        def _(act):
            for c in range(B):
                act.activation(yT[:, c, :], k.bank(YB + c), ACT.Copy).then_inc(s["y_out"], 1)

        @block.tensor
        def _(pe):
            for c in range(B):
                pe.wait_ge(s["y_out"], c + 1)
                for t in range(NT):
                    last = pe.transpose(ps[:, YB + 4 + c, t * P:(t + 1) * P], yT[:, c, t * P:(t + 1) * P], k.ident[:])
                last.then_inc(s["y_tok"], 1)

        @block.vector
        def _(v):
            for c in range(B):
                v.wait_ge(s["y_tok"], c + 1)
                v.tensor_tensor(k.x[:, c * NT:(c + 1) * NT, :], k.x[:, c * NT:(c + 1) * NT, :],
                                k.bank(YB + 4 + c).rearrange("p (t n) -> p t n", n=P), ALU.add)


def stage_attention_1(k):
    nc, d = k.nc, k.dram
    G = H1 // 4
    AHEAD = 2
    OFF = [0, 4 * P, 7 * P, 9 * P, 10 * P]
    EVAC = [(OFF[0], OFF[1]), (OFF[1], OFF[2]), (OFF[2], OFF[4])]
    SB, PB, OB, TB = 0, 4, 6, 7

    with ExitStack() as ctx:
        def sb(name, shape, dt=F32):
            return k.sb(ctx, "a1_" + name, shape, dt)

        wqkv = sb("wqkv", [P, 3 * P])
        wstack = [sb(f"wstack{n}", [P, G, 4, 4, HD1]) for n in "qk"]
        wo_nat = sb("wo_nat", [HD1, H1, P])
        wo = sb("wo", [P, G, P])
        brow = sb("brow", [P, P])
        row = sb("row", [P, 1], I32)
        sel_i = [sb(f"sel_i{n}", [P, 1], I32) for n in range(2)]
        sel = [sb(f"sel{n}", [P, 1]) for n in range(2)]
        mask = sb("mask", [P, S])
        zT = sb("zT", [P, S])
        vpad = sb("vpad", [P, NT, H1, 32])
        qhi, khi = sb("qhi", [P, S], F32R), sb("khi", [P, S], F32R)
        qz = [[sb(f"qz{r}{j}", [P, S], F32R) for j in range(4)] for r in range(2)]
        ks = [sb(f"ks{r}", [P, S], F32R) for r in range(2)]
        sc = [sb(f"sc{r}", [P, S]) for r in range(4)]
        nmax = sb("nmax", [P, 3, NT])
        sums = sb("sums", [P, 3, NT])
        rsum = sb("rsum", [P, 3, NT])
        prob = sb("prob", [P, 3, NT, S])
        pt = [[sb(f"pt{r}{j}", [P, OFF[4]]) for j in range(4)] for r in range(2)]
        oT = sb("oT", [P, G, S])
        names = ("loaded consts sel wo_zero zTr zT_out q_done k_done qhi_ready khi_ready qk_ready v_done "
                 "v_out score tile_scored exp_done rs_ready prob_ready ptr pt_a pt_v pv o_out y_done y_used batch_done")
        s = {n: k.sem("a1_" + n) for n in names.split()}
        ps = k.ps

        def keys(i):
            return (i + 1) * P

        with nc.Block() as block:
            @block.sync
            def _(sp):
                sp.dma_start(wqkv[:], d["L1_attn_w_qkv"]).then_inc(s["loaded"], 16)
                sp.dma_start(brow[:], d["L1_attn_b_out"].partition_broadcast(P)).then_inc(s["loaded"], 16)
                sp.wait_ge(s["wo_zero"], 1)
                wo_d = d["L1_attn_w_out"].rearrange("(g j e) n -> j e g n", j=4, e=HD1)
                for j in range(4):
                    sp.dma_start(wo[32 * j:32 * j + HD1, :, :], wo_d[j]).then_inc(s["loaded"], 16)
                sp.wait_ge(s["loaded"], 16 * 6)

            @block.gpsimd
            def _(pool):
                layernorm_pool(k, pool)
                pool.memset(vpad[:].rearrange("p t h e -> p (t h e)"), 0.0)
                pool.memset(wo[:], 0.0).then_inc(s["wo_zero"], 1)
                for r in range(2):
                    for j in range(4):
                        pool.memset(qz[r][j][:].bitcast(F32), 0.0)
                pool.iota(row[:], [[0, 1]], base=0, channel_multiplier=1).then_inc(s["consts"], 1)
                pool.memset(mask[:], 0.0).then_inc(s["consts"], 1)
                pool.wait_ge(s["consts"], 2)
                pool.affine_select(out=mask[:], in_=mask[:], compare_op=ALU.is_ge, fill=-1.0e10, base=S - P,
                                   pattern=[[-1, S]], channel_multiplier=1)

            @block.vector
            def _(v):
                layernorm_vector(k, v, k.x)
                v.wait_ge(s["consts"], 1)
                for n, shift in enumerate((3, 4)):
                    v.tensor_scalar(sel_i[n][:], row[:], shift, 1, ALU.logical_shift_right, ALU.bitwise_and).then_inc(s["sel"], 1)
                v.wait_ge(s["sel"], 2)
                for n in range(2):
                    v.tensor_scalar(sel[n][:], sel_i[n][:], -1.0, None, ALU.mult)
                v.wait_ge(s["loaded"], 16 * 6)
                for n, scale in ((0, HD1 ** -0.5), (1, 1.0)):
                    src = wqkv[:, n * P:(n + 1) * P].rearrange("p (h e) -> p h e", e=HD1)
                    dst = wstack[n][:].rearrange("p g j c e -> p (g j) c e")
                    for c in range(4):
                        v.tensor_scalar(dst[:, :, c, :], src, scale, None, ALU.mult)

        with nc.Block() as block:
            @block.vector
            def _(v):
                with v.Fori(0, B) as b:
                    take_batch(k, v, b)

                    def prepare(g):
                        r, n = g % 2, b * G + g + 1
                        v.wait_ge(s["qhi_ready"], n)
                        for j in range(4):
                            rows = slice(32 * j, 32 * j + 32)
                            last = v.scalar_tensor_tensor(qz[r][j][rows, :], qhi[rows, :].bitcast(F32), sel[0][rows, 0:1],
                                                          ps[rows, TB, :], ALU.mult, ALU.add)
                        last.then_inc(s["qk_ready"], 1)
                        v.wait_ge(s["khi_ready"], n)
                        v.scalar_tensor_tensor(ks[r][:], khi[:].bitcast(F32), sel[1][:, 0:1], ps[:, TB, :], ALU.mult,
                                               ALU.add).then_inc(s["qk_ready"], 1)

                    def score(h, i):
                        u = h * NT + i
                        v.wait_ge(s["score"], b * H1 * NT + u + 1)
                        if u >= 4:
                            v.wait_ge(s["exp_done"], b * H1 * NT + u - 3)
                        k.settle(v)
                        v.tensor_tensor_reduce(sc[u % 4][:, 0:keys(i)], ps[:, SB + u % 4, 0:keys(i)],
                                               mask[:, S - P - i * P:S], -1.0, 3.0e38, ALU.add, ALU.min,
                                               nmax[:, h % 3, i:i + 1]).then_inc(s["tile_scored"], 1)

                    def invert(h):
                        v.wait_ge(s["exp_done"], b * H1 * NT + h * NT + NT)
                        v.reciprocal(rsum[:, h % 3, :], sums[:, h % 3, :]).then_inc(s["rs_ready"], 1)

                    def evacuate(h):
                        r, j = h // 4 % 2, h % 4
                        v.wait_ge(s["ptr"], b * H1 * 3 + 3 * h + 3)
                        if h >= 8:
                            v.wait_ge(s["pv"], b * G + h // 4 - 1)
                        lo, hi = EVAC[2]
                        v.tensor_copy(pt[r][j][:, lo:hi], ps[:, PB + (3 * h + 2) % 2, 0:hi - lo]).then_inc(s["pt_v"], 1)

                    prepare(0)
                    for h in range(AHEAD):
                        for i in range(NT):
                            score(h, i)
                    invert(0)
                    for h in range(H1):
                        if h % 4 == 0 and h // 4 + 1 < G:
                            prepare(h // 4 + 1)
                        for i in range(NT):
                            if h + AHEAD < H1:
                                score(h + AHEAD, i)
                            if i == 1 and h + 1 < H1:
                                invert(h + 1)
                            if i == 3:
                                evacuate(h)
                    for t in range(NT):
                        v.wait_ge(s["y_done"], b * NT + t + 1)
                        v.tensor_tensor(k.x[:, b * NT + t, :], k.x[:, b * NT + t, :], ps[:, TB, t * P:(t + 1) * P],
                                        ALU.add).then_inc(s["y_used"], 1)
                    v.wait_ge(s["y_used"], b * NT + NT)
                    v.tensor_tensor(k.x[:, bass.ds(b * NT, NT), :], k.x[:, bass.ds(b * NT, NT), :],
                                    brow[:].unsqueeze(1).to_broadcast([P, NT, P]), ALU.add).then_inc(s["batch_done"], 1)
                    v.wait_ge(s["batch_done"], b + 1)

            @block.gpsimd
            def _(pool):
                with pool.Fori(0, B) as b:
                    for h in range(H1):
                        pool.wait_ge(s["rs_ready"], b * H1 + h + 1)
                        k.settle(pool)
                        for i in range(NT):
                            last = pool.tensor_scalar(prob[:, h % 3, i, 0:keys(i)], prob[:, h % 3, i, 0:keys(i)],
                                                      rsum[:, h % 3, i:i + 1], 0.0, ALU.mult, ALU.add)
                        last.then_inc(s["prob_ready"], 1)

            @block.scalar
            def _(act):
                with act.Fori(0, B) as b:
                    act.wait_ge(s["zTr"], b + 1)
                    act.activation(zT[:], k.bank(OB), ACT.Copy).then_inc(s["zT_out"], 1)

                    def prepare(g):
                        n = b * G + g + 1
                        act.wait_ge(s["q_done"], n)
                        act.activation(qhi[:], ps[:, TB, :], ACT.Copy).then_inc(s["qhi_ready"], 1)
                        act.wait_ge(s["k_done"], n)
                        act.activation(khi[:], ps[:, TB, :], ACT.Copy).then_inc(s["khi_ready"], 1)

                    def exp(h, i):
                        u = h * NT + i
                        act.wait_ge(s["tile_scored"], b * H1 * NT + u + 1)
                        if i == 0 and h >= 3:
                            act.wait_ge(s["ptr"], b * H1 * 3 + 3 * (h - 2))
                        act.activation(prob[:, h % 3, i, 0:keys(i)], sc[u % 4][:, 0:keys(i)], ACT.Exp, scale=-1.0,
                                       bias=nmax[:, h % 3, i:i + 1], accum_out=sums[:, h % 3, i:i + 1]).then_inc(s["exp_done"], 1)

                    def evacuate(h, n):
                        r, j = h // 4 % 2, h % 4
                        act.wait_ge(s["ptr"], b * H1 * 3 + 3 * h + n + 1)
                        if h >= 8 and n == 0:
                            act.wait_ge(s["pv"], b * G + h // 4 - 1)
                        lo, hi = EVAC[n]
                        act.activation(pt[r][j][:, lo:hi], ps[:, PB + (3 * h + n) % 2, 0:hi - lo], ACT.Copy).then_inc(s["pt_a"], 1)

                    def output(g):
                        act.wait_ge(s["pv"], b * G + g + 1)
                        act.activation(oT[:, g, :], k.bank(OB), ACT.Copy).then_inc(s["o_out"], 1)

                    act.wait_ge(s["v_done"], b + 1)
                    act.activation(vpad[:, :, :, 0:HD1],
                                   k.bank(PB).rearrange("p (t h e) -> p t h e", h=H1, e=HD1), ACT.Copy).then_inc(s["v_out"], 1)
                    prepare(0)
                    for h in range(AHEAD):
                        for i in range(NT):
                            exp(h, i)
                    for h in range(H1):
                        if h % 4 == 0 and h // 4 + 1 < G:
                            prepare(h // 4 + 1)
                        for i in range(NT):
                            if i % 2 == 0:
                                evacuate(h, i // 2)
                            if h + AHEAD < H1:
                                exp(h + AHEAD, i)
                        if h % 4 == 0 and h:
                            output(h // 4 - 1)
                    output(G - 1)

            @block.tensor
            def _(pe):
                with pe.Fori(0, B) as b:
                    pe.wait_ge(s["batch_done"], b)
                    pe.wait_ge(k.zb_ready, k.n_batches + b + 1)
                    for t in range(NT):
                        last = pe.transpose(ps[:, OB, t * P:(t + 1) * P], k.zb[:, t, :], k.ident[:])
                    last.then_inc(s["zTr"], 1)
                    pe.wait_ge(s["zT_out"], b + 1)
                    for t in range(NT):
                        last = pe.matmul(ps[:, PB, t * P:(t + 1) * P], zT[:, t * P:(t + 1) * P], wqkv[:, 2 * P:3 * P],
                                         start=True, stop=True)
                    last.then_inc(s["v_done"], 1)

                    def prepare(g):
                        if g:
                            pe.wait_ge(s["qk_ready"], b * 2 * G + 2 * g)
                        for n, done in ((0, "q_done"), (1, "k_done")):
                            if n:
                                pe.wait_ge(s["qk_ready"], b * 2 * G + 2 * g + 1)
                            pe.matmul(ps[:, TB, :], wstack[n][:, g, :, :, :].rearrange("p j c e -> p (j c e)"), zT[:],
                                      start=True, stop=True).then_inc(s[done], 1)

                    def score(h, i):
                        r, j, u = h // 4 % 2, h % 4, h * NT + i
                        if i == 0 and j == 0:
                            pe.wait_ge(s["qk_ready"], b * 2 * G + 2 * (h // 4) + 2)
                        if u >= 4:
                            pe.wait_ge(s["tile_scored"], b * H1 * NT + u - 3)
                        pe.matmul(ps[:, SB + u % 4, 0:keys(i)], qz[r][j][:, i * P:(i + 1) * P], ks[r][:, 0:keys(i)],
                                  start=True, stop=True).then_inc(s["score"], 1)

                    def transpose_probs(h, n):
                        if n == 0 and h:
                            pe.wait_ge(s["pt_a"], b * 2 * H1 + 2 * h)
                        elif n == 1 and h:
                            pe.wait_ge(s["pt_v"], b * H1 + h)
                        elif n == 2:
                            pe.wait_ge(s["pt_a"], b * 2 * H1 + 2 * h + 1)
                        if n == 0:
                            pe.wait_ge(s["prob_ready"], b * H1 + h + 1)
                        at = 0
                        for kt in ((0,), (1,), (2, 3))[n]:
                            for i in range(kt, NT):
                                last = pe.transpose(ps[:, PB + (3 * h + n) % 2, at:at + P],
                                                    prob[:, h % 3, i, kt * P:(kt + 1) * P], k.ident[:])
                                at += P
                        last.then_inc(s["ptr"], 1)

                    def values(g):
                        r = g % 2
                        if g:
                            pe.wait_ge(s["o_out"], b * G + g)
                        pe.wait_ge(s["pt_a"], b * 2 * H1 + 2 * (4 * g + 4))
                        pe.wait_ge(s["pt_v"], b * H1 + 4 * g + 4)
                        for kt in range(NT):
                            for j in range(4):
                                last = pe.matmul(ps[32 * j:32 * j + 32, OB, kt * P:S], vpad[:, kt, 4 * g + j, :],
                                                 pt[r][j][:, OFF[kt]:OFF[kt + 1]], start=(kt == 0), stop=(kt == NT - 1))
                        last.then_inc(s["pv"], 1)

                    prepare(0)
                    for h in range(AHEAD):
                        for i in range(NT):
                            score(h, i)
                    pe.wait_ge(s["v_out"], b + 1)
                    for h in range(H1):
                        if h % 4 == 0 and h // 4 + 1 < G:
                            prepare(h // 4 + 1)
                        for i in range(NT):
                            if h + AHEAD < H1:
                                score(h + AHEAD, i)
                            if i < 2:
                                transpose_probs(h, i)
                        transpose_probs(h, 2)
                        if h % 4 == 0 and h:
                            values(h // 4 - 1)
                    values(G - 1)
                    pe.wait_ge(s["o_out"], b * G + G)
                    for t in range(NT):
                        if t:
                            pe.wait_ge(s["y_used"], b * NT + t)
                        for g in range(G):
                            last = pe.matmul(ps[:, TB, t * P:(t + 1) * P], oT[:, g, t * P:(t + 1) * P], wo[:, g, :],
                                             start=(g == 0), stop=(g == G - 1))
                        last.then_inc(s["y_done"], 1)
    k.n_ln += 1
    k.n_batches += B


def stage_experts_1(k):
    nc, d = k.nc, k.dram
    ROWS = 3 * NE1
    FB = FF1 // P
    EXPERTS = 2
    ITS = NE1 // EXPERTS
    CH = B
    E_UNITS = CH * FB
    UNITS = EXPERTS * E_UNITS
    CHUNKS = EXPERTS * CH
    MID = 4
    LAG = 3
    R = 4
    RSTEPS = 23
    YB, GB, VB, CB, TB = 0, 4, 5, 6, 7
    ALPHA, LIMIT = 1.702, 9.0

    with ExitStack() as ctx:
        def sb(name, shape, dt=F32):
            return k.sb(ctx, "f1_" + name, shape, dt)

        xh, xl = sb("xh", [P, B, S], F32R), sb("xl", [P, B, S], F32R)
        bh, bl = sb("bh", [P, S], F32R), sb("bl", [P, S], F32R)
        gw = sb("gw", [P, NE1])
        gwh, gwl = sb("gwh", [P, NE1], F32R), sb("gwl", [P, NE1], F32R)
        b1n = sb("b1n", [NE1 * FB, 2 * P])
        b1 = sb("b1", [P, 2, NE1 * FB])
        b2 = sb("b2", [NE1, P])
        order = sb("order", [P, NE1])
        sel_f = sb("sel_f", [ROWS, NE1, P])
        sel = sb("sel", [ROWS, NE1, P], BF16)
        ct = sb("ct", [ROWS, B * S], BF16)
        ct32 = sb("ct32", [NE1, B * S])
        g1, g2, eq, m1, m2, comb, scaled, rest = (sb(n, [P, NT, NE1]) for n in ("g1", "g2", "eq", "mask1", "mask2", "comb", "scaled", "rest"))
        top1, top2, best, ex, den, inv, second = (sb(n, [P, NT]) for n in ("top1", "top2", "best", "ex", "den", "inv", "second"))
        parts = sb("parts", [P, NT, 3, NE1], BF16)
        wn = [sb(f"wn{r}", [P, FB, 2, P]) for r in range(2)]
        dn = [sb(f"dn{r}", [P, FB, P]) for r in range(2)]
        wh = [sb(f"wh{r}", [P, FB, 2, P], F32R) for r in range(2)]
        wl = [sb(f"wl{r}", [P, FB, 2, P], F32R) for r in range(2)]
        dT = [sb(f"dT{r}", [P, FB, P]) for r in range(2)]
        gate, val, sg, hid, hidw = ([sb(f"{n}{r}", [P, S]) for r in range(R)] for n in ("gate", "val", "sg", "hid", "hidw"))
        ce = [sb(f"ce{r}", [P, S]) for r in range(2)]
        yT = sb("yT", [P, B, S])
        names = ("loaded consts b1T w_out step zTr bh_ready bl_ready logits exp_in exp_out ptr ct_out w_in wt_done dt_done "
                 "wh_out wl_out dt_out g_done v_done c_done g_out v_out c_out sig_out clipped h_done hid_done "
                 "y_units y_out y_tok")
        s = {n: k.sem("f1_" + n) for n in names.split()}
        ps = k.ps

        with nc.Block() as block:
            @block.sync
            def _(sp):
                sp.dma_start(gw[:], d["L1_ffn_gate_w"]).then_inc(s["loaded"], 16)
                sp.dma_start(b1n[:], d["L1_ffn_dense_1_b"].rearrange("e (a n) -> (e a) n", a=FB)).then_inc(s["loaded"], 16)
                sp.dma_start(b2[:], d["L1_ffn_dense_2_b"]).then_inc(s["loaded"], 16)
                sp.wait_ge(s["loaded"], 16 * 3)

            @block.gpsimd
            def _(pool):
                layernorm_pool(k, pool)
                for e in range(NE1):
                    pool.memset(order[:, e:e + 1], float(NE1 - e))
                pool.memset(sel_f[:].rearrange("p e c -> p (e c)"), 0.0).then_inc(s["consts"], 1)
                for part in range(3):
                    pool.wait_ge(s["consts"], part + 1)
                    pool.affine_select(out=sel_f[:], in_=sel_f[:], compare_op=ALU.not_equal, fill=1.0, base=-part * NE1,
                                       pattern=[[-1, NE1], [0, P]], channel_multiplier=1).then_inc(s["consts"], 1)
                pool.wait_ge(s["consts"], 4)
                pool.tensor_copy(sel[:].rearrange("p e c -> p (e c)"), sel_f[:].rearrange("p e c -> p (e c)"))

            @block.tensor
            def _(pe):
                pe.wait_ge(s["loaded"], 16 * 3)
                for gv in range(2):
                    last = pe.transpose(ps[:, 0, gv * NE1 * FB:(gv + 1) * NE1 * FB],
                                        b1n[:].rearrange("e (p g) -> e g p", g=2)[:, gv, :], k.ident[0:NE1 * FB, 0:NE1 * FB])
                last.then_inc(s["b1T"], 1)

            @block.vector
            def _(v):
                layernorm_vector(k, v, k.x)
                v.wait_ge(s["loaded"], 16 * 3)
                v.tensor_copy(gwh[:], gw[:]).then_inc(s["w_out"], 1)
                v.wait_ge(s["w_out"], 1)
                v.tensor_tensor(gwl[:], gw[:], gwh[:].bitcast(F32), ALU.subtract)
                v.wait_ge(s["b1T"], 1)
                v.tensor_copy(b1[:].rearrange("p g n -> p (g n)"), ps[:, 0, 0:2 * NE1 * FB])

        with nc.Block() as block:
            @block.vector
            def _(v):
                with v.Fori(0, B) as b:
                    take_batch(k, v, b)
                    step = chain(v, s["step"], RSTEPS, b)
                    v.wait_ge(s["bh_ready"], b + 1)
                    v.tensor_tensor(bl[:], k.bank(TB), bh[:].bitcast(F32), ALU.subtract).then_inc(s["bl_ready"], 1)
                    v.tensor_copy(xh[:, b, :], bh[:].bitcast(F32))
                    v.wait_ge(s["bl_ready"], b + 1)
                    v.tensor_copy(xl[:, b, :], bl[:].bitcast(F32))

                    def wide(a):
                        return a[:].unsqueeze(2).to_broadcast([P, NT, NE1])

                    def best_of(gates, top, mask):
                        step(v.tensor_reduce(top[:], gates[:], AX, ALU.max))
                        step(v.tensor_tensor(eq[:], gates[:], wide(top), ALU.is_equal))
                        step(v.tensor_tensor(eq[:], eq[:], order[:].unsqueeze(1).to_broadcast([P, NT, NE1]), ALU.mult))
                        step(v.tensor_reduce(best[:], eq[:], AX, ALU.max))
                        step(v.tensor_tensor(mask[:], eq[:], wide(best), ALU.is_equal))

                    v.wait_ge(s["logits"], b + 1)
                    step(v.tensor_copy(g1[:], ps[:, 0:NT, 0:NE1]))
                    best_of(g1, top1, m1)
                    step(v.scalar_tensor_tensor(g2[:], m1[:], NEG, g1[:], ALU.mult, ALU.add))
                    best_of(g2, top2, m2)
                    v.tensor_tensor(ex[:], top2[:], top1[:], ALU.subtract).then_inc(s["exp_in"], 1)
                    v.wait_ge(s["exp_out"], b + 1)
                    step(v.tensor_scalar(inv[:], ex[:], 1.0, None, ALU.add))
                    step(v.reciprocal(den[:], inv[:]))
                    v.tensor_tensor(m1[:], m1[:], wide(den), ALU.mult)
                    step(v.tensor_tensor(second[:], ex[:], den[:], ALU.mult))
                    step(v.tensor_tensor(m2[:], m2[:], wide(second), ALU.mult))
                    step(v.tensor_tensor(comb[:], m1[:], m2[:], ALU.add))
                    step(v.tensor_scalar(scaled[:], comb[:], 1.0 / ALPHA, None, ALU.mult))
                    step(v.tensor_copy(parts[:, :, 0, :], scaled[:]))
                    step(v.tensor_tensor(rest[:], scaled[:], parts[:, :, 0, :], ALU.subtract))
                    step(v.tensor_copy(parts[:, :, 1, :], rest[:]))
                    step(v.tensor_tensor(rest[:], rest[:], parts[:, :, 1, :], ALU.subtract))
                    step(v.tensor_copy(parts[:, :, 2, :], rest[:]))
                    assert step.count[0] == RSTEPS, step.count[0]

            @block.scalar
            def _(act):
                with act.Fori(0, B) as b:
                    act.wait_ge(s["zTr"], b + 1)
                    act.activation(bh[:], k.bank(TB), ACT.Copy).then_inc(s["bh_ready"], 1)
                    act.wait_ge(s["exp_in"], b + 1)
                    act.activation(ex[:], ex[:], ACT.Exp).then_inc(s["exp_out"], 1)
                    act.wait_ge(s["ptr"], b + 1)
                    act.activation(ct[:, bass.ds(b * S, S)], ps[0:ROWS, CB, 0:S // 2].bitcast(BF16), ACT.Copy)
                    act.activation(ct32[:, bass.ds(b * S, S)], ps[0:NE1, VB, :], ACT.Copy).then_inc(s["ct_out"], 1)

            @block.tensor
            def _(pe):
                with pe.Fori(0, B) as b:
                    pe.wait_ge(s["step"], b * RSTEPS)
                    pe.wait_ge(k.zb_ready, k.n_batches + b + 1)
                    for t in range(NT):
                        last = pe.transpose(ps[:, TB, t * P:(t + 1) * P], k.zb[:, t, :], k.ident[:])
                    last.then_inc(s["zTr"], 1)
                    pe.wait_ge(s["bl_ready"], b + 1)
                    for t in range(NT):
                        tok = slice(t * P, (t + 1) * P)
                        last = split_product(pe, ps[:, t, 0:NE1], (bh[:, tok], bl[:, tok]), (gwh[:], gwl[:]))
                    last.then_inc(s["logits"], 1)
                    pe.wait_ge(s["step"], b * RSTEPS + RSTEPS)
                    pe.wait_ge(s["ct_out"], b)
                    for t in range(NT):
                        tok = slice(t * P, (t + 1) * P)
                        pe.transpose(ps[0:ROWS, CB, 0:S // 2].bitcast(BF16)[:, tok], parts[:, t, :, :].rearrange("p a e -> p (a e)"), k.ident_bf[:])
                        last = pe.transpose(ps[0:NE1, VB, tok], comb[:, t, :], k.ident[:])
                    last.then_inc(s["ptr"], 1)

        first = d["L1_ffn_dense_1_w"].rearrange("e (f p g) i -> e p f g i", p=P, g=2)
        down = d["L1_ffn_dense_2_w"].rearrange("e i (f n) -> e i f n", n=P)

        with nc.Block() as block:
            @block.sync
            def _(sp):
                with sp.Fori(0, ITS) as it:
                    sp.wait_ge(s["dt_done"], it * EXPERTS)
                    for e in range(EXPERTS):
                        sp.dma_start(wn[e][:], first[it * EXPERTS + e]).then_inc(s["w_in"], 16)
                        sp.dma_start(dn[e][:], down[it * EXPERTS + e]).then_inc(s["w_in"], 16)

            @block.tensor
            def _(pe):
                for c in range(CH):
                    pe.matmul(k.bank(YB + c), b2[:], ct32[:, c * S:(c + 1) * S], start=True, stop=False, skip_group_check=True)
                with pe.Fori(0, ITS) as it:
                    def prepare(e, chunks):
                        pe.wait_ge(s["w_in"], (it + 1) * 32 * EXPERTS)
                        pe.wait_ge(s["wl_out"], it * EXPERTS + e)
                        pe.wait_ge(s["wh_out"], it * EXPERTS + e)
                        for j in range(2 * FB):
                            last = pe.transpose(ps[:, TB, j * P:(j + 1) * P], wn[e][:, j // 2, j % 2, :], k.ident[:])
                        last.then_inc(s["wt_done"], 1)
                        pe.wait_ge(s["c_out"], it * CHUNKS + chunks)
                        for f in range(FB):
                            last = pe.transpose(ps[:, CB, f * P:(f + 1) * P], dn[e][:, f, :], k.ident[:])
                        last.then_inc(s["dt_done"], 1)

                    def hidden(w):
                        e, c, f = w // E_UNITS, w % E_UNITS // FB, w % FB
                        if c == 0 and f == 0:
                            pe.wait_ge(s["wh_out"], it * EXPERTS + e + 1)
                            pe.wait_ge(s["wl_out"], it * EXPERTS + e + 1)
                            pe.wait_ge(s["dt_out"], it * EXPERTS + e + 1)
                        x = (xh[:, c, :], xl[:, c, :])
                        pe.wait_ge(s["g_out"], it * UNITS + w)
                        split_product(pe, k.bank(GB), (wh[e][:, f, 0, :], wl[e][:, f, 0, :]), x).then_inc(s["g_done"], 1)
                        pe.wait_ge(s["v_out"], it * UNITS + w)
                        split_product(pe, k.bank(VB), (wh[e][:, f, 1, :], wl[e][:, f, 1, :]), x).then_inc(s["v_done"], 1)
                        if f == 0:
                            pe.wait_ge(s["c_out"], it * CHUNKS + w // FB)
                            pe.wait_ge(s["dt_out"], it * EXPERTS + (1 if w < MID else 2))
                            k.settle(pe)
                            pe.matmul(k.bank(CB), sel[:, it * EXPERTS + e, :], ct[:, c * S:(c + 1) * S], start=True,
                                      stop=True).then_inc(s["c_done"], 1)

                    def output(w):
                        e, c, f = w // E_UNITS, w % E_UNITS // FB, w % FB
                        pe.wait_ge(s["hid_done"], it * UNITS + w + 1)
                        pe.matmul(k.bank(YB + c), dT[e][:, f, :], hidw[w % R][:], start=False, stop=False,
                                  skip_group_check=True).then_inc(s["y_units"], 1)

                    prepare(0, 0)
                    for w in range(UNITS + LAG):
                        if w == MID:
                            prepare(1, MID // FB)
                        if w < UNITS:
                            hidden(w)
                        if w >= LAG:
                            output(w - LAG)

            @block.scalar
            def _(act):
                with act.Fori(0, ITS) as it:
                    def prepare(e):
                        act.wait_ge(s["wt_done"], it * EXPERTS + e + 1)
                        act.activation(wh[e][:].rearrange("p f g n -> p (f g n)"), k.bank(TB), ACT.Copy).then_inc(s["wh_out"], 1)
                        act.wait_ge(s["dt_done"], it * EXPERTS + e + 1)
                        act.activation(dT[e][:].rearrange("p f n -> p (f n)"), ps[:, CB, 0:FB * P], ACT.Copy).then_inc(s["dt_out"], 1)

                    prepare(0)
                    for w in range(UNITS):
                        e, f = w // E_UNITS, w % FB
                        if w == MID:
                            prepare(1)
                        column = (it * EXPERTS + e) * FB + f
                        act.wait_ge(s["g_out"], it * UNITS + w + 1)
                        if w >= R:
                            act.wait_ge(s["h_done"], it * UNITS + w - R + 1)
                        act.activation(sg[w % R][:], gate[w % R][:], ACT.Silu, scale=ALPHA).then_inc(s["sig_out"], 1)
                        act.wait_ge(s["v_done"], it * UNITS + w + 1)
                        k.settle(act)
                        act.activation(val[w % R][:], k.bank(VB), ACT.Identity, bias=b1[:, 1, bass.ds(column, 1)]).then_inc(s["v_out"], 1)
                        if f == 0:
                            m = w // FB
                            act.wait_ge(s["c_done"], it * CHUNKS + m + 1)
                            if m >= 2:
                                act.wait_ge(s["hid_done"], it * UNITS + (m - 1) * FB)
                            act.activation(ce[m % 2][:], k.bank(CB), ACT.Copy).then_inc(s["c_out"], 1)

            @block.vector
            def _(v):
                with v.Fori(0, ITS) as it:
                    def prepare(e):
                        v.wait_ge(s["wh_out"], it * EXPERTS + e + 1)
                        v.tensor_tensor(wl[e][:].rearrange("p f g n -> p (f g n)"), k.bank(TB),
                                        wh[e][:].rearrange("p f g n -> p (f g n)").bitcast(F32), ALU.subtract).then_inc(s["wl_out"], 1)

                    def gates(w):
                        e, f = w // E_UNITS, w % FB
                        column = (it * EXPERTS + e) * FB + f
                        v.wait_ge(s["g_done"], it * UNITS + w + 1)
                        if w >= R:
                            v.wait_ge(s["sig_out"], it * UNITS + w - R + 1)
                        v.tensor_scalar(gate[w % R][:], k.bank(GB), b1[:, 0, bass.ds(column, 1)], LIMIT, ALU.add,
                                        ALU.min).then_inc(s["g_out"], 1)

                    def swiglu(w):
                        v.wait_ge(s["v_out"], it * UNITS + w + 1)
                        v.tensor_scalar(val[w % R][:], val[w % R][:], LIMIT, -LIMIT, ALU.min, ALU.max).then_inc(s["clipped"], 1)
                        v.wait_ge(s["clipped"], it * UNITS + w + 1)
                        v.wait_ge(s["sig_out"], it * UNITS + w + 1)
                        if w >= R:
                            v.wait_ge(s["hid_done"], it * UNITS + w - R + 1)
                        v.scalar_tensor_tensor(hid[w % R][:], val[w % R][:], 1.0, sg[w % R][:], ALU.add, ALU.mult).then_inc(s["h_done"], 1)

                    prepare(0)
                    for w in range(UNITS + 1):
                        if w == MID:
                            prepare(1)
                        if w < UNITS:
                            gates(w)
                        if w >= 1:
                            swiglu(w - 1)

            @block.gpsimd
            def _(pool):
                with pool.Fori(0, ITS) as it:
                    def weigh(w):
                        m = w // FB
                        pool.wait_ge(s["h_done"], it * UNITS + w + 1)
                        pool.wait_ge(s["c_out"], it * CHUNKS + m + 1)
                        if w >= R:
                            pool.wait_ge(s["y_units"], it * UNITS + w - R + 1)
                        pool.tensor_tensor(hidw[w % R][:], hid[w % R][:], ce[m % 2][:], ALU.mult).then_inc(s["hid_done"], 1)

                    for w in range(UNITS):
                        weigh(w)

        residual_block(k, s, yT, YB)
    k.n_ln += 1
    k.n_batches += B
STAGES = [stage_attention_0, stage_cross_attention_0, stage_experts_0, stage_attention_1, stage_cross_attention_1, stage_experts_1]


def build(nc, dram, out):
    with ExitStack() as ctx:
        k = Kernel(nc, ctx, dram, out)
        stage_setup(k)
        for stage in STAGES:
            stage(k)
            k.end_stage()
        stage_store(k)



_INS = (
    "x", "ctx_1024", "mask_Bx1xSxS2_if1", "L0_attn_gamma",
    "L0_attn_w_q", "L0_attn_w_kv", "L0_attn_null_kv", "L0_attn_q_scale",
    "L0_attn_k_scale", "L0_attn_w_out", "L0_xattn_Wq", "L0_xattn_bq",
    "L0_xattn_Wk", "L0_xattn_bk", "L0_xattn_Wv", "L0_xattn_bv",
    "L0_xattn_Wo", "L0_xattn_bo", "L0_ffn_router_w", "L0_ffn_expert_bias",
    "L0_ffn_w_gate", "L0_ffn_w_down", "L0_ffn_w_gate_shared", "L0_ffn_w_down_shared",
    "L1_attn_w_qkv", "L1_attn_w_out", "L1_attn_b_out", "L1_xattn_Wv",
    "L1_xattn_Wk", "L1_xattn_Wq", "L1_xattn_Wo", "L1_xattn_bo",
    "L1_ffn_gate_w", "L1_ffn_dense_1_w", "L1_ffn_dense_1_b", "L1_ffn_dense_2_w",
    "L1_ffn_dense_2_b",
)


def kernel(**inputs):
    import numpy as _np
    import concourse.bacc as _bacc
    from concourse import mybir as _mybir
    from concourse.bass_utils import run_bass_kernel_spmd as _run

    nc = _bacc.Bacc("TRN2", target_bir_lowering=False, num_devices=1)
    arrays, dram = {}, {}
    for name in _INS:
        a = _np.ascontiguousarray(inputs[name])
        arrays[f"in_{name}_dram"] = a
        dram[name] = nc.dram_tensor(f"in_{name}_dram", a.shape, _mybir.dt.from_np(a.dtype), kind="ExternalInput").ap()
    out = nc.dram_tensor("out_0_dram", (B, S, D), F32, kind="ExternalOutput").ap()
    build(nc, dram, out)
    r = _run(nc, [arrays], core_ids=[0])
    return r.results[0]["out_0_dram"]
```

```python
from contextlib import ExitStack
import math

import numpy as np

import concourse.bass as bass
from concourse import mybir

ALU = mybir.AluOpType
ACT = mybir.ActivationFunctionType
AX = mybir.AxisListType.X
F32 = mybir.dt.float32
F32R = mybir.dt.float32r
BF16 = mybir.dt.bfloat16
I32 = mybir.dt.int32

P = 128
B = 4
S = 512
D = 128
NT = S // P
TT = B * NT
KC = 77
EPS = 1e-5

H0, HD0 = 16, 64
HC0, HDC0 = 8, 16
H1, HD1 = 16, 8
NE0, IN0, TOP0 = 160, 64, 8
NE1, FF1 = 8, 256
NEG = -1.0e30


def alibi_slopes():
    start = 2.0 ** (-2.0 ** (-(math.log2(H0) - 3.0)))
    return [float(np.float32(start * start ** i)) for i in range(H0)]


class Kernel:

    def __init__(self, nc, ctx, dram, out):
        self.nc, self.ctx, self.dram, self.out = nc, ctx, dram, out
        self.sems = []
        sb = self.sb
        self.ps = ctx.enter_context(nc.psum_tensor("ps", [P, 8, 512], F32))
        self.x = sb(ctx, "x_resid", [P, TT, D])
        self.ident = sb(ctx, "ident", [P, P])
        self.ident_bf = sb(ctx, "ident_bf", [P, P], BF16)
        self.mhalf = sb(ctx, "mhalf", [P, NT])
        self.stats = sb(ctx, "ln_stats", [P, TT, 6])
        self.mv = sb(ctx, "ln_mean_var", [P, TT, 2])
        self.ve = sb(ctx, "ln_var_eps", [P, TT])
        self.rstd = sb(ctx, "ln_rstd", [P, TT])
        self.z = sb(ctx, "ln_out", [P, TT, D])
        self.zb = sb(ctx, "ln_batch", [P, 2 * NT, D])
        self.zb_ready = self.sem("zb_ready")
        self.n_batches = 0
        self.var_ready = self.sem("var_ready")
        self.rstd_ready = self.sem("rstd_ready")
        self.ln_step = self.sem("ln_step")
        self.z_ready = self.sem("z_ready")
        self.passed = self.sem("passed")
        self.n_ln = 0
        self.sems = []

    def sb(self, ctx, name, shape, dt=F32):
        return ctx.enter_context(self.nc.sbuf_tensor(name, shape, dt))

    def sem(self, name):
        self.sems.append(self.nc.alloc_semaphore(name=name))
        return self.sems[-1]

    def end_stage(self):
        self.nc.clear_and_free_semaphores(self.sems)
        self.nc.all_engine_barrier()
        self.sems = []

    def settle(self, engine):
        engine.sem_inc(self.passed, 1)

    def bank(self, b):
        return self.ps[:, b, :]


def split_product(pe, out, left, right, start=True, stop=True, skip=False):
    (lh, ll), (rh, rl) = left, right
    pe.matmul(out, lh, rh, start=start, stop=False, skip_group_check=skip)
    pe.matmul(out, ll, rh, start=False, stop=False, skip_group_check=skip)
    return pe.matmul(out, lh, rl, start=False, stop=stop, skip_group_check=skip)


def chain(engine, sem, per_pass=0, i=0):
    count = [0]

    def step(ins, k=None):
        count[0] += 1
        ins.then_inc(sem, 1)
        engine.wait_ge(sem, i * per_pass + count[0])
        if k:
            k.settle(engine)

    step.count = count
    return step


def layernorm_vector(k, v, src, n=0):
    n = k.n_ln + n
    step = chain(v, k.ln_step)
    step.count[0] = 2 * B * n

    def statistics(b):
        tiles = range(b * NT, (b + 1) * NT)
        for t in tiles:
            last = v.bn_stats(k.stats[:, t, :], src[:, t, :])
        step(last)
        for t in tiles:
            last = v.bn_aggr(k.mv[:, t, :], k.stats[:, t, :])
        step(last)
        v.tensor_scalar(k.ve[:, b * NT:(b + 1) * NT], k.mv[:, b * NT:(b + 1) * NT, 1], EPS, None, ALU.add).then_inc(k.var_ready, 1)

    def scale(b):
        v.wait_ge(k.rstd_ready, B * n + b + 1)
        for t in range(b * NT, (b + 1) * NT):
            last = v.tensor_scalar(k.z[:, t, :], src[:, t, :], k.mv[:, t, 0:1], k.rstd[:, t:t + 1], ALU.subtract, ALU.mult)
        last.then_inc(k.z_ready, 1)

    for b in range(B + 1):
        if b < B:
            statistics(b)
        if b:
            scale(b - 1)
    v.wait_ge(k.z_ready, B * (n + 1))


def take_batch(k, v, b, batches=1):
    tiles = batches * NT
    v.tensor_copy(k.zb[:, 0:tiles, :], k.z[:, bass.ds(b * tiles, tiles), :]).then_inc(k.zb_ready, 1)


def layernorm_pool(k, pool, n=0):
    for b in range(B):
        pool.wait_ge(k.var_ready, B * (k.n_ln + n) + b + 1)
        tiles = slice(b * NT, (b + 1) * NT)
        pool.tensor_tensor(k.rstd[:, tiles], k.ve[:, tiles], k.mhalf[:], ALU.pow).then_inc(k.rstd_ready, 1)


def stage_setup(k):
    nc, d = k.nc, k.dram
    made, x_in = k.sem("const_made"), k.sem("x_loaded")
    with nc.Block() as block:
        @block.sync
        def _(sp):
            sp.dma_start(k.x[:], d["x"].rearrange("b (t p) d -> p (b t) d", p=P)).then_inc(x_in, 16)
            sp.wait_ge(x_in, 16)

        @block.gpsimd
        def _(pool):
            pool.memset(k.mhalf[:], -0.5)
            pool.memset(k.ident[:], 1.0).then_inc(made, 1)
            pool.wait_ge(made, 1)
            pool.affine_select(out=k.ident[:], in_=k.ident[:], compare_op=ALU.is_equal, fill=0.0, base=0,
                               pattern=[[1, P]], channel_multiplier=-1).then_inc(made, 1)
            pool.wait_ge(made, 2)
            pool.tensor_copy(k.ident_bf[:], k.ident[:]).then_inc(made, 1)
            pool.wait_ge(made, 3)


def stage_store(k):
    nc = k.nc
    stored = k.sem("out_stored")
    with nc.Block() as block:
        @block.sync
        def _(sp):
            sp.dma_start(k.out.rearrange("b (t p) d -> p (b t) d", p=P), k.x[:]).then_inc(stored, 16)
            sp.wait_ge(stored, 16)
def stage_attention_0(k):
    nc, d = k.nc, k.dram
    PAIRS = H0 // 2
    NULLS = 2
    W = H0 * HD0
    NK = NULLS + S
    AHEAD = 2
    RP = 3
    STEPS = NT * 6
    slopes = alibi_slopes()

    def keys(i):
        return NULLS + (i + 1) * P

    with ExitStack() as ctx:
        def sb(name, shape, dt=F32):
            return k.sb(ctx, "a0_" + name, shape, dt)

        wqkv = [[sb(f"w{n}{part}", [P, W], F32R) for part in "hl"] for n in "qkv"]
        wo = [sb(f"wo_{part}", [P, PAIRS, D], F32R) for part in "hl"]
        gamma = sb("gamma", [P, 1])
        qs_col = sb("qs_col", [P, 1])
        ks_col = sb("ks_col", [P, 1])
        kscale = sb("kscale", [P, 1])
        dist = sb("dist", [P, NK])
        nk_raw = sb("nk_raw", [NULLS, H0, HD0])
        nk_sq = sb("nk_sq", [NULLS, H0, HD0])
        nk_r = sb("nk_r", [NULLS, H0])
        nk_n = sb("nk_n", [NULLS, H0, HD0])
        nkh = sb("nkh", [P, PAIRS, NULLS], F32R)
        nkl = sb("nkl", [P, PAIRS, NULLS], F32R)
        nv = sb("nv", [4, PAIRS, P])
        xh, xl = sb("xh", [P, S], F32R), sb("xl", [P, S], F32R)
        sq = sb("sq", [P, 2, W])
        ss = sb("ss", [P, 2, H0])
        norm = sb("norm", [P, 2, H0])
        rnorm = sb("rnorm", [P, 2, H0])
        qn, kn, vv = (sb(n, [P, NT, W]) for n in ("qn", "kn", "vv"))
        qh = [[sb(f"qh{r}{e}", [P, S], F32R) for e in range(2)] for r in range(2)]
        ql = [[sb(f"ql{r}{e}", [P, S], F32R) for e in range(2)] for r in range(2)]
        kh = [sb(f"kh{r}", [P, NK], F32R) for r in range(2)]
        kl = [sb(f"kl{r}", [P, NK], F32R) for r in range(2)]
        ptok = [sb(f"ptok{r}", [P, NT, 4]) for r in range(2)]
        bias = [sb(f"bias{r}", [P, NK]) for r in range(2)]
        sc = [sb(f"sc{r}", [P, NK]) for r in range(2)]
        nmax = sb("nmax", [P, RP, NT])
        sums = sb("sums", [P, RP, NT])
        rsum = sb("rsum", [P, RP, NT])
        prob = sb("prob", [P, RP, NT, NK + 2])
        pt = [[sb(f"pt{r}_{kt}", [P, S - kt * P]) for kt in range(NT)] for r in range(2)]
        pn = sb("pn", [4, S])
        oh, ol = sb("oh", [P, S], F32R), sb("ol", [P, S], F32R)
        yT = sq[:, 0, 0:S]

        names = ("loaded staged0 staged1 split split_a consts nulls step zT_ready xh_ready xT_ready q_done k_done v_done "
                 "sq_q sq_k ssum norm_ready v_free qT kT qhi_ready qst_ready kh_ready kst_ready bias_ready "
                 "score tile_scored exp_done prob_ready ptr pt_evac pt_evac_a nptr npt_evac pv oh_ready o_ready y_done yT_ready "
                 "y_tok batch_done nT nt_done nkh_done rs_ready")
        s = {n: k.sem("a0_" + n) for n in names.split()}
        ps = k.ps
        TB, OB, YB = 4, 6, 7
        PB = (3, 5)

        def slot(i):
            return ps[:, 0:2, :].rearrange("p a n -> p (a n)") if i % 2 else ps[:, 2, :]

        weights = [("wq", wqkv[0]), ("wk", wqkv[1]), ("wv", wqkv[2]), ("wo", wo)]

        with nc.Block() as block:
            @block.sync
            def _(sp):
                src = {"wq": d["L0_attn_w_q"], "wk": d["L0_attn_w_kv"][:, 0:W], "wv": d["L0_attn_w_kv"][:, W:2 * W],
                       "wo": d["L0_attn_w_out"].rearrange("(h p) d -> p h d", p=P)}
                for n, (name, _) in enumerate(weights):
                    if n >= 2:
                        sp.wait_ge(s["split"], n - 1)
                    dst = sq[:, n % 2, :] if name != "wo" else sq[:, n % 2, :].rearrange("p (h d) -> p h d", d=D)
                    sp.dma_start(dst, src[name]).then_inc(s[f"staged{n % 2}"], 16)
                for col, name in ((gamma, "L0_attn_gamma"),):
                    sp.dma_start(col[:], d[name].rearrange("(p a) -> p a", a=1)).then_inc(s["loaded"], 16)
                for half in range(2):
                    sp.dma_start(qs_col[half * HD0:(half + 1) * HD0, :],
                                 d["L0_attn_q_scale"].rearrange("(p a) -> p a", a=1)).then_inc(s["loaded"], 16)
                    sp.dma_start(ks_col[half * HD0:(half + 1) * HD0, :],
                                 d["L0_attn_k_scale"].rearrange("(p a) -> p a", a=1)).then_inc(s["loaded"], 16)
                nkv = d["L0_attn_null_kv"].rearrange("h (n two) d -> two n h d", two=2)
                sp.dma_start(nk_raw[:], nkv[0]).then_inc(s["loaded"], 16)
                sp.wait_ge(s["nulls"], 1)
                nvp = d["L0_attn_null_kv"].rearrange("(g e) (n two) d -> e two n g d", two=2, e=2)
                for e in range(2):
                    sp.dma_start(nv[2 * e:2 * e + 2, :, e * HD0:(e + 1) * HD0], nvp[e, 1]).then_inc(s["loaded"], 16)
                sp.wait_ge(s["loaded"], 16 * 8)

            @block.gpsimd
            def _(pool):
                pool.memset(nv[:], 0.0).then_inc(s["nulls"], 1)
                layernorm_pool(k, pool)
                for r in range(2):
                    for half in (qh, ql):
                        for e in range(2):
                            pool.memset(half[r][e][:].bitcast(F32), 0.0)
                pool.iota(dist[:], [[1, NK]], base=-(S - P) - NULLS, channel_multiplier=-1,
                          allow_small_or_imprecise_dtypes=True).then_inc(s["consts"], 1)
                pool.wait_ge(s["consts"], 1)
                pool.affine_select(out=dist[:], in_=dist[:], compare_op=ALU.is_ge, fill=NEG,
                                   base=(S - P) + NULLS, pattern=[[-1, NK]], channel_multiplier=1).then_inc(s["consts"], 1)
                layernorm_pool(k, pool, 1)

            @block.scalar
            def _(act):
                for n, (name, halves) in enumerate(weights):
                    act.wait_ge(s[f"staged{n % 2}"], 16 * (n // 2 + 1))
                    dst = halves[0][:] if name != "wo" else halves[0][:].rearrange("p h d -> p (h d)")
                    act.activation(dst, sq[:, n % 2, :], ACT.Copy).then_inc(s["split_a"], 1)
                act.wait_ge(s["nt_done"], 1)
                act.activation(nk_r[:], nk_r[:], ACT.Sqrt).then_inc(s["nt_done"], 1)
                act.wait_ge(s["nT"], 1)
                act.activation(nkh[:].rearrange("p h n -> p (h n)"), ps[:, 0, 0:H0], ACT.Identity,
                               scale=kscale[:, 0:1]).then_inc(s["nkh_done"], 1)

            @block.vector
            def _(v):
                layernorm_vector(k, v, k.x)
                for n, (name, halves) in enumerate(weights):
                    v.wait_ge(s["split_a"], n + 1)
                    flat = (lambda t: t[:]) if name != "wo" else (lambda t: t[:].rearrange("p h d -> p (h d)"))
                    v.tensor_tensor(flat(halves[1]), sq[:, n % 2, :], flat(halves[0]).bitcast(F32), ALU.subtract).then_inc(s["split"], 1)
                layernorm_vector(k, v, k.z, 1)
                step = chain(v, s["step"])
                v.wait_ge(s["loaded"], 16 * 8)
                step(v.scalar_tensor_tensor(kscale[:], qs_col[:], 8.0, ks_col[:], ALU.mult, ALU.mult))
                step(v.tensor_tensor(nk_sq[:], nk_raw[:], nk_raw[:], ALU.mult))
                v.tensor_reduce(nk_r[:], nk_sq[:], AX, ALU.add).then_inc(s["nt_done"], 1)
                v.wait_ge(s["nt_done"], 2)
                step(v.tensor_scalar(nk_r[:], nk_r[:], 1e-12, None, ALU.max))
                step(v.reciprocal(nk_r[:], nk_r[:]))
                v.tensor_tensor(nk_n[:], nk_raw[:], nk_r[:].unsqueeze(2).to_broadcast([NULLS, H0, HD0]), ALU.mult).then_inc(s["nt_done"], 1)
                v.wait_ge(s["nkh_done"], 1)
                v.scalar_tensor_tensor(nkl[:].rearrange("p h n -> p (h n)"), ps[:, 0, 0:H0], kscale[:, 0:1],
                                       nkh[:].rearrange("p h n -> p (h n)").bitcast(F32), ALU.mult, ALU.subtract)

            @block.tensor
            def _(pe):
                pe.wait_ge(s["nt_done"], 3)
                for g in range(PAIRS):
                    last = pe.transpose(ps[:, 0, NULLS * g:NULLS * g + NULLS],
                                        nk_n[:, 2 * g:2 * g + 2, :].rearrange("p e d -> p (e d)"), k.ident[0:NULLS, 0:NULLS])
                last.then_inc(s["nT"], 1)

        step0 = 4

        with nc.Block() as block:
            @block.vector
            def _(v):
                with v.Fori(0, B) as b:
                    v.wait_ge(s["batch_done"], b)
                    take_batch(k, v, b)
                    step = chain(v, s["step"], STEPS, b)
                    step.count[0] = step0
                    v.wait_ge(s["xh_ready"], b + 1)
                    v.scalar_tensor_tensor(xl[:], k.bank(0), gamma[:, 0:1], xh[:].bitcast(F32), ALU.mult,
                                           ALU.subtract).then_inc(s["xT_ready"], 1)
                    for t in range(NT):
                        for j, (squared, dst) in enumerate((("sq_q", qn), ("sq_k", kn))):
                            v.wait_ge(s[squared], b * NT + t + 1)
                            v.tensor_reduce(ss[:, j, :], sq[:, j, :].rearrange("p (h e) -> p h e", e=HD0), AX,
                                            ALU.add).then_inc(s["ssum"], 1)
                            v.wait_ge(s["norm_ready"], b * 2 * NT + 2 * t + j + 1)
                            step(v.tensor_scalar(norm[:, j, :], norm[:, j, :], 1e-12, None, ALU.max))
                            step(v.reciprocal(rnorm[:, j, :], norm[:, j, :]))
                            step(v.tensor_tensor(dst[:, t, :].rearrange("p (h e) -> p h e", e=HD0),
                                                 ps[:, 2 * j:2 * j + 2, :].rearrange("p a (h e) -> p (a h) e", e=HD0),
                                                 rnorm[:, j, :].unsqueeze(2).to_broadcast([P, H0, HD0]), ALU.mult))

                    def prepare_q(g):
                        r = g % 2
                        v.wait_ge(s["qhi_ready"], b * PAIRS + g + 1)
                        for e in range(2):
                            rows = slice(e * HD0, (e + 1) * HD0)
                            last = v.tensor_tensor(ql[r][e][rows, :], ps[rows, TB, :], qh[r][e][rows, :].bitcast(F32),
                                                   ALU.subtract)
                        last.then_inc(s["qst_ready"], 1)

                    def prepare_k(g):
                        r = g % 2
                        v.wait_ge(s["kh_ready"], b * PAIRS + g + 1)
                        v.scalar_tensor_tensor(kl[r][:, NULLS:NK], ps[:, TB, :], kscale[:, 0:1],
                                               kh[r][:, NULLS:NK].bitcast(F32), ALU.mult, ALU.subtract).then_inc(s["kst_ready"], 1)

                    def score(h, i):
                        u = h * NT + i
                        if i == 0:
                            v.wait_ge(s["bias_ready"], b * H0 + h + 1)
                        v.wait_ge(s["score"], b * H0 * NT + u + 1)
                        if u >= 2:
                            v.wait_ge(s["exp_done"], b * H0 * NT + u - 1)
                        k.settle(v)
                        v.tensor_tensor_reduce(sc[u % 2][:, 0:keys(i)], slot(i)[:, 0:keys(i)],
                                               bias[h % 2][:, S - P - i * P:NK], -1.0, 3.0e38, ALU.add, ALU.min,
                                               nmax[:, h % RP, i:i + 1]).then_inc(s["tile_scored"], 1)

                    def output_low(g):
                        v.wait_ge(s["oh_ready"], b * PAIRS + g + 1)
                        v.tensor_tensor(ol[:], k.bank(OB), oh[:].bitcast(F32), ALU.subtract).then_inc(s["o_ready"], 1)

                    def invert(h):
                        v.wait_ge(s["exp_done"], b * H0 * NT + h * NT + NT)
                        v.reciprocal(rsum[:, h % RP, :], sums[:, h % RP, :]).then_inc(s["rs_ready"], 1)

                    def evacuate(h, kt):
                        r = h % 2
                        v.wait_ge(s["ptr"], b * H0 * NT + h * NT + kt + 1)
                        if h >= 2:
                            v.wait_ge(s["pv"], b * H0 + h - 1)
                        v.tensor_copy(pt[r][kt][:], ps[:, PB[kt % 2], 0:S - kt * P]).then_inc(s["pt_evac"], 1)

                    prepare_q(0)
                    prepare_k(0)
                    for h in range(AHEAD):
                        for i in range(NT):
                            score(h, i)
                    invert(0)
                    prepare_q(1)
                    prepare_k(1)
                    for h in range(H0):
                        if h % 2 == 0 and h:
                            output_low(h // 2 - 1)
                        for i in range(NT):
                            if h + AHEAD < H0:
                                score(h + AHEAD, i)
                            if i == 0 and h + 1 < H0:
                                invert(h + 1)
                            if i == 2 and h // 2 + 2 < PAIRS:
                                (prepare_k if h % 2 else prepare_q)(h // 2 + 2)
                            if i % 2:
                                evacuate(h, i)
                    output_low(PAIRS - 1)
                    v.wait_ge(s["y_tok"], b + 1)
                    v.tensor_tensor(k.x[:, bass.ds(b * NT, NT), :], k.x[:, bass.ds(b * NT, NT), :],
                                    k.bank(TB).rearrange("p (t d) -> p t d", d=D), ALU.add).then_inc(s["batch_done"], 1)
                    assert step.count[0] == step0 + STEPS

            @block.gpsimd
            def _(pool):
                with pool.Fori(0, B) as b:
                    pool.wait_ge(s["batch_done"], b)

                    def head_constants(h):
                        r = h % 2
                        if h >= 2:
                            pool.wait_ge(s["tile_scored"], b * H0 * NT + (h - 1) * NT)
                        k.settle(pool)
                        last = pool.tensor_scalar(bias[r][:], dist[:], slopes[h], 1.0, ALU.mult, ALU.mult)
                        if h % 2 == 0:
                            r = h // 2 % 2
                            pool.tensor_copy(kh[r][:, 0:NULLS], nkh[:, h // 2, :].bitcast(F32))
                            last = pool.tensor_copy(kl[r][:, 0:NULLS], nkl[:, h // 2, :].bitcast(F32))
                        last.then_inc(s["bias_ready"], 1)

                    for h in range(AHEAD):
                        head_constants(h)
                    for h in range(H0):
                        r = h % RP
                        pool.wait_ge(s["rs_ready"], b * H0 + h + 1)
                        k.settle(pool)
                        for i in range(NT):
                            last = pool.tensor_scalar(prob[:, r, i, 0:keys(i)], prob[:, r, i, 0:keys(i)], rsum[:, r, i:i + 1],
                                                      0.0, ALU.mult, ALU.add)
                        last.then_inc(s["prob_ready"], 1)
                        if h + AHEAD < H0:
                            head_constants(h + AHEAD)
                        pool.wait_ge(s["prob_ready"], b * 2 * H0 + 2 * h + 1)
                        k.settle(pool)
                        pool.tensor_copy(ptok[h // 2 % 2][:, :, 2 * (h % 2):2 * (h % 2) + 2], prob[:, r, :, 0:NULLS]).then_inc(s["prob_ready"], 1)

            @block.scalar
            def _(act):
                with act.Fori(0, B) as b:
                    act.wait_ge(s["zT_ready"], b + 1)
                    act.activation(xh[:], k.bank(0), ACT.Identity, scale=gamma[:, 0:1]).then_inc(s["xh_ready"], 1)
                    for t in range(NT):
                        n = b * NT + t + 1
                        act.wait_ge(s["q_done"], n)
                        act.activation(sq[:, 0, :], ps[:, 0:2, :].rearrange("p a n -> p (a n)"), ACT.Square).then_inc(s["sq_q"], 1)
                        act.wait_ge(s["ssum"], 2 * (b * NT + t) + 1)
                        act.activation(norm[:, 0, :], ss[:, 0, :], ACT.Sqrt).then_inc(s["norm_ready"], 1)
                        act.wait_ge(s["k_done"], n)
                        act.activation(sq[:, 1, :], ps[:, 2:4, :].rearrange("p a n -> p (a n)"), ACT.Square).then_inc(s["sq_k"], 1)
                        act.wait_ge(s["v_done"], n)
                        act.activation(vv[:, t, :], ps[:, 6:8, :].rearrange("p a n -> p (a n)"), ACT.Copy).then_inc(s["v_free"], 1)
                        act.wait_ge(s["ssum"], 2 * (b * NT + t) + 2)
                        act.activation(norm[:, 1, :], ss[:, 1, :], ACT.Sqrt).then_inc(s["norm_ready"], 1)

                    def prepare_q(g):
                        act.wait_ge(s["qT"], b * PAIRS + g + 1)
                        for e in range(2):
                            rows = slice(e * HD0, (e + 1) * HD0)
                            last = act.activation(qh[g % 2][e][rows, :], ps[rows, TB, :], ACT.Copy)
                        last.then_inc(s["qhi_ready"], 1)

                    def prepare_k(g):
                        r = g % 2
                        act.wait_ge(s["kT"], b * PAIRS + g + 1)
                        act.activation(kh[r][:, NULLS:NK], ps[:, TB, :], ACT.Identity, scale=kscale[:, 0:1]).then_inc(s["kh_ready"], 1)

                    def exp(h, i):
                        r, u = h % RP, h * NT + i
                        act.wait_ge(s["tile_scored"], b * H0 * NT + u + 1)
                        if h >= RP:
                            act.wait_ge(s["ptr"], b * H0 * NT + (h - RP + 1) * NT)
                            act.wait_ge(s["prob_ready"], b * 2 * H0 + 2 * (h - RP + 1))
                        act.activation(prob[:, r, i, 0:keys(i)], sc[u % 2][:, 0:keys(i)], ACT.Exp, scale=-1.0,
                                       bias=nmax[:, r, i:i + 1], accum_out=sums[:, r, i:i + 1]).then_inc(s["exp_done"], 1)

                    def evacuate(h, kt):
                        r = h % 2
                        act.wait_ge(s["ptr"], b * H0 * NT + h * NT + kt + 1)
                        if h >= 2:
                            act.wait_ge(s["pv"], b * H0 + h - 1)
                        act.activation(pt[r][kt][:], ps[:, PB[kt % 2], 0:S - kt * P], ACT.Copy).then_inc(s["pt_evac_a"], 1)

                    prepare_q(0)
                    prepare_k(0)
                    for h in range(AHEAD):
                        for i in range(NT):
                            exp(h, i)
                    prepare_q(1)
                    prepare_k(1)
                    for h in range(H0):
                        for i in range(NT):
                            if i % 2 == 0:
                                evacuate(h, i)
                            if i == 0 and h % 2:
                                act.wait_ge(s["nptr"], b * PAIRS + h // 2 + 1)
                                if h > 2:
                                    act.wait_ge(s["pv"], b * H0 + h - 1)
                                act.activation(pn[:], ps[0:4, PB[1], :], ACT.Copy).then_inc(s["npt_evac"], 1)
                            if h + AHEAD < H0:
                                exp(h + AHEAD, i)
                            if i == 1 and h // 2 + 2 < PAIRS:
                                (prepare_k if h % 2 else prepare_q)(h // 2 + 2)
                        if h % 2:
                            g = h // 2
                            act.wait_ge(s["pv"], b * H0 + h + 1)
                            if g:
                                act.wait_ge(s["y_done"], b * PAIRS + g)
                            act.activation(oh[:], k.bank(OB), ACT.Copy).then_inc(s["oh_ready"], 1)
                    act.wait_ge(s["y_done"], b * PAIRS + PAIRS)
                    act.activation(yT, k.bank(YB), ACT.Copy).then_inc(s["yT_ready"], 1)

            @block.tensor
            def _(pe):
                with pe.Fori(0, B) as b:
                    pe.wait_ge(s["step"], b * STEPS + step0)
                    pe.wait_ge(k.zb_ready, k.n_batches + b + 1)
                    for t in range(NT):
                        last = pe.transpose(ps[:, 0, t * P:(t + 1) * P], k.zb[:, t, :], k.ident[:])
                    last.then_inc(s["zT_ready"], 1)
                    pe.wait_ge(s["xT_ready"], b + 1)
                    for t in range(NT):
                        tok = slice(t * P, (t + 1) * P)
                        for j, done in ((0, "q_done"), (1, "k_done"), (2, "v_done")):
                            if t and j < 2:
                                pe.wait_ge(s["step"], b * STEPS + step0 + 6 * (t - 1) + 3 + 3 * j)
                            if t and j == 2:
                                pe.wait_ge(s["v_free"], b * NT + t)
                            for half in range(2):
                                cols = slice(half * 512, half * 512 + 512)
                                last = split_product(pe, k.bank((0, 2, 6)[j] + half), (xh[:, tok], xl[:, tok]),
                                                     (wqkv[j][0][:, cols], wqkv[j][1][:, cols]))
                            last.then_inc(s[done], 1)
                    pe.wait_ge(s["v_free"], b * NT + NT)

                    def prepare(g, src, done):
                        for t in range(NT):
                            last = pe.transpose(ps[:, TB, t * P:(t + 1) * P], src[:, t, g * P:(g + 1) * P], k.ident[:])
                        last.then_inc(s[done], 1)

                    def keys_ready(h):
                        if h % 2 == 0:
                            pe.wait_ge(s["kst_ready"], b * PAIRS + h // 2 + 1)
                            pe.wait_ge(s["bias_ready"], b * H0 + h + 1)

                    def score(h, i):
                        r, e, u = h // 2 % 2, h % 2, h * NT + i
                        if i == 0:
                            keys_ready(h)
                        if u >= 2:
                            pe.wait_ge(s["tile_scored"], b * H0 * NT + u - 1)
                        tile = slice(i * P, (i + 1) * P)
                        for lo, hi in ((0, min(keys(i), 512)), (512, keys(i))):
                            if hi > lo:
                                last = split_product(pe, slot(i)[:, lo:hi], (qh[r][e][:, tile], ql[r][e][:, tile]),
                                                     (kh[r][:, lo:hi], kl[r][:, lo:hi]))
                        last.then_inc(s["score"], 1)

                    def evacuated(h, kt):
                        if kt % 2:
                            pe.wait_ge(s["pt_evac"], b * H0 * 2 + h * 2 + kt // 2 + 1)
                        else:
                            pe.wait_ge(s["pt_evac_a"], b * H0 * 2 + h * 2 + kt // 2 + 1)

                    def transpose_probs(h, kt):
                        r, u = h % RP, h * NT + kt
                        if u >= 2:
                            evacuated((u - 2) // NT, (u - 2) % NT)
                        if kt == 1 and h % 2:
                            pe.wait_ge(s["npt_evac"], b * PAIRS + h // 2 + 1)
                        if kt == 0:
                            pe.wait_ge(s["prob_ready"], b * 2 * H0 + 2 * h + 1)
                        for i in range(kt, NT):
                            last = pe.transpose(ps[:, PB[kt % 2], (i - kt) * P:(i - kt + 1) * P],
                                                prob[:, r, i, NULLS + kt * P:NULLS + (kt + 1) * P], k.ident[:])
                        last.then_inc(s["ptr"], 1)

                    def values(h, kt):
                        r, e = h % 2, h % 2
                        evacuated(h, kt)
                        last = pe.matmul(ps[e * HD0:(e + 1) * HD0, OB, kt * P:S], vv[:, kt, h * HD0:(h + 1) * HD0], pt[r][kt][:],
                                         start=(kt == 0), stop=(kt == NT - 1 and e == 0), skip_group_check=True)
                        if kt == NT - 1 and e == 0:
                            last.then_inc(s["pv"], 1)

                    def pair_nulls(g):
                        evacuated(2 * g, 3)
                        pe.wait_ge(s["prob_ready"], b * 2 * H0 + 4 * g + 4)
                        for i in range(NT):
                            last = pe.transpose(ps[0:4, PB[1], i * P:(i + 1) * P], ptok[g % 2][:, i, :], k.ident[:])
                        last.then_inc(s["nptr"], 1)

                    def pair_end(g):
                        pe.wait_ge(s["npt_evac"], b * PAIRS + g + 1)
                        pe.matmul(k.bank(OB), nv[:, g, :], pn[:], start=False, stop=True,
                                  skip_group_check=True).then_inc(s["pv"], 1)

                    def project(g):
                        pe.wait_ge(s["o_ready"], b * PAIRS + g + 1)
                        split_product(pe, k.bank(YB), (wo[0][:, g, :], wo[1][:, g, :]), (oh[:], ol[:]), start=(g == 0),
                                      stop=(g == PAIRS - 1)).then_inc(s["y_done"], 1)

                    pe.wait_ge(s["step"], b * STEPS + step0 + 6 * NT)
                    for g in range(2):
                        if g:
                            pe.wait_ge(s["kst_ready"], b * PAIRS + g)
                        prepare(g, qn, "qT")
                        pe.wait_ge(s["qst_ready"], b * PAIRS + g + 1)
                        prepare(g, kn, "kT")
                        if g == 0:
                            for h in range(AHEAD):
                                for i in range(NT):
                                    score(h, i)
                    for h in range(H0):
                        g = h // 2
                        if g + 2 < PAIRS:
                            if h % 2:
                                pe.wait_ge(s["qst_ready"], b * PAIRS + g + 3)
                                prepare(g + 2, kn, "kT")
                            else:
                                pe.wait_ge(s["kst_ready"], b * PAIRS + g + 2)
                                prepare(g + 2, qn, "qT")
                        for i in range(NT):
                            if h + AHEAD < H0:
                                score(h + AHEAD, i)
                            transpose_probs(h, i)
                            if i == 3 and h % 2 == 0 and h:
                                project(g - 1)
                            if i == 0 and h % 2:
                                pair_nulls(g)
                            if i == 0:
                                if h % 2 == 0 and h:
                                    pe.wait_ge(s["o_ready"], b * PAIRS + h // 2)
                            else:
                                values(h, i - 1)
                        values(h, NT - 1)
                        if h % 2:
                            pair_end(g)
                    project(PAIRS - 1)
                    pe.wait_ge(s["yT_ready"], b + 1)
                    for t in range(NT):
                        last = pe.transpose(ps[:, TB, t * P:(t + 1) * P], yT[:, t * P:(t + 1) * P], k.ident[:])
                    last.then_inc(s["y_tok"], 1)
    k.n_ln += 2
    k.n_batches += B


def cross_attention(k, pre, heads, hd, weights, biases, out_bias, scale, causal, mask):
    nc, d = k.nc, k.dram
    HALF = 8
    U1 = heads // HALF
    NB = 2
    TI = NB * NT
    U = TI * U1
    G = heads // 4
    STEPS = U * (2 + (mask is not None)) + U1 * NB * causal
    RP = 4

    with ExitStack() as ctx:
        def sb(name, shape, dt=F32):
            return k.sb(ctx, pre + name, shape, dt)

        def sem(name):
            return k.sem(pre + name)

        w_nat = sb("w_nat", [P, 4, P])
        wt = sb("w", [P, 3, P])
        wo = sb("wo", [P, G, P])
        woT = sb("woT", [P, P])
        bcol = sb("bcol", [P, 2])
        brow = sb("brow", [P, 2, P])
        head_mask = sb("head_mask", [P, heads])
        ctx_nat = sb("ctx_nat", [KC, B, D])
        ctxT = sb("ctxT", [P, B, KC])
        kT = sb("kT", [P, B, KC])
        kb = sb("kb", [P, B, heads, KC])
        vall = sb("vall", [KC, B, P])
        vpad = sb("vpad", [KC, NB, heads, 32])
        zT, qT = sb("zT", [P, NB, S]), sb("qT", [P, NB * S])
        sc = [sb(f"sc{r}", [P, HALF, KC]) for r in range(2)]
        pr = [sb(f"pr{r}", [P, HALF, KC]) for r in range(RP)]
        mx = [sb(f"mx{r}", [P, HALF]) for r in range(2)]
        sm = [sb(f"sm{r}", [P, HALF]) for r in range(2)]
        rs = [sb(f"rs{r}", [P, HALF]) for r in range(2)]
        pT = [sb(f"pT{r}", [KC, HALF, P]) for r in range(2)]
        oT = [sb(f"oT{r}", [P, 2, P]) for r in range(2)]
        cmask = sb("cmask", [P, KC])
        if mask is not None:
            mraw = sb("mraw", [P, TT, KC], I32)
            drop = sb("drop", [P, TT, KC])

        names = ("loaded diagonal wT wT_out ctxTr ctxT_out kv_done kv_out zTr zT_out q_done q_out vpad_done score "
                 "scored exp_done inverted normed ptr pt_evac pv o_evac y_done batch_done step woz wo_out consts y_used")
        s = {n: sem(n) for n in names.split()}
        ps = k.ps
        diag = weights[0].shape[0] == hd
        if diag:
            w_rep = sb("w_rep", [P, 3, hd])
        n_loads = 0

        with nc.Block() as block:
            loads = []
            if diag:
                for j in range(3):
                    loads.append((w_rep[:, j, :], weights[j].unsqueeze(0).to_broadcast([heads, hd, hd])))
            else:
                for j in range(3):
                    loads.append((w_nat[:, j, :], weights[j]))
            loads.append((w_nat[:, 3, :], weights[3]))
            loads.append((ctx_nat[:], d["ctx_1024"].rearrange("b k d -> k b d")))
            if biases is not None:
                for j in range(2):
                    loads.append((bcol[:, j:j + 1], biases[j].rearrange("(p a) -> p a", a=1)))
                loads.append((brow[:, 0, :], biases[2].partition_broadcast(P)))
            loads.append((brow[:, 1, :], out_bias.partition_broadcast(P)))
            if mask is not None:
                loads.append((mraw[:], mask.rearrange("b a (t p) k -> p (b a t) k", p=P)))

            @block.sync
            def _(sp):
                for dst, src in loads:
                    sp.dma_start(dst, src).then_inc(s["loaded"], 16)
                sp.wait_ge(s["loaded"], 16 * len(loads))

            @block.gpsimd
            def _(pool):
                pool.memset(vpad[:], 0.0)
                if biases is None:
                    pool.memset(bcol[:], 0.0)
                    pool.memset(brow[:, 0, :], 0.0)
                pool.memset(woT[:], 1.0)
                pool.memset(cmask[:], 0.0)
                pool.memset(head_mask[:], 1.0).then_inc(s["consts"], 1)
                pool.wait_ge(s["consts"], 1)
                pool.affine_select(out=head_mask[:], in_=head_mask[:], compare_op=ALU.is_ge, fill=0.0, base=0,
                                   pattern=[[-hd, heads]], channel_multiplier=1).then_inc(s["consts"], 1)
                pool.wait_ge(s["consts"], 2)
                pool.affine_select(out=head_mask[:], in_=head_mask[:], compare_op=ALU.is_ge, fill=0.0, base=hd - 1,
                                   pattern=[[hd, heads]], channel_multiplier=-1).then_inc(s["consts"], 1)
                pool.affine_select(out=cmask[:], in_=cmask[:], compare_op=ALU.is_ge, fill=NEG, base=0,
                                   pattern=[[-1, KC]], channel_multiplier=1).then_inc(s["consts"], 1)
                pool.wait_ge(s["consts"], 4)
                layernorm_pool(k, pool)

            @block.tensor
            def _(pe):
                pe.wait_ge(s["loaded"], 16 * len(loads))
                if diag:
                    pe.wait_ge(s["diagonal"], 1)
                for j in range(3):
                    last = pe.transpose(ps[:, 0, j * P:(j + 1) * P], w_nat[:, j, :], k.ident[:])
                last.then_inc(s["wT"], 1)
                for g in range(G):
                    for j in range(4):
                        h = 4 * g + j
                        last = pe.transpose(ps[0:hd, 1 + g, j * P:(j + 1) * P],
                                            w_nat[:, 3, h * hd:(h + 1) * hd], k.ident[:])
                last.then_inc(s["wT"], 1)
                for b in range(B):
                    last = pe.transpose(ps[:, 6, b * KC:(b + 1) * KC], ctx_nat[:, b, :], k.ident[0:KC, 0:KC])
                last.then_inc(s["ctxTr"], 1)
                pe.wait_ge(s["ctxT_out"], 1)
                pe.wait_ge(s["wT_out"], 1)
                pe.matmul(ps[:, 7, 0:B * KC], wt[:, 1, :], ctxT[:].rearrange("p b k -> p (b k)"), start=True,
                          stop=True).then_inc(s["kv_done"], 1)
                for b in range(B):
                    last = pe.matmul(ps[0:KC, 0, b * P:(b + 1) * P], ctxT[:, b, :], wt[:, 2, :], start=True, stop=True)
                last.then_inc(s["kv_done"], 1)

            @block.scalar
            def _(act):
                act.wait_ge(s["wT"], 1)
                act.activation(wt[:].rearrange("p j d -> p (j d)"), ps[:, 0, 0:3 * P], ACT.Copy).then_inc(s["wT_out"], 1)
                act.wait_ge(s["kv_done"], 1)
                act.activation(kT[:].rearrange("p b k -> p (b k)"), ps[:, 7, 0:B * KC], ACT.Identity,
                               bias=bcol[:, 1:2]).then_inc(s["kv_out"], 1)

            @block.vector
            def _(v):
                v.memset(wo[:], 0.0).then_inc(s["woz"], 1)
                layernorm_vector(k, v, k.x)
                if diag:
                    v.wait_ge(s["consts"], 4)
                    v.wait_ge(s["loaded"], 16 * len(loads))
                    for j in range(3):
                        last = v.tensor_tensor(w_nat[:, j, :].rearrange("p (h e) -> p h e", e=hd),
                                               w_rep[:, j, :].unsqueeze(1).to_broadcast([P, heads, hd]),
                                               head_mask[:].unsqueeze(2).to_broadcast([P, heads, hd]), ALU.mult)
                    last.then_inc(s["diagonal"], 1)
                v.wait_ge(s["woz"], 1)
                v.wait_ge(s["wT"], 2)
                for h in range(heads):
                    last = v.tensor_copy(wo[32 * (h % 4):32 * (h % 4) + hd, h // 4, :], ps[0:hd, 1 + h // 4, (h % 4) * P:(h % 4 + 1) * P])
                last.then_inc(s["wo_out"], 1)
                v.wait_ge(s["ctxTr"], 1)
                v.tensor_copy(ctxT[:].rearrange("p b k -> p (b k)"), ps[:, 6, 0:B * KC]).then_inc(s["ctxT_out"], 1)
                v.wait_ge(s["loaded"], 16 * len(loads))
                v.tensor_tensor(k.x[:], k.x[:], brow[:, 1, :].unsqueeze(1).to_broadcast([P, TT, P]), ALU.add)
                v.wait_ge(s["consts"], 4)
                v.wait_ge(s["kv_out"], 1)
                for b in range(B):
                    v.tensor_tensor(kb[:, b, :, :], kT[:, b, :].unsqueeze(1).to_broadcast([P, heads, KC]),
                                    head_mask[:].unsqueeze(2).to_broadcast([P, heads, KC]), ALU.mult)
                v.wait_ge(s["kv_done"], 2)
                v.tensor_tensor(vall[:], ps[0:KC, 0, :].rearrange("p (b d) -> p b d", d=P),
                                brow[0:KC, 0, :].unsqueeze(1).to_broadcast([KC, B, P]), ALU.add)
                if mask is not None:
                    v.tensor_scalar(drop[:], mraw[:], 0, -1.0e20, ALU.is_equal, ALU.mult)

        with nc.Block() as block:
            @block.gpsimd
            def _(pool):
                with pool.Fori(0, B // NB) as b:
                    pool.wait_ge(s["batch_done"], b)
                    pool.tensor_copy(vpad[:, :, :, 0:hd], vall[:, bass.ds(b * NB, NB), :].rearrange("p b (h e) -> p b h e", e=hd)).then_inc(s["vpad_done"], 1)
                    for u in range(U):
                        pool.wait_ge(s["inverted"], b * U + u + 1)
                        pool.tensor_tensor(pr[u % RP][:], pr[u % RP][:], rs[u % 2][:].unsqueeze(2).to_broadcast([P, HALF, KC]),
                                           ALU.mult).then_inc(s["normed"], 1)

            @block.vector
            def _(v):
                with v.Fori(0, B // NB) as b:
                    take_batch(k, v, b, NB)
                    step = chain(v, s["step"], STEPS, b)

                    def soften(u):
                        i, half = u // U1, u % U1
                        v.wait_ge(s["score"], b * U + u + 1)
                        if u >= 2:
                            v.wait_ge(s["exp_done"], b * U + u - 1)
                        src = ps[:, 2 * (u % 2):2 * (u % 2) + 2, :].rearrange("p a (h n) -> p (a h) n", n=P)[:, :, 0:KC]
                        dst = sc[u % 2][:]
                        if mask is not None:
                            step(v.tensor_tensor(dst, src, drop[:, b * TI + i, :].unsqueeze(1).to_broadcast([P, HALF, KC]), ALU.add))
                            src = dst
                        elif causal and i % NT == 0:
                            step(v.tensor_tensor(dst, src, cmask[:].unsqueeze(1).to_broadcast([P, HALF, KC]), ALU.add))
                            src = dst
                        step(v.tensor_reduce(mx[u % 2][:], src, AX, ALU.max))
                        v.tensor_tensor(dst, src, mx[u % 2][:].unsqueeze(2).to_broadcast([P, HALF, KC]),
                                        ALU.subtract).then_inc(s["scored"], 1)

                    def invert(u):
                        v.wait_ge(s["exp_done"], b * U + u + 1)
                        step(v.tensor_reduce(sm[u % 2][:], pr[u % RP][:], AX, ALU.add))
                        if u >= 2:
                            v.wait_ge(s["normed"], b * U + u - 1)
                        v.reciprocal(rs[u % 2][:], sm[u % 2][:]).then_inc(s["inverted"], 1)

                    def output(u):
                        v.wait_ge(s["pv"], b * U + u + 1)
                        if u >= 2:
                            v.wait_ge(s["y_done"], b * U + u - 1)
                        v.tensor_copy(oT[u % 2][:].rearrange("p g q -> p (g q)"), ps[:, 6, 0:2 * P]).then_inc(s["o_evac"], 1)

                    def residual(i):
                        v.wait_ge(s["y_done"], b * U + (i + 1) * U1)
                        v.tensor_tensor(k.x[:, b * TI + i, :], k.x[:, b * TI + i, :], ps[:, 7, 0:P],
                                        ALU.add).then_inc(s["y_used"] if i < TI - 1 else s["batch_done"], 1)

                    for w in range(U + 5):
                        if w >= 5 and (w - 5) % U1 == U1 - 1:
                            residual((w - 5) // U1)
                        if w < U:
                            soften(w)
                        if 1 <= w <= U:
                            invert(w - 1)
                        if 3 <= w < U + 3:
                            output(w - 3)
                    assert step.count[0] == STEPS, (step.count[0], STEPS)

            @block.scalar
            def _(act):
                with act.Fori(0, B // NB) as b:
                    act.wait_ge(s["zTr"], b + 1)
                    act.activation(zT[:], ps[:, 4:4 + NB, :], ACT.Copy).then_inc(s["zT_out"], 1)
                    act.wait_ge(s["q_done"], b + 1)
                    act.activation(qT[:], ps[:, 4:4 + NB, :].rearrange("p b n -> p (b n)"), ACT.Identity, bias=bcol[:, 0:1]).then_inc(s["q_out"], 1)

                    def exps(u):
                        act.wait_ge(s["scored"], b * U + u + 1)
                        if u >= RP:
                            act.wait_ge(s["ptr"], b * U + u - RP + 1)
                        act.activation(pr[u % RP][:], sc[u % 2][:], ACT.Exp, scale=scale).then_inc(s["exp_done"], 1)

                    def evacuate(u):
                        act.wait_ge(s["ptr"], b * U + u + 1)
                        if u >= 2:
                            act.wait_ge(s["pv"], b * U + u - 1)
                        act.activation(pT[u % 2][:].rearrange("p h q -> p (h q)"),
                                       ps[0:KC, 4:6, :].rearrange("p a n -> p (a n)"), ACT.Copy).then_inc(s["pt_evac"], 1)

                    for w in range(U + 2):
                        if w < U:
                            exps(w)
                        if w >= 2:
                            evacuate(w - 2)

            @block.tensor
            def _(pe):
                with pe.Fori(0, B // NB) as b:
                    pe.wait_ge(s["batch_done"], b)
                    pe.wait_ge(k.zb_ready, k.n_batches + b + 1)
                    for t in range(TI):
                        last = pe.transpose(ps[:, 4 + t // NT, t % NT * P:(t % NT + 1) * P], k.zb[:, t, :], k.ident[:])
                    last.then_inc(s["zTr"], 1)
                    pe.wait_ge(s["zT_out"], b + 1)
                    for c in range(NB):
                        last = pe.matmul(k.bank(4 + c), wt[:, 0, :], zT[:, c, :], start=True, stop=True)
                    last.then_inc(s["q_done"], 1)
                    pe.wait_ge(s["q_out"], b + 1)

                    def scores(u):
                        i, half = u // U1, u % U1
                        if u >= 2:
                            pe.wait_ge(s["scored"], b * U + u - 1)
                        for a in range(2):
                            h = half * HALF + 4 * a
                            last = pe.matmul(ps[:, 2 * (u % 2) + a, :].rearrange("p (h n) -> p h n", n=P)[:, :, 0:KC], qT[:, i * P:(i + 1) * P],
                                             kb[:, b * NB + i // NT, h:h + 4, :], start=True, stop=True)
                        last.then_inc(s["score"], 1)

                    def values(u):
                        i, half = u // U1, u % U1
                        pe.wait_ge(s["pt_evac"], b * U + u + 1)
                        if u == 0:
                            pe.wait_ge(s["vpad_done"], b + 1)
                        else:
                            pe.wait_ge(s["o_evac"], b * U + u)
                        for j in range(HALF):
                            last = pe.matmul(ps[32 * (j % 4):32 * (j % 4) + 32, 6, (j // 4) * P:(j // 4 + 1) * P],
                                             vpad[:, i // NT, half * HALF + j, :], pT[u % 2][:, j, :], start=True, stop=True)
                        last.then_inc(s["pv"], 1)

                    def project(u):
                        i, half = u // U1, u % U1
                        pe.wait_ge(s["o_evac"], b * U + u + 1)
                        if half == 0 and i:
                            pe.wait_ge(s["y_used"], b * (TI - 1) + i)
                        for g in range(2):
                            last = pe.matmul(ps[:, 7, 0:P], oT[u % 2][:, g, :], wo[:, half * 2 + g, :],
                                             start=(half == 0 and g == 0), stop=(half == U1 - 1 and g == 1))
                        last.then_inc(s["y_done"], 1)

                    def transpose_probs(u):
                        pe.wait_ge(s["normed"], b * U + u + 1)
                        if u:
                            pe.wait_ge(s["pt_evac"], b * U + u)
                        for j in range(HALF):
                            last = pe.transpose(ps[0:KC, 4 + j // 4, (j % 4) * P:(j % 4 + 1) * P], pr[u % RP][:, j, :], k.ident[:])
                        last.then_inc(s["ptr"], 1)

                    for w in range(U + 4):
                        if w < U:
                            scores(w)
                        if 3 <= w < U + 3:
                            values(w - 3)
                        if 2 <= w < U + 2:
                            transpose_probs(w - 2)
                        if w >= 4:
                            project(w - 4)
    k.n_ln += 1
    k.n_batches += B // NB


def stage_cross_attention_0(k):
    d = k.dram
    cross_attention(k, "x0_", HC0, HDC0, [d["L0_xattn_W" + n] for n in "qkvo"], [d["L0_xattn_b" + n] for n in "qkv"],
                    d["L0_xattn_bo"], HDC0 ** -0.5, True, None)


def stage_cross_attention_1(k):
    d = k.dram
    cross_attention(k, "x1_", H1, HD1, [d["L1_xattn_W" + n] for n in "qkvo"], None,
                    d["L1_xattn_bo"], float(D) ** -0.5, False, d["mask_Bx1xSxS2_if1"])


def stage_experts_0(k):
    nc, d = k.nc, k.dram
    NB = 2
    TI = NB * NT
    PAIRS = NE0 // 2
    GE = 40
    GROUPS = NE0 // GE
    ROWS = 3 * GE
    PER_IT = 4
    ITS = PAIRS // PER_IT
    assert GROUPS == PER_IT and GE == 2 * ITS
    CH = B
    UNITS = PER_IT * CH
    LAG = 3
    R = 4
    AHEAD = LAG + 1
    RSTEPS = 13
    TAKEN = -3.0e38
    YB, HB, CB, TB = 0, 4, 6, 7

    with ExitStack() as ctx:
        def sb(name, shape, dt=F32):
            return k.sb(ctx, "f0_" + name, shape, dt)

        xh, xl = sb("xh", [P, B, S], F32R), sb("xl", [P, B, S], F32R)
        bh, bl = sb("bh", [P, NB * S], F32R), sb("bl", [P, NB * S], F32R)
        rw = sb("rw", [P, 2, P])
        rwh, rwl = sb("rwh", [P, NE0], F32R), sb("rwl", [P, NE0], F32R)
        ebias = sb("ebias", [P, NE0])
        wgs, wds = sb("wgs", [IN0, P]), sb("wds", [P, IN0])
        wgsh, wgsl = sb("wgsh", [P, IN0], F32R), sb("wgsl", [P, IN0], F32R)
        wdsT = sb("wdsT", [IN0, P])
        sel_f = sb("sel_f", [ROWS, GE // 2, 2, IN0])
        sel = sb("sel", [ROWS, GE // 2, P], BF16)
        ct = sb("ct", [ROWS, GROUPS, B * S], BF16)
        lg, prb, rep, comb, rest = (sb(n, [P, TI, NE0]) for n in ("lg", "prb", "rep", "comb", "rest"))
        top = sb("top", [P, TI, 8])
        tot, inv = sb("tot", [P, TI]), sb("inv", [P, TI])
        parts = sb("parts", [P, TI, GROUPS, 3, GE], BF16)
        gn = [sb(f"gn{r}", [P, 2, P]) for r in range(2)]
        dn = [sb(f"dn{r}", [P, 4, IN0]) for r in range(2)]
        wh = [sb(f"wh{r}", [P, 4, P], F32R) for r in range(2)]
        wl = [sb(f"wl{r}", [P, 4, P], F32R) for r in range(2)]
        act_h = [sb(f"act_h{r}", [P, S]) for r in range(R)]
        hid = [sb(f"hid{r}", [P, S]) for r in range(R)]
        hh = [sb(f"hh{r}", [P, S], F32R) for r in range(R)]
        hl = [sb(f"hl{r}", [P, S], F32R) for r in range(R)]
        yT = sb("yT", [P, B, S])
        names = ("loaded consts wT w_out step zTr bh_ready bl_ready logits sig_in sig ptr ct_out sh_h sh_act "
                 "w_ina w_inb wt_done wh_out wl_out h_done c_done act_done hid_done hh_done hl_done y_units y_out y_tok")
        s = {n: k.sem("f0_" + n) for n in names.split()}
        ps = k.ps

        with nc.Block() as block:
            @block.sync
            def _(sp):
                r = d["L0_ffn_router_w"]
                sp.dma_start(rw[:, 0, :], r[0:P, :]).then_inc(s["loaded"], 16)
                sp.dma_start(rw[0:NE0 - P, 1, :], r[P:NE0, :]).then_inc(s["loaded"], 16)
                sp.dma_start(ebias[:], d["L0_ffn_expert_bias"].partition_broadcast(P)).then_inc(s["loaded"], 16)
                sp.dma_start(wgs[:], d["L0_ffn_w_gate_shared"]).then_inc(s["loaded"], 16)
                sp.dma_start(wds[:], d["L0_ffn_w_down_shared"]).then_inc(s["loaded"], 16)
                sp.wait_ge(s["loaded"], 16 * 5)

            @block.gpsimd
            def _(pool):
                layernorm_pool(k, pool)
                pool.memset(sel_f[:].rearrange("p j h c -> p (j h c)"), 0.0).then_inc(s["consts"], 1)
                for part in range(3):
                    pool.wait_ge(s["consts"], part + 1)
                    pool.affine_select(out=sel_f[:].rearrange("p j h c -> p (j h) c"), in_=sel_f[:].rearrange("p j h c -> p (j h) c"),
                                       compare_op=ALU.not_equal, fill=1.0, base=-part * GE, pattern=[[-1, GE], [0, IN0]],
                                       channel_multiplier=1).then_inc(s["consts"], 1)

            @block.tensor
            def _(pe):
                pe.wait_ge(s["loaded"], 16 * 5)
                pe.transpose(ps[:, 0, 0:P], rw[:, 0, :], k.ident[:])
                pe.transpose(ps[:, 0, P:NE0], rw[0:NE0 - P, 1, :], k.ident[0:NE0 - P, 0:NE0 - P])
                pe.transpose(ps[:, 0, NE0:NE0 + IN0], wgs[:], k.ident[0:IN0, 0:IN0])
                pe.transpose(ps[0:IN0, 0, 256:256 + P], wds[:], k.ident[:]).then_inc(s["wT"], 1)

            @block.scalar
            def _(act):
                act.wait_ge(s["wT"], 1)
                act.activation(rwh[:], ps[:, 0, 0:NE0], ACT.Copy)
                act.activation(wgsh[:], ps[:, 0, NE0:NE0 + IN0], ACT.Copy)
                act.activation(wdsT[:], ps[0:IN0, 0, 256:256 + P], ACT.Copy).then_inc(s["w_out"], 1)
                act.wait_ge(s["consts"], 4)
                act.activation(sel[:].rearrange("p j c -> p (j c)"), sel_f[:].rearrange("p j h c -> p (j h c)"), ACT.Copy)

            @block.vector
            def _(v):
                layernorm_vector(k, v, k.x)
                v.wait_ge(s["w_out"], 1)
                v.tensor_tensor(rwl[:], ps[:, 0, 0:NE0], rwh[:].bitcast(F32), ALU.subtract)
                v.tensor_tensor(wgsl[:], ps[:, 0, NE0:NE0 + IN0], wgsh[:].bitcast(F32), ALU.subtract)

        def logit_out(t):
            return ps[:, t // 2, t % 2 * 256:t % 2 * 256 + NE0]

        def parts_out(t):
            return ps[0:ROWS, t // 2, :].bitcast(BF16).rearrange("p (t g n) -> p t g n", t=2, n=P)[:, t % 2, :, :]

        with nc.Block() as block:
            @block.vector
            def _(v):
                with v.Fori(0, B // NB) as b:
                    take_batch(k, v, b, NB)
                    step = chain(v, s["step"], RSTEPS, b)
                    v.wait_ge(s["bh_ready"], b + 1)
                    v.tensor_tensor(bl[:], ps[:, CB:CB + NB, :].rearrange("p b n -> p (b n)"), bh[:].bitcast(F32), ALU.subtract).then_inc(s["bl_ready"], 1)
                    v.tensor_copy(xh[:, bass.ds(b * NB, NB), :].rearrange("p b n -> p (b n)"), bh[:].bitcast(F32))
                    v.wait_ge(s["bl_ready"], b + 1)
                    v.tensor_copy(xl[:, bass.ds(b * NB, NB), :].rearrange("p b n -> p (b n)"), bl[:].bitcast(F32))
                    for t in range(0, TI, 2):
                        v.wait_ge(s["logits"], b * TI + t + 2)
                        last = v.tensor_tensor(lg[:, t:t + 2, :], ps[:, t // 2, :].rearrange("p (t n) -> p t n", t=2)[:, :, 0:NE0],
                                               ebias[:].unsqueeze(1).to_broadcast([P, 2, NE0]), ALU.add)
                    last.then_inc(s["sig_in"], 1)
                    v.wait_ge(s["sig_in"], b + 1)
                    k.settle(v)
                    for t in range(TI):
                        last = v.max(top[:, t, :], lg[:, t, :])
                    step(last, k)
                    for t in range(TI):
                        last = v.match_replace(rep[:, t, :], top[:, t, :], lg[:, t, :], TAKEN)
                    step(last)
                    v.wait_ge(s["sig"], b + 1)
                    step(v.scalar_tensor_tensor(comb[:], rep[:], TAKEN, prb[:], ALU.is_equal, ALU.mult))
                    step(v.tensor_reduce(tot[:], comb[:], AX, ALU.add))
                    step(v.tensor_scalar(tot[:], tot[:], 1e-9, None, ALU.add))
                    step(v.reciprocal(inv[:], tot[:]))
                    step(v.tensor_scalar(inv[:], inv[:], 2.5, None, ALU.mult))
                    step(v.tensor_tensor(comb[:], comb[:], inv[:].unsqueeze(2).to_broadcast([P, TI, NE0]), ALU.mult))
                    def by_iteration(a):
                        return a.rearrange("p (n g e) -> p g n e", g=GROUPS, e=2)

                    def by_group(a):
                        return a.rearrange("p g (n e) -> p g n e", e=2)

                    src = comb
                    for part in range(3):
                        for t in range(TI):
                            last = v.tensor_copy(by_group(parts[:, t, :, part, :]), by_iteration(src[:, t, :]))
                        step(last)
                        if part < 2:
                            for t in range(TI):
                                last = v.tensor_tensor(by_iteration(rest[:, t, :]), by_iteration(src[:, t, :]),
                                                       by_group(parts[:, t, :, part, :]), ALU.subtract)
                            step(last)
                        src = rest
                    assert step.count[0] == RSTEPS, step.count[0]

            @block.scalar
            def _(act):
                with act.Fori(0, B // NB) as b:
                    act.wait_ge(s["zTr"], b + 1)
                    act.activation(bh[:], ps[:, CB:CB + NB, :].rearrange("p b n -> p (b n)"), ACT.Copy).then_inc(s["bh_ready"], 1)
                    act.wait_ge(s["sig_in"], b + 1)
                    act.activation(prb[:], lg[:], ACT.Sigmoid).then_inc(s["sig"], 1)
                    act.wait_ge(s["ptr"], b + 1)
                    for t in range(TI):
                        last = act.activation(ct[:, :, bass.ds(b * NB * S + t * P, P)], parts_out(t), ACT.Copy)
                    last.then_inc(s["ct_out"], 1)

            @block.tensor
            def _(pe):
                with pe.Fori(0, B // NB) as b:
                    pe.wait_ge(s["step"], b * RSTEPS)
                    pe.wait_ge(k.zb_ready, k.n_batches + b + 1)
                    for t in range(TI):
                        last = pe.transpose(ps[:, CB + t // NT, t % NT * P:(t % NT + 1) * P], k.zb[:, t, :], k.ident[:])
                    last.then_inc(s["zTr"], 1)
                    pe.wait_ge(s["bl_ready"], b + 1)
                    pe.wait_ge(s["ct_out"], b)
                    for t in range(TI):
                        tok = slice(t * P, (t + 1) * P)
                        split_product(pe, logit_out(t), (bh[:, tok], bl[:, tok]), (rwh[:], rwl[:])).then_inc(s["logits"], 1)
                    pe.wait_ge(s["step"], b * RSTEPS + RSTEPS)
                    for t in range(TI):
                        for g in range(GROUPS):
                            last = pe.transpose(parts_out(t)[:, g, :], parts[:, t, g, :, :].rearrange("p a e -> p (a e)"), k.ident_bf[:])
                    last.then_inc(s["ptr"], 1)

        with nc.Block() as block:
            @block.tensor
            def _(pe):
                for c in range(CH):
                    if c >= 2:
                        pe.wait_ge(s["sh_act"], c - 1)
                    split_product(pe, ps[0:IN0, HB + c % 2, :], (wgsh[:], wgsl[:]), (xh[:, c, :], xl[:, c, :])).then_inc(s["sh_h"], 1)
                for c in range(CH):
                    pe.wait_ge(s["sh_act"], c + 1)
                    pe.matmul(k.bank(YB + c), wdsT[:], yT[0:IN0, c, :], start=True, stop=False, skip_group_check=True)

            @block.scalar
            def _(act):
                for c in range(CH):
                    act.wait_ge(s["sh_h"], c + 1)
                    act.activation(yT[0:IN0, c, :], ps[0:IN0, HB + c % 2, :], ACT.Silu).then_inc(s["sh_act"], 1)

        gate = d["L0_ffn_w_gate"].rearrange("(n q e) i h -> n (e i) q h", q=2, e=2)
        down = d["L0_ffn_w_down"].rearrange("(n e) h i -> n h e i", e=4)

        with nc.Block() as block:
            @block.sync
            def _(sp):
                def load(half, block, transposed):
                    if transposed is not None:
                        sp.wait_ge(s["wt_done"], transposed)
                    sp.dma_start(gn[half][:], gate[block]).then_inc(s["w_in" + "ab"[half]], 16)
                    sp.dma_start(dn[half][:], down[block]).then_inc(s["w_in" + "ab"[half]], 16)

                load(0, 0, None)
                with sp.Fori(0, ITS - 1) as n:
                    load(1, n * 2 + 1, n * 2)
                    load(0, n * 2 + 2, n * 2 + 1)
                n = ITS - 1
                load(1, n * 2 + 1, n * 2)
                load(0, 0, n * 2 + 1)

            @block.tensor
            def _(pe):
                def prepare(half, n):
                    pe.wait_ge(s["w_in" + "ab"[half]], (n + 1) * 32)
                    if not (isinstance(n, int) and half == 0):
                        pe.wait_ge(s["wl_out"], n * 2 + half)
                    for q in range(2):
                        pe.transpose(ps[:, TB, q * P:(q + 1) * P], gn[half][:, q, :], k.ident[:])
                    for q in range(2):
                        last = pe.transpose(ps[:, TB, (2 + q) * P:(3 + q) * P],
                                            dn[half][:, 2 * q:2 * q + 2, :].rearrange("p e i -> p (e i)"), k.ident[:])
                    last.then_inc(s["wt_done"], 1)

                def hidden(n, w, first):
                    q, c = w // CH, w % CH
                    half = q // 2
                    if q % 2 == 0 and c == 0:
                        pe.wait_ge(s["wl_out"], n * 2 + half + 1)
                    if not first or w >= 2:
                        pe.wait_ge(s["act_done"], n * UNITS + w - 1)
                    split_product(pe, k.bank(HB + w % 2), (wh[half][:, q % 2, :], wl[half][:, q % 2, :]),
                                  (xh[:, c, :], xl[:, c, :])).then_inc(s["h_done"], 1)
                    if not first or w:
                        pe.wait_ge(s["hid_done"], n * UNITS + w)
                    pe.matmul(k.bank(CB), sel[:, n, :], ct[:, q, c * S:(c + 1) * S], start=True,
                              stop=True).then_inc(s["c_done"], 1)

                def output(n, w):
                    q, c = w % UNITS // CH, w % CH
                    pe.wait_ge(s["hl_done"], n * UNITS + w + 1)
                    half, j = q // 2, 2 + q % 2
                    split_product(pe, k.bank(YB + c), (wh[half][:, j, :], wl[half][:, j, :]), (hh[w % R][:], hl[w % R][:]),
                                  start=False, stop=False, skip=True).then_inc(s["y_units"], 1)

                def iteration(n, first):
                    for w in range(UNITS):
                        if w == AHEAD:
                            prepare(1, n)
                        elif w == UNITS // 2 + AHEAD:
                            prepare(0, n + 1)
                        hidden(n, w, first)
                        if not first or w >= LAG:
                            output(n, w - LAG)

                prepare(0, 0)
                iteration(0, True)
                with pe.Fori(1, ITS) as n:
                    iteration(n, False)
                for w in range(LAG):
                    output(ITS, w - LAG)

            @block.scalar
            def _(act):
                def prepare(half, n):
                    act.wait_ge(s["wt_done"], n * 2 + half + 1)
                    act.activation(wh[half][:].rearrange("p q n -> p (q n)"), k.bank(TB), ACT.Copy).then_inc(s["wh_out"], 1)

                def high(n, w, first=False):
                    act.wait_ge(s["hid_done"], n * UNITS + w + 1)
                    if not first or w >= R:
                        act.wait_ge(s["y_units"], n * UNITS + w - R + 1)
                    act.activation(hh[w % R][:], hid[w % R][:], ACT.Copy).then_inc(s["hh_done"], 1)

                def iteration(n, first):
                    for w in range(UNITS):
                        if w == AHEAD:
                            prepare(1, n)
                        elif w == UNITS // 2 + AHEAD:
                            prepare(0, n + 1)
                        act.wait_ge(s["h_done"], n * UNITS + w + 1)
                        if not first or w >= R:
                            act.wait_ge(s["hid_done"], n * UNITS + w - R + 1)
                        act.activation(act_h[w % R][:], k.bank(HB + w % 2), ACT.Silu).then_inc(s["act_done"], 1)
                        if not first or w:
                            high(n, w - 1, first)

                prepare(0, 0)
                iteration(0, True)
                with act.Fori(1, ITS) as n:
                    iteration(n, False)
                high(ITS, -1)

            @block.vector
            def _(v):
                def prepare(half, n):
                    v.wait_ge(s["wh_out"], n * 2 + half + 1)
                    v.tensor_tensor(wl[half][:].rearrange("p q n -> p (q n)"), k.bank(TB),
                                    wh[half][:].rearrange("p q n -> p (q n)").bitcast(F32), ALU.subtract).then_inc(s["wl_out"], 1)

                def low(n, w):
                    v.wait_ge(s["hh_done"], n * UNITS + w + 1)
                    v.tensor_tensor(hl[w % R][:], hid[w % R][:], hh[w % R][:].bitcast(F32), ALU.subtract).then_inc(s["hl_done"], 1)

                def iteration(n, first):
                    for w in range(UNITS):
                        if w == AHEAD:
                            prepare(1, n)
                        elif w == UNITS // 2 + AHEAD:
                            prepare(0, n + 1)
                        v.wait_ge(s["act_done"], n * UNITS + w + 1)
                        v.wait_ge(s["c_done"], n * UNITS + w + 1)
                        if not first or w >= R:
                            v.wait_ge(s["hl_done"], n * UNITS + w - R + 1)
                        v.tensor_tensor(hid[w % R][:], act_h[w % R][:], k.bank(CB), ALU.mult).then_inc(s["hid_done"], 1)
                        if not first or w:
                            low(n, w - 1)

                prepare(0, 0)
                iteration(0, True)
                with v.Fori(1, ITS) as n:
                    iteration(n, False)
                low(ITS, -1)

        residual_block(k, s, yT, YB)
    k.n_ln += 1
    k.n_batches += B // NB


def residual_block(k, s, yT, YB):
    nc, ps = k.nc, k.ps
    with nc.Block() as block:
        @block.scalar
        def _(act):
            for c in range(B):
                act.activation(yT[:, c, :], k.bank(YB + c), ACT.Copy).then_inc(s["y_out"], 1)

        @block.tensor
        def _(pe):
            for c in range(B):
                pe.wait_ge(s["y_out"], c + 1)
                for t in range(NT):
                    last = pe.transpose(ps[:, YB + 4 + c, t * P:(t + 1) * P], yT[:, c, t * P:(t + 1) * P], k.ident[:])
                last.then_inc(s["y_tok"], 1)

        @block.vector
        def _(v):
            for c in range(B):
                v.wait_ge(s["y_tok"], c + 1)
                v.tensor_tensor(k.x[:, c * NT:(c + 1) * NT, :], k.x[:, c * NT:(c + 1) * NT, :],
                                k.bank(YB + 4 + c).rearrange("p (t n) -> p t n", n=P), ALU.add)


def stage_attention_1(k):
    nc, d = k.nc, k.dram
    G = H1 // 4
    AHEAD = 2
    OFF = [0, 4 * P, 7 * P, 9 * P, 10 * P]
    EVAC = [(OFF[0], OFF[1]), (OFF[1], OFF[2]), (OFF[2], OFF[4])]
    SB, PB, OB, TB = 0, 4, 6, 7

    with ExitStack() as ctx:
        def sb(name, shape, dt=F32):
            return k.sb(ctx, "a1_" + name, shape, dt)

        wqkv = sb("wqkv", [P, 3 * P])
        wstack = [sb(f"wstack{n}", [P, G, 4, 4, HD1]) for n in "qk"]
        wo_nat = sb("wo_nat", [HD1, H1, P])
        wo = sb("wo", [P, G, P])
        brow = sb("brow", [P, P])
        row = sb("row", [P, 1], I32)
        sel_i = [sb(f"sel_i{n}", [P, 1], I32) for n in range(2)]
        sel = [sb(f"sel{n}", [P, 1]) for n in range(2)]
        mask = sb("mask", [P, S])
        zT = sb("zT", [P, S])
        vpad = sb("vpad", [P, NT, H1, 32])
        qhi, khi = sb("qhi", [P, S], F32R), sb("khi", [P, S], F32R)
        qz = [[sb(f"qz{r}{j}", [P, S], F32R) for j in range(4)] for r in range(2)]
        ks = [sb(f"ks{r}", [P, S], F32R) for r in range(2)]
        sc = [sb(f"sc{r}", [P, S]) for r in range(4)]
        nmax = sb("nmax", [P, 3, NT])
        sums = sb("sums", [P, 3, NT])
        rsum = sb("rsum", [P, 3, NT])
        prob = sb("prob", [P, 3, NT, S])
        pt = [[sb(f"pt{r}{j}", [P, OFF[4]]) for j in range(4)] for r in range(2)]
        oT = sb("oT", [P, G, S])
        names = ("loaded consts sel wo_zero zTr zT_out q_done k_done qhi_ready khi_ready qk_ready v_done "
                 "v_out score tile_scored exp_done rs_ready prob_ready ptr pt_a pt_v pv o_out y_done  batch_done")
        s = {n: k.sem("a1_" + n) for n in names.split()}
        ps = k.ps

        def keys(i):
            return (i + 1) * P

        def key_bank(g):
            return TB if g else OB

        with nc.Block() as block:
            @block.sync
            def _(sp):
                sp.dma_start(wqkv[:], d["L1_attn_w_qkv"]).then_inc(s["loaded"], 16)
                sp.dma_start(brow[:], d["L1_attn_b_out"].partition_broadcast(P)).then_inc(s["loaded"], 16)
                sp.wait_ge(s["wo_zero"], 1)
                wo_d = d["L1_attn_w_out"].rearrange("(g j e) n -> j e g n", j=4, e=HD1)
                for j in range(4):
                    sp.dma_start(wo[32 * j:32 * j + HD1, :, :], wo_d[j]).then_inc(s["loaded"], 16)
                sp.wait_ge(s["loaded"], 16 * 6)

            @block.gpsimd
            def _(pool):
                layernorm_pool(k, pool)
                pool.memset(vpad[:].rearrange("p t h e -> p (t h e)"), 0.0)
                pool.memset(wo[:], 0.0).then_inc(s["wo_zero"], 1)
                for r in range(2):
                    for j in range(4):
                        pool.memset(qz[r][j][:].bitcast(F32), 0.0)
                pool.iota(row[:], [[0, 1]], base=0, channel_multiplier=1).then_inc(s["consts"], 1)
                pool.memset(mask[:], 0.0).then_inc(s["consts"], 1)
                pool.wait_ge(s["consts"], 2)
                pool.affine_select(out=mask[:], in_=mask[:], compare_op=ALU.is_ge, fill=-1.0e10, base=S - P,
                                   pattern=[[-1, S]], channel_multiplier=1)

            @block.vector
            def _(v):
                layernorm_vector(k, v, k.x)
                v.wait_ge(s["consts"], 1)
                for n, shift in enumerate((3, 4)):
                    v.tensor_scalar(sel_i[n][:], row[:], shift, 1, ALU.logical_shift_right, ALU.bitwise_and).then_inc(s["sel"], 1)
                v.wait_ge(s["sel"], 2)
                for n in range(2):
                    v.tensor_scalar(sel[n][:], sel_i[n][:], -1.0, None, ALU.mult)
                v.wait_ge(s["loaded"], 16 * 6)
                v.tensor_tensor(k.x[:], k.x[:], brow[:].unsqueeze(1).to_broadcast([P, TT, P]), ALU.add)
                for n, scale in ((0, HD1 ** -0.5), (1, 1.0)):
                    src = wqkv[:, n * P:(n + 1) * P].rearrange("p (h e) -> p h e", e=HD1)
                    dst = wstack[n][:].rearrange("p g j c e -> p (g j) c e")
                    for c in range(4):
                        v.tensor_scalar(dst[:, :, c, :], src, scale, None, ALU.mult)

        with nc.Block() as block:
            @block.vector
            def _(v):
                with v.Fori(0, B) as b:
                    take_batch(k, v, b)

                    def prepare_q(g, j):
                        r, rows = g % 2, slice(32 * j, 32 * j + 32)
                        if j == 0:
                            v.wait_ge(s["qhi_ready"], b * G + g + 1)
                        last = v.scalar_tensor_tensor(qz[r][j][rows, :], qhi[rows, :].bitcast(F32), sel[0][rows, 0:1],
                                                      ps[rows, TB, :], ALU.mult, ALU.add)
                        if j == 3:
                            last.then_inc(s["qk_ready"], 1)

                    def prepare_k(g):
                        r = g % 2
                        v.wait_ge(s["khi_ready"], b * G + g + 1)
                        v.scalar_tensor_tensor(ks[r][:], khi[:].bitcast(F32), sel[1][:, 0:1], k.bank(key_bank(g)), ALU.mult,
                                               ALU.add).then_inc(s["qk_ready"], 1)

                    def score(h, i):
                        u = h * NT + i
                        v.wait_ge(s["score"], b * H1 * NT + u + 1)
                        if u >= 4:
                            v.wait_ge(s["exp_done"], b * H1 * NT + u - 3)
                        k.settle(v)
                        v.tensor_tensor_reduce(sc[u % 4][:, 0:keys(i)], ps[:, SB + u % 4, 0:keys(i)],
                                               mask[:, S - P - i * P:S], -1.0, 3.0e38, ALU.add, ALU.min,
                                               nmax[:, h % 3, i:i + 1]).then_inc(s["tile_scored"], 1)

                    def invert(h):
                        v.wait_ge(s["exp_done"], b * H1 * NT + h * NT + NT)
                        v.reciprocal(rsum[:, h % 3, :], sums[:, h % 3, :]).then_inc(s["rs_ready"], 1)

                    def evacuate(h):
                        r, j = h // 4 % 2, h % 4
                        v.wait_ge(s["ptr"], b * H1 * 3 + 3 * h + 3)
                        if h >= 8:
                            v.wait_ge(s["pv"], b * G + h // 4 - 1)
                        lo, hi = EVAC[2]
                        v.tensor_copy(pt[r][j][:, lo:hi], ps[:, PB + (3 * h + 2) % 2, 0:hi - lo]).then_inc(s["pt_v"], 1)

                    for j in range(4):
                        prepare_q(0, j)
                    prepare_k(0)
                    for h in range(AHEAD):
                        for i in range(NT):
                            score(h, i)
                    invert(0)
                    for h in range(H1):
                        ahead = h // 4 + 1 < G
                        if ahead and h % 4 == 1:
                            prepare_k(h // 4 + 1)
                        for i in range(NT):
                            if ahead and h % 4 == 0:
                                prepare_q(h // 4 + 1, i)
                            if h + AHEAD < H1:
                                score(h + AHEAD, i)
                            if i == 1 and h + 1 < H1:
                                invert(h + 1)
                            if i == 3:
                                evacuate(h)
                    v.wait_ge(s["y_done"], b + 1)
                    v.tensor_tensor(k.x[:, bass.ds(b * NT, NT), :], k.x[:, bass.ds(b * NT, NT), :],
                                    ps[:, SB:SB + NT, 0:P], ALU.add).then_inc(s["batch_done"], 1)

            @block.gpsimd
            def _(pool):
                with pool.Fori(0, B) as b:
                    for h in range(H1):
                        pool.wait_ge(s["rs_ready"], b * H1 + h + 1)
                        k.settle(pool)
                        for i in range(NT):
                            last = pool.tensor_scalar(prob[:, h % 3, i, 0:keys(i)], prob[:, h % 3, i, 0:keys(i)],
                                                      rsum[:, h % 3, i:i + 1], 0.0, ALU.mult, ALU.add)
                        last.then_inc(s["prob_ready"], 1)

            @block.scalar
            def _(act):
                with act.Fori(0, B) as b:
                    act.wait_ge(s["zTr"], b + 1)
                    act.activation(zT[:], k.bank(OB), ACT.Copy).then_inc(s["zT_out"], 1)

                    def prepare_q(g):
                        act.wait_ge(s["q_done"], b * G + g + 1)
                        act.activation(qhi[:], ps[:, TB, :], ACT.Copy).then_inc(s["qhi_ready"], 1)

                    def prepare_k(g):
                        act.wait_ge(s["k_done"], b * G + g + 1)
                        act.activation(khi[:], k.bank(key_bank(g)), ACT.Copy).then_inc(s["khi_ready"], 1)

                    def exp(h, i):
                        u = h * NT + i
                        act.wait_ge(s["tile_scored"], b * H1 * NT + u + 1)
                        if i == 0 and h >= 3:
                            act.wait_ge(s["ptr"], b * H1 * 3 + 3 * (h - 2))
                        act.activation(prob[:, h % 3, i, 0:keys(i)], sc[u % 4][:, 0:keys(i)], ACT.Exp, scale=-1.0,
                                       bias=nmax[:, h % 3, i:i + 1], accum_out=sums[:, h % 3, i:i + 1]).then_inc(s["exp_done"], 1)

                    def evacuate(h, n):
                        r, j = h // 4 % 2, h % 4
                        act.wait_ge(s["ptr"], b * H1 * 3 + 3 * h + n + 1)
                        if h >= 8 and n == 0:
                            act.wait_ge(s["pv"], b * G + h // 4 - 1)
                        lo, hi = EVAC[n]
                        act.activation(pt[r][j][:, lo:hi], ps[:, PB + (3 * h + n) % 2, 0:hi - lo], ACT.Copy).then_inc(s["pt_a"], 1)

                    def output(g):
                        act.wait_ge(s["pv"], b * G + g + 1)
                        act.activation(oT[:, g, :], k.bank(OB), ACT.Copy).then_inc(s["o_out"], 1)

                    act.wait_ge(s["v_done"], b + 1)
                    act.activation(vpad[:, :, :, 0:HD1],
                                   k.bank(PB).rearrange("p (t h e) -> p t h e", h=H1, e=HD1), ACT.Copy).then_inc(s["v_out"], 1)
                    prepare_q(0)
                    prepare_k(0)
                    for h in range(AHEAD):
                        for i in range(NT):
                            exp(h, i)
                    for h in range(H1):
                        if h % 4 < 2 and h // 4 + 1 < G:
                            (prepare_k if h % 4 else prepare_q)(h // 4 + 1)
                        for i in range(NT):
                            if i % 2 == 0:
                                evacuate(h, i // 2)
                            if h + AHEAD < H1:
                                exp(h + AHEAD, i)
                        if h % 4 == 0 and h:
                            output(h // 4 - 1)
                    output(G - 1)

            @block.tensor
            def _(pe):
                with pe.Fori(0, B) as b:
                    pe.wait_ge(s["batch_done"], b)
                    pe.wait_ge(k.zb_ready, k.n_batches + b + 1)
                    for t in range(NT):
                        last = pe.transpose(ps[:, OB, t * P:(t + 1) * P], k.zb[:, t, :], k.ident[:])
                    last.then_inc(s["zTr"], 1)
                    pe.wait_ge(s["zT_out"], b + 1)
                    for t in range(NT):
                        last = pe.matmul(ps[:, PB, t * P:(t + 1) * P], zT[:, t * P:(t + 1) * P], wqkv[:, 2 * P:3 * P],
                                         start=True, stop=True)
                    last.then_inc(s["v_done"], 1)

                    def prepare(g, n):
                        if g:
                            pe.wait_ge(s["qk_ready"], b * 2 * G + 2 * g + n)
                        pe.matmul(k.bank(key_bank(g) if n else TB), wstack[n][:, g, :, :, :].rearrange("p j c e -> p (j c e)"), zT[:],
                                  start=True, stop=True).then_inc(s["k_done" if n else "q_done"], 1)

                    def score(h, i):
                        r, j, u = h // 4 % 2, h % 4, h * NT + i
                        if i == 0 and j == 0:
                            pe.wait_ge(s["qk_ready"], b * 2 * G + 2 * (h // 4) + 2)
                        if u >= 4:
                            pe.wait_ge(s["tile_scored"], b * H1 * NT + u - 3)
                        pe.matmul(ps[:, SB + u % 4, 0:keys(i)], qz[r][j][:, i * P:(i + 1) * P], ks[r][:, 0:keys(i)],
                                  start=True, stop=True).then_inc(s["score"], 1)

                    def transpose_probs(h, n):
                        if n == 0 and h:
                            pe.wait_ge(s["pt_a"], b * 2 * H1 + 2 * h)
                        elif n == 1 and h:
                            pe.wait_ge(s["pt_v"], b * H1 + h)
                        elif n == 2:
                            pe.wait_ge(s["pt_a"], b * 2 * H1 + 2 * h + 1)
                        if n == 0:
                            pe.wait_ge(s["prob_ready"], b * H1 + h + 1)
                        at = 0
                        for kt in ((0,), (1,), (2, 3))[n]:
                            for i in range(kt, NT):
                                last = pe.transpose(ps[:, PB + (3 * h + n) % 2, at:at + P],
                                                    prob[:, h % 3, i, kt * P:(kt + 1) * P], k.ident[:])
                                at += P
                        last.then_inc(s["ptr"], 1)

                    def values(g):
                        r = g % 2
                        if g:
                            pe.wait_ge(s["o_out"], b * G + g)
                        pe.wait_ge(s["pt_a"], b * 2 * H1 + 2 * (4 * g + 4))
                        pe.wait_ge(s["pt_v"], b * H1 + 4 * g + 4)
                        for kt in range(NT):
                            for j in range(4):
                                last = pe.matmul(ps[32 * j:32 * j + 32, OB, kt * P:S], vpad[:, kt, 4 * g + j, :],
                                                 pt[r][j][:, OFF[kt]:OFF[kt + 1]], start=(kt == 0), stop=(kt == NT - 1))
                        last.then_inc(s["pv"], 1)

                    prepare(0, 0)
                    prepare(0, 1)
                    for h in range(AHEAD):
                        for i in range(NT):
                            score(h, i)
                    pe.wait_ge(s["v_out"], b + 1)
                    for h in range(H1):
                        if h % 4 < 2 and h // 4 + 1 < G:
                            prepare(h // 4 + 1, h % 4)
                        for i in range(NT):
                            if h + AHEAD < H1:
                                score(h + AHEAD, i)
                            if i < 2:
                                transpose_probs(h, i)
                        transpose_probs(h, 2)
                        if h % 4 == 0 and h:
                            values(h // 4 - 1)
                    values(G - 1)
                    pe.wait_ge(s["o_out"], b * G + G)
                    for t in range(NT):
                        for g in range(G):
                            last = pe.matmul(ps[:, SB + t, 0:P], oT[:, g, t * P:(t + 1) * P], wo[:, g, :],
                                             start=(g == 0), stop=(g == G - 1))
                    last.then_inc(s["y_done"], 1)
    k.n_ln += 1
    k.n_batches += B


def stage_experts_1(k):
    nc, d = k.nc, k.dram
    ROWS = 3 * NE1
    FB = FF1 // P
    EXPERTS = 2
    ITS = NE1 // EXPERTS
    CH = B
    E_UNITS = CH * FB
    UNITS = EXPERTS * E_UNITS
    CHUNKS = EXPERTS * CH
    MID = 4
    LAG = 3
    R = 4
    YB, GB, VB, CB, TB = 0, 4, 5, 6, 7
    ALPHA, LIMIT = 1.702, 9.0

    with ExitStack() as ctx:
        def sb(name, shape, dt=F32):
            return k.sb(ctx, "f1_" + name, shape, dt)

        xh, xl = sb("xh", [P, B, S], F32R), sb("xl", [P, B, S], F32R)
        bh, bl = sb("bh", [P, S], F32R), sb("bl", [P, S], F32R)
        gw = sb("gw", [P, NE1])
        gwh, gwl = sb("gwh", [P, NE1], F32R), sb("gwl", [P, NE1], F32R)
        b1n = sb("b1n", [NE1 * FB, 2 * P])
        b1 = sb("b1", [P, 2, NE1 * FB])
        b2 = sb("b2", [NE1, P])
        order = sb("order", [P, NE1])
        sel_f = sb("sel_f", [ROWS, NE1, P])
        sel = sb("sel", [ROWS, NE1, P], BF16)
        ct = sb("ct", [ROWS, B * S], BF16)
        ct32 = sb("ct32", [NE1, B * S])
        g1, g2, eq, m1, m2, comb, scaled, rest = (sb(n, [P, TT, NE1]) for n in ("g1", "g2", "eq", "mask1", "mask2", "comb", "scaled", "rest"))
        top1, top2, best, ex, den, inv, second = (sb(n, [P, TT]) for n in ("top1", "top2", "best", "ex", "den", "inv", "second"))
        parts = sb("parts", [P, TT, 3, NE1], BF16)
        wn = [sb(f"wn{r}", [P, FB, 2, P]) for r in range(2)]
        dn = [sb(f"dn{r}", [P, FB, P]) for r in range(2)]
        wh = [sb(f"wh{r}", [P, FB, 2, P], F32R) for r in range(2)]
        wl = [sb(f"wl{r}", [P, FB, 2, P], F32R) for r in range(2)]
        dT = [sb(f"dT{r}", [P, FB, P]) for r in range(2)]
        gate, val, sg, hid, hidw = ([sb(f"{n}{r}", [P, S]) for r in range(R)] for n in ("gate", "val", "sg", "hid", "hidw"))
        ce = [sb(f"ce{r}", [P, S]) for r in range(2)]
        yT = sb("yT", [P, B, S])
        names = ("loaded consts b1T w_out step zTr bh_ready bl_ready logits exp_in exp_out g1_ready parts_ready ptr w_ina w_inb wt_done dt_done "
                 "wh_out wl_out dt_out g_done v_done c_done g_out v_out c_out sig_out clipped h_done hid_done "
                 "y_units y_out y_tok")
        s = {n: k.sem("f1_" + n) for n in names.split()}
        ps = k.ps

        with nc.Block() as block:
            @block.sync
            def _(sp):
                sp.dma_start(gw[:], d["L1_ffn_gate_w"]).then_inc(s["loaded"], 16)
                sp.dma_start(b1n[:], d["L1_ffn_dense_1_b"].rearrange("e (a n) -> (e a) n", a=FB)).then_inc(s["loaded"], 16)
                sp.dma_start(b2[:], d["L1_ffn_dense_2_b"]).then_inc(s["loaded"], 16)
                sp.wait_ge(s["loaded"], 16 * 3)

            @block.gpsimd
            def _(pool):
                layernorm_pool(k, pool)
                for e in range(NE1):
                    pool.memset(order[:, e:e + 1], float(NE1 - e))
                pool.memset(sel_f[:].rearrange("p e c -> p (e c)"), 0.0).then_inc(s["consts"], 1)
                for part in range(3):
                    pool.wait_ge(s["consts"], part + 1)
                    pool.affine_select(out=sel_f[:], in_=sel_f[:], compare_op=ALU.not_equal, fill=1.0, base=-part * NE1,
                                       pattern=[[-1, NE1], [0, P]], channel_multiplier=1).then_inc(s["consts"], 1)

            @block.scalar
            def _(act):
                act.wait_ge(s["consts"], 4)
                act.activation(sel[:].rearrange("p e c -> p (e c)"), sel_f[:].rearrange("p e c -> p (e c)"), ACT.Copy)

            @block.tensor
            def _(pe):
                pe.wait_ge(s["loaded"], 16 * 3)
                for gv in range(2):
                    last = pe.transpose(ps[:, 0, gv * NE1 * FB:(gv + 1) * NE1 * FB],
                                        b1n[:].rearrange("e (p g) -> e g p", g=2)[:, gv, :], k.ident[0:NE1 * FB, 0:NE1 * FB])
                last.then_inc(s["b1T"], 1)

            @block.vector
            def _(v):
                layernorm_vector(k, v, k.x)
                v.wait_ge(s["loaded"], 16 * 3)
                v.tensor_copy(gwh[:], gw[:]).then_inc(s["w_out"], 1)
                v.wait_ge(s["w_out"], 1)
                v.tensor_tensor(gwl[:], gw[:], gwh[:].bitcast(F32), ALU.subtract)
                v.wait_ge(s["b1T"], 1)
                v.tensor_copy(b1[:].rearrange("p g n -> p (g n)"), ps[:, 0, 0:2 * NE1 * FB])

        with nc.Block() as block:
            @block.vector
            def _(v):
                with v.Fori(0, B) as b:
                    take_batch(k, v, b)
                    v.wait_ge(s["bh_ready"], b + 1)
                    v.tensor_tensor(bl[:], k.bank(TB), bh[:].bitcast(F32), ALU.subtract).then_inc(s["bl_ready"], 1)
                    v.tensor_copy(xh[:, b, :], bh[:].bitcast(F32))
                    v.wait_ge(s["bl_ready"], b + 1)
                    v.tensor_copy(xl[:, b, :], bl[:].bitcast(F32))

                    v.wait_ge(s["logits"], b + 1)
                    v.tensor_copy(g1[:, bass.ds(b * NT, NT), :], ps[:, 0:NT, 0:NE1]).then_inc(s["g1_ready"], 1)

                step = chain(v, s["step"])
                v.wait_ge(s["g1_ready"], B)

                def wide(a):
                    return a[:].unsqueeze(2).to_broadcast([P, TT, NE1])

                def best_of(gates, top, mask):
                    step(v.tensor_reduce(top[:], gates[:], AX, ALU.max))
                    step(v.tensor_tensor(eq[:], gates[:], wide(top), ALU.is_equal))
                    step(v.tensor_tensor(eq[:], eq[:], order[:].unsqueeze(1).to_broadcast([P, TT, NE1]), ALU.mult))
                    step(v.tensor_reduce(best[:], eq[:], AX, ALU.max))
                    step(v.tensor_tensor(mask[:], eq[:], wide(best), ALU.is_equal))

                best_of(g1, top1, m1)
                step(v.scalar_tensor_tensor(g2[:], m1[:], NEG, g1[:], ALU.mult, ALU.add))
                best_of(g2, top2, m2)
                v.tensor_tensor(ex[:], top2[:], top1[:], ALU.subtract).then_inc(s["exp_in"], 1)
                v.wait_ge(s["exp_out"], 1)
                step(v.tensor_scalar(inv[:], ex[:], 1.0, None, ALU.add))
                step(v.reciprocal(den[:], inv[:]))
                v.tensor_tensor(m1[:], m1[:], wide(den), ALU.mult)
                step(v.tensor_tensor(second[:], ex[:], den[:], ALU.mult))
                step(v.tensor_tensor(m2[:], m2[:], wide(second), ALU.mult))
                step(v.tensor_tensor(comb[:], m1[:], m2[:], ALU.add))
                step(v.tensor_scalar(scaled[:], comb[:], 1.0 / ALPHA, None, ALU.mult))
                step(v.tensor_copy(parts[:, :, 0, :], scaled[:]))
                step(v.tensor_tensor(rest[:], scaled[:], parts[:, :, 0, :], ALU.subtract))
                step(v.tensor_copy(parts[:, :, 1, :], rest[:]))
                step(v.tensor_tensor(rest[:], rest[:], parts[:, :, 1, :], ALU.subtract))
                v.tensor_copy(parts[:, :, 2, :], rest[:]).then_inc(s["parts_ready"], 1)

            @block.scalar
            def _(act):
                with act.Fori(0, B) as b:
                    act.wait_ge(s["zTr"], b + 1)
                    act.activation(bh[:], k.bank(TB), ACT.Copy).then_inc(s["bh_ready"], 1)
                act.wait_ge(s["exp_in"], 1)
                act.activation(ex[:], ex[:], ACT.Exp).then_inc(s["exp_out"], 1)
                act.wait_ge(s["ptr"], 1)
                act.activation(ct[:], ps[0:ROWS, CB:CB + 2, :].bitcast(BF16).rearrange("p a n -> p (a n)"), ACT.Copy)
                act.activation(ct32[:], ps[0:NE1, 0:B, :].rearrange("p a n -> p (a n)"), ACT.Copy)

            @block.tensor
            def _(pe):
                with pe.Fori(0, B) as b:
                    pe.wait_ge(s["g1_ready"], b)
                    pe.wait_ge(k.zb_ready, k.n_batches + b + 1)
                    for t in range(NT):
                        last = pe.transpose(ps[:, TB, t * P:(t + 1) * P], k.zb[:, t, :], k.ident[:])
                    last.then_inc(s["zTr"], 1)
                    pe.wait_ge(s["bl_ready"], b + 1)
                    for t in range(NT):
                        tok = slice(t * P, (t + 1) * P)
                        last = split_product(pe, ps[:, t, 0:NE1], (bh[:, tok], bl[:, tok]), (gwh[:], gwl[:]))
                    last.then_inc(s["logits"], 1)
                pe.wait_ge(s["parts_ready"], 1)
                for t in range(TT):
                    pe.transpose(ps[0:ROWS, CB:CB + 2, :].bitcast(BF16).rearrange("p a n -> p (a n)")[:, t * P:(t + 1) * P],
                                 parts[:, t, :, :].rearrange("p a e -> p (a e)"), k.ident_bf[:])
                for t in range(TT):
                    last = pe.transpose(ps[0:NE1, t // NT, t % NT * P:(t % NT + 1) * P], comb[:, t, :], k.ident[:])
                last.then_inc(s["ptr"], 1)

        first = d["L1_ffn_dense_1_w"].rearrange("e (f p g) i -> e p f g i", p=P, g=2)
        down = d["L1_ffn_dense_2_w"].rearrange("e i (f n) -> e i f n", n=P)

        with nc.Block() as block:
            @block.sync
            def _(sp):
                def load(e, expert, transposed):
                    if transposed is not None:
                        sp.wait_ge(s["dt_done"], transposed)
                    sp.dma_start(wn[e][:], first[expert]).then_inc(s["w_in" + "ab"[e]], 16)
                    sp.dma_start(dn[e][:], down[expert]).then_inc(s["w_in" + "ab"[e]], 16)

                load(0, 0, None)
                with sp.Fori(0, ITS - 1) as it:
                    load(1, it * EXPERTS + 1, it * EXPERTS)
                    load(0, it * EXPERTS + 2, it * EXPERTS + 1)
                load(1, NE1 - 1, NE1 - 2)
                load(0, 0, NE1 - 1)

            @block.tensor
            def _(pe):
                def prepare(e, it, chunks):
                    pe.wait_ge(s["w_in" + "ab"[e]], (it + 1) * 32)
                    if chunks is not None:
                        pe.wait_ge(s["wl_out"], it * EXPERTS + e)
                        pe.wait_ge(s["wh_out"], it * EXPERTS + e)
                    for j in range(2 * FB):
                        last = pe.transpose(ps[:, TB, j * P:(j + 1) * P], wn[e][:, j // 2, j % 2, :], k.ident[:])
                    last.then_inc(s["wt_done"], 1)
                    if chunks is not None:
                        pe.wait_ge(s["c_out"], chunks)
                    for f in range(FB):
                        last = pe.transpose(ps[:, CB, f * P:(f + 1) * P], dn[e][:, f, :], k.ident[:])
                    last.then_inc(s["dt_done"], 1)

                prepare(0, 0, None)
                for c in range(CH):
                    pe.matmul(k.bank(YB + c), b2[:], ct32[:, c * S:(c + 1) * S], start=True, stop=False, skip_group_check=True)
                with pe.Fori(0, ITS) as it:
                    def hidden(w):
                        e, c, f = w // E_UNITS, w % E_UNITS // FB, w % FB
                        if c == 0 and f == 0:
                            pe.wait_ge(s["wh_out"], it * EXPERTS + e + 1)
                            pe.wait_ge(s["wl_out"], it * EXPERTS + e + 1)
                            pe.wait_ge(s["dt_out"], it * EXPERTS + e + 1)
                        x = (xh[:, c, :], xl[:, c, :])
                        pe.wait_ge(s["g_out"], it * UNITS + w)
                        split_product(pe, k.bank(GB), (wh[e][:, f, 0, :], wl[e][:, f, 0, :]), x).then_inc(s["g_done"], 1)
                        pe.wait_ge(s["v_out"], it * UNITS + w)
                        split_product(pe, k.bank(VB), (wh[e][:, f, 1, :], wl[e][:, f, 1, :]), x).then_inc(s["v_done"], 1)
                        if f == 0:
                            pe.wait_ge(s["c_out"], it * CHUNKS + w // FB)
                            pe.wait_ge(s["dt_out"], it * EXPERTS + 1 + (w >= MID) + (w >= E_UNITS + MID))
                            k.settle(pe)
                            pe.matmul(k.bank(CB), sel[:, it * EXPERTS + e, :], ct[:, c * S:(c + 1) * S], start=True,
                                      stop=True).then_inc(s["c_done"], 1)

                    def output(w):
                        e, c, f = w // E_UNITS, w % E_UNITS // FB, w % FB
                        pe.wait_ge(s["hid_done"], it * UNITS + w + 1)
                        pe.matmul(k.bank(YB + c), dT[e][:, f, :], hidw[w % R][:], start=False, stop=False,
                                  skip_group_check=True).then_inc(s["y_units"], 1)

                    for w in range(UNITS + LAG):
                        if w == MID:
                            prepare(1, it, it * CHUNKS + MID // FB)
                        elif w == E_UNITS + MID:
                            prepare(0, it + 1, it * CHUNKS + (E_UNITS + MID) // FB)
                        if w < UNITS:
                            hidden(w)
                        if w >= LAG:
                            output(w - LAG)

            @block.scalar
            def _(act):
                def prepare(e, it):
                    act.wait_ge(s["wt_done"], it * EXPERTS + e + 1)
                    act.activation(wh[e][:].rearrange("p f g n -> p (f g n)"), k.bank(TB), ACT.Copy).then_inc(s["wh_out"], 1)
                    act.wait_ge(s["dt_done"], it * EXPERTS + e + 1)
                    act.activation(dT[e][:].rearrange("p f n -> p (f n)"), ps[:, CB, 0:FB * P], ACT.Copy).then_inc(s["dt_out"], 1)

                prepare(0, 0)
                with act.Fori(0, ITS) as it:
                    for w in range(UNITS):
                        e, f = w // E_UNITS, w % FB
                        if w == MID:
                            prepare(1, it)
                        elif w == E_UNITS + MID:
                            prepare(0, it + 1)
                        column = (it * EXPERTS + e) * FB + f
                        act.wait_ge(s["g_out"], it * UNITS + w + 1)
                        if w >= R:
                            act.wait_ge(s["h_done"], it * UNITS + w - R + 1)
                        act.activation(sg[w % R][:], gate[w % R][:], ACT.Silu, scale=ALPHA).then_inc(s["sig_out"], 1)
                        act.wait_ge(s["v_done"], it * UNITS + w + 1)
                        k.settle(act)
                        act.activation(val[w % R][:], k.bank(VB), ACT.Identity, bias=b1[:, 1, bass.ds(column, 1)]).then_inc(s["v_out"], 1)
                        if f == 0:
                            m = w // FB
                            act.wait_ge(s["c_done"], it * CHUNKS + m + 1)
                            if m >= 2:
                                act.wait_ge(s["hid_done"], it * UNITS + (m - 1) * FB)
                            act.activation(ce[m % 2][:], k.bank(CB), ACT.Copy).then_inc(s["c_out"], 1)

            @block.vector
            def _(v):
                def prepare(e, it):
                    v.wait_ge(s["wh_out"], it * EXPERTS + e + 1)
                    v.tensor_tensor(wl[e][:].rearrange("p f g n -> p (f g n)"), k.bank(TB),
                                    wh[e][:].rearrange("p f g n -> p (f g n)").bitcast(F32), ALU.subtract).then_inc(s["wl_out"], 1)

                prepare(0, 0)
                with v.Fori(0, ITS) as it:

                    def gates(w):
                        e, f = w // E_UNITS, w % FB
                        column = (it * EXPERTS + e) * FB + f
                        v.wait_ge(s["g_done"], it * UNITS + w + 1)
                        if w >= R:
                            v.wait_ge(s["sig_out"], it * UNITS + w - R + 1)
                        v.tensor_scalar(gate[w % R][:], k.bank(GB), b1[:, 0, bass.ds(column, 1)], LIMIT, ALU.add,
                                        ALU.min).then_inc(s["g_out"], 1)

                    def swiglu(w):
                        v.wait_ge(s["v_out"], it * UNITS + w + 1)
                        v.tensor_scalar(val[w % R][:], val[w % R][:], LIMIT, -LIMIT, ALU.min, ALU.max).then_inc(s["clipped"], 1)
                        v.wait_ge(s["clipped"], it * UNITS + w + 1)
                        v.wait_ge(s["sig_out"], it * UNITS + w + 1)
                        if w >= R:
                            v.wait_ge(s["hid_done"], it * UNITS + w - R + 1)
                        v.scalar_tensor_tensor(hid[w % R][:], val[w % R][:], 1.0, sg[w % R][:], ALU.add, ALU.mult).then_inc(s["h_done"], 1)

                    for w in range(UNITS + 1):
                        if w == MID:
                            prepare(1, it)
                        elif w == E_UNITS + MID:
                            prepare(0, it + 1)
                        if w < UNITS:
                            gates(w)
                        if w >= 1:
                            swiglu(w - 1)

            @block.gpsimd
            def _(pool):
                with pool.Fori(0, ITS) as it:
                    def weigh(w):
                        m = w // FB
                        pool.wait_ge(s["h_done"], it * UNITS + w + 1)
                        pool.wait_ge(s["c_out"], it * CHUNKS + m + 1)
                        if w >= R:
                            pool.wait_ge(s["y_units"], it * UNITS + w - R + 1)
                        pool.tensor_tensor(hidw[w % R][:], hid[w % R][:], ce[m % 2][:], ALU.mult).then_inc(s["hid_done"], 1)

                    for w in range(UNITS):
                        weigh(w)

        residual_block(k, s, yT, YB)
    k.n_ln += 1
    k.n_batches += B
STAGES = [stage_attention_0, stage_cross_attention_0, stage_experts_0, stage_attention_1, stage_cross_attention_1, stage_experts_1]


def build(nc, dram, out):
    with ExitStack() as ctx:
        k = Kernel(nc, ctx, dram, out)
        stage_setup(k)
        for stage in STAGES:
            stage(k)
            k.end_stage()
        stage_store(k)



_INS = (
    "x", "ctx_1024", "mask_Bx1xSxS2_if1", "L0_attn_gamma",
    "L0_attn_w_q", "L0_attn_w_kv", "L0_attn_null_kv", "L0_attn_q_scale",
    "L0_attn_k_scale", "L0_attn_w_out", "L0_xattn_Wq", "L0_xattn_bq",
    "L0_xattn_Wk", "L0_xattn_bk", "L0_xattn_Wv", "L0_xattn_bv",
    "L0_xattn_Wo", "L0_xattn_bo", "L0_ffn_router_w", "L0_ffn_expert_bias",
    "L0_ffn_w_gate", "L0_ffn_w_down", "L0_ffn_w_gate_shared", "L0_ffn_w_down_shared",
    "L1_attn_w_qkv", "L1_attn_w_out", "L1_attn_b_out", "L1_xattn_Wv",
    "L1_xattn_Wk", "L1_xattn_Wq", "L1_xattn_Wo", "L1_xattn_bo",
    "L1_ffn_gate_w", "L1_ffn_dense_1_w", "L1_ffn_dense_1_b", "L1_ffn_dense_2_w",
    "L1_ffn_dense_2_b",
)


def kernel(**inputs):
    import numpy as _np
    import concourse.bacc as _bacc
    from concourse import mybir as _mybir
    from concourse.bass_utils import run_bass_kernel_spmd as _run

    nc = _bacc.Bacc("TRN2", target_bir_lowering=False, num_devices=1)
    arrays, dram = {}, {}
    for name in _INS:
        a = _np.ascontiguousarray(inputs[name])
        arrays[f"in_{name}_dram"] = a
        dram[name] = nc.dram_tensor(f"in_{name}_dram", a.shape, _mybir.dt.from_np(a.dtype), kind="ExternalInput").ap()
    out = nc.dram_tensor("out_0_dram", (B, S, D), F32, kind="ExternalOutput").ap()
    build(nc, dram, out)
    r = _run(nc, [arrays], core_ids=[0])
    return r.results[0]["out_0_dram"]
```
